# Optimizing a Trainium2 kernel written in Bass

```python
import numpy as np
import jax
import jax.numpy as jnp

def _softmax(x, axis=-1):
    return jax.nn.softmax(x, axis=axis)

def _gelu(x):
    return jax.nn.gelu(x, approximate=True)

def _silu(x):
    return jax.nn.silu(x)

def _sigmoid(x):
    return jax.nn.sigmoid(x)

def _layernorm(x, axis=-1, eps=1e-05):
    m = jnp.mean(x, axis=axis, keepdims=True)
    v = jnp.var(x, axis=axis, keepdims=True)
    return (x - m) / jnp.sqrt(v + eps)

def _scatter_add(tgt, idx, src, axis=0):
    return tgt.at[idx].add(src)

def _segment_sum(src, seg, n):
    return jax.ops.segment_sum(src, seg, n)
kernel_name = 'mk_macaron_d1_jaxref_r4_8a5028'

def setup_inputs(seed: int=0):
    np.random.seed(seed)
    _w = jnp.asarray

    def _L0_attn_setup():
        import jax, jax.numpy as jnp
        import numpy as np
        import math
        N_HEAD = 16
        V_HEAD = 32
        NOPE = 32
        ROPE_D = 64
        KEEP = 64
        EPS = 1e-06

        def _freqs(T, dim=ROPE_D, theta=10000.0):
            f = 1.0 / theta ** (jnp.arange(0, dim, 2, dtype=jnp.float32) / dim)
            t = jnp.arange(T, dtype=jnp.float32)
            a = jnp.outer(t, f)
            return (jnp.cos(a), jnp.sin(a))

        def _rope(x, cos, sin):
            S = x.shape[-2]
            c = cos[:S][None, None]
            s = sin[:S][None, None]
            x1, x2 = jnp.split(x, 2, axis=-1)
            return jnp.concatenate([x1 * c - x2 * s, x1 * s + x2 * c], axis=-1)

        def _rms(x, g, eps=EPS):
            return x * jax.lax.rsqrt(jnp.mean(x * x, axis=-1, keepdims=True) + eps) * g

        def _attn(q, k, v, causal):
            scale = 1.0 / math.sqrt(q.shape[-1])
            s = jnp.einsum('bhqd,bhkd->bhqk', q, k) * scale
            if causal:
                Tq, Tk = (s.shape[-2], s.shape[-1])
                mask = jnp.tril(jnp.ones((Tq, Tk), dtype=bool))
                s = jnp.where(mask, s, jnp.finfo(s.dtype).min)
            return jnp.einsum('bhqk,bhkd->bhqd', jax.nn.softmax(s, axis=-1), v)

        def _forward(x, w_cq, g_qnorm, w_dq_nope, w_dq_rope, w_ckv, g_kvnorm, w_dk_nope, w_dv, w_krope, w_imp, w_selk, w_selv, w_wink, w_winv, w_gate, w_proj):
            B, T, C = x.shape
            cos, sin = _freqs(T)
            nq = _rms(x @ w_cq, g_qnorm)
            q_nope = (nq @ w_dq_nope).reshape(B, T, N_HEAD, NOPE).transpose(0, 2, 1, 3)
            q_rope = (nq @ w_dq_rope).reshape(B, T, N_HEAD, ROPE_D).transpose(0, 2, 1, 3)
            q_rope = _rope(q_rope, cos, sin)
            q = jnp.concatenate([q_nope, q_rope], axis=-1)
            gate = jax.nn.softmax((x @ w_gate).mean(axis=1), axis=-1)
            ckv = _rms(x @ w_ckv, g_kvnorm)
            k_nope = (ckv @ w_dk_nope).reshape(B, T, N_HEAD, NOPE).transpose(0, 2, 1, 3)
            v1 = (ckv @ w_dv).reshape(B, T, N_HEAD, V_HEAD).transpose(0, 2, 1, 3)
            k_rope = (x @ w_krope).reshape(B, T, 1, ROPE_D).transpose(0, 2, 1, 3) / N_HEAD
            k_rope = _rope(k_rope, cos, sin)
            k1 = jnp.concatenate([k_nope, jnp.broadcast_to(k_rope, (B, N_HEAD, T, ROPE_D))], axis=-1)
            scores = (x @ w_imp)[..., 0]
            _, idx = jax.lax.top_k(scores, KEEP)
            idx = jnp.sort(idx, axis=1)
            sel = jnp.take_along_axis(x, idx[:, :, None], axis=1)
            ks = (sel @ w_selk).reshape(B, KEEP, N_HEAD, NOPE + ROPE_D).transpose(0, 2, 1, 3)
            vs = (sel @ w_selv).reshape(B, KEEP, N_HEAD, V_HEAD).transpose(0, 2, 1, 3)
            ks = jnp.concatenate([ks[..., :NOPE], _rope(ks[..., NOPE:], cos, sin)], axis=-1)
            kw = (x @ w_wink).reshape(B, T, N_HEAD, NOPE + ROPE_D).transpose(0, 2, 1, 3)
            vw = (x @ w_winv).reshape(B, T, N_HEAD, V_HEAD).transpose(0, 2, 1, 3)
            kw = jnp.concatenate([kw[..., :NOPE], _rope(kw[..., NOPE:], cos, sin)], axis=-1)
            a1 = _attn(q, k1, v1, causal=True)
            a2 = _attn(q, ks, vs, causal=False)
            a3 = _attn(q, kw, vw, causal=True)
            g = gate[:, :, None, None, None]
            out = g[:, 0] * a1 + g[:, 1] * a2 + g[:, 2] * a3
            out = out.transpose(0, 2, 1, 3).reshape(B, T, N_HEAD * V_HEAD)
            return out @ w_proj
        key = jax.random.key(seed)
        ks = jax.random.split(key, 20)
        B, T, C = (2, 256, 256)
        q_lora, kv_lora = (96, 32)
        std = 0.02

        def w(k, shape):
            return jax.random.normal(k, shape, dtype=jnp.float32) * std
        return {'x': jax.random.normal(ks[0], (B, T, C), dtype=jnp.float32), 'w_cq': w(ks[1], (C, q_lora)), 'g_qnorm': jnp.ones((q_lora,), jnp.float32), 'w_dq_nope': w(ks[2], (q_lora, N_HEAD * NOPE)), 'w_dq_rope': w(ks[3], (q_lora, N_HEAD * ROPE_D)), 'w_ckv': w(ks[4], (C, kv_lora)), 'g_kvnorm': jnp.ones((kv_lora,), jnp.float32), 'w_dk_nope': w(ks[5], (kv_lora, N_HEAD * NOPE)), 'w_dv': w(ks[6], (kv_lora, N_HEAD * V_HEAD)), 'w_krope': w(ks[7], (C, ROPE_D)), 'w_imp': w(ks[8], (C, 1)), 'w_selk': w(ks[9], (C, N_HEAD * (NOPE + ROPE_D))), 'w_selv': w(ks[10], (C, N_HEAD * V_HEAD)), 'w_wink': w(ks[11], (C, N_HEAD * (NOPE + ROPE_D))), 'w_winv': w(ks[12], (C, N_HEAD * V_HEAD)), 'w_gate': w(ks[13], (C, 3)), 'w_proj': w(ks[14], (N_HEAD * V_HEAD, C))}
    _L0_attn_in = _L0_attn_setup()

    def _L0_ffn_setup():
        import jax, jax.numpy as jnp
        import numpy as np
        N_EXPERTS = 8
        CAP_FACTOR = 1.25
        BATCH, SEQ, DMODEL, DFF = (4, 512, 256, 1024)
        key = jax.random.key(seed)
        k0, k1, k2, k3 = jax.random.split(key, 4)
        x = jax.random.normal(k0, (BATCH, SEQ, DMODEL), dtype=jnp.float32)
        Wr = jax.random.normal(k1, (DMODEL, N_EXPERTS), dtype=jnp.float32) * 0.02
        W1 = jax.random.normal(k2, (N_EXPERTS, DMODEL, DFF), dtype=jnp.float32) * 0.02
        W2 = jax.random.normal(k3, (N_EXPERTS, DFF, DMODEL), dtype=jnp.float32) * 0.02
        return {'x': x, 'Wr': Wr, 'W1': W1, 'W2': W2}
    _L0_ffn_in = _L0_ffn_setup()
    _d = {'L0_attn_x': _L0_attn_in['x'], 'L0_attn_w_cq': _L0_attn_in['w_cq'], 'L0_attn_g_qnorm': _L0_attn_in['g_qnorm'], 'L0_attn_w_dq_nope': _L0_attn_in['w_dq_nope'], 'L0_attn_w_dq_rope': _L0_attn_in['w_dq_rope'], 'L0_attn_w_ckv': _L0_attn_in['w_ckv'], 'L0_attn_g_kvnorm': _L0_attn_in['g_kvnorm'], 'L0_attn_w_dk_nope': _L0_attn_in['w_dk_nope'], 'L0_attn_w_dv': _L0_attn_in['w_dv'], 'L0_attn_w_krope': _L0_attn_in['w_krope'], 'L0_attn_w_imp': _L0_attn_in['w_imp'], 'L0_attn_w_selk': _L0_attn_in['w_selk'], 'L0_attn_w_selv': _L0_attn_in['w_selv'], 'L0_attn_w_wink': _L0_attn_in['w_wink'], 'L0_attn_w_winv': _L0_attn_in['w_winv'], 'L0_attn_w_gate': _L0_attn_in['w_gate'], 'L0_attn_w_proj': _L0_attn_in['w_proj'], 'L0_ffn_Wr': _L0_ffn_in['Wr'], 'L0_ffn_W1': _L0_ffn_in['W1'], 'L0_ffn_W2': _L0_ffn_in['W2']}
    _x0 = _d['L0_attn_x']
    _d['L0_attn_x'] = jax.random.normal(jax.random.fold_in(jax.random.key(seed), 1), (4, 1024, 256), dtype=_x0.dtype)
    del _x0
    return _d

def reference(L0_attn_x, L0_attn_w_cq, L0_attn_g_qnorm, L0_attn_w_dq_nope, L0_attn_w_dq_rope, L0_attn_w_ckv, L0_attn_g_kvnorm, L0_attn_w_dk_nope, L0_attn_w_dv, L0_attn_w_krope, L0_attn_w_imp, L0_attn_w_selk, L0_attn_w_selv, L0_attn_w_wink, L0_attn_w_winv, L0_attn_w_gate, L0_attn_w_proj, L0_ffn_Wr, L0_ffn_W1, L0_ffn_W2):

    def _L0_attn_ref(x, w_cq, g_qnorm, w_dq_nope, w_dq_rope, w_ckv, g_kvnorm, w_dk_nope, w_dv, w_krope, w_imp, w_selk, w_selv, w_wink, w_winv, w_gate, w_proj):
        import jax, jax.numpy as jnp
        import numpy as np
        import math
        N_HEAD = 16
        V_HEAD = 32
        NOPE = 32
        ROPE_D = 64
        KEEP = 64
        EPS = 1e-06

        def _freqs(T, dim=ROPE_D, theta=10000.0):
            f = 1.0 / theta ** (jnp.arange(0, dim, 2, dtype=jnp.float32) / dim)
            t = jnp.arange(T, dtype=jnp.float32)
            a = jnp.outer(t, f)
            return (jnp.cos(a), jnp.sin(a))

        def _rope(x, cos, sin):
            S = x.shape[-2]
            c = cos[:S][None, None]
            s = sin[:S][None, None]
            x1, x2 = jnp.split(x, 2, axis=-1)
            return jnp.concatenate([x1 * c - x2 * s, x1 * s + x2 * c], axis=-1)

        def _rms(x, g, eps=EPS):
            return x * jax.lax.rsqrt(jnp.mean(x * x, axis=-1, keepdims=True) + eps) * g

        def _attn(q, k, v, causal):
            scale = 1.0 / math.sqrt(q.shape[-1])
            s = jnp.einsum('bhqd,bhkd->bhqk', q, k) * scale
            if causal:
                Tq, Tk = (s.shape[-2], s.shape[-1])
                mask = jnp.tril(jnp.ones((Tq, Tk), dtype=bool))
                s = jnp.where(mask, s, jnp.finfo(s.dtype).min)
            return jnp.einsum('bhqk,bhkd->bhqd', jax.nn.softmax(s, axis=-1), v)

        def _forward(x, w_cq, g_qnorm, w_dq_nope, w_dq_rope, w_ckv, g_kvnorm, w_dk_nope, w_dv, w_krope, w_imp, w_selk, w_selv, w_wink, w_winv, w_gate, w_proj):
            B, T, C = x.shape
            cos, sin = _freqs(T)
            nq = _rms(x @ w_cq, g_qnorm)
            q_nope = (nq @ w_dq_nope).reshape(B, T, N_HEAD, NOPE).transpose(0, 2, 1, 3)
            q_rope = (nq @ w_dq_rope).reshape(B, T, N_HEAD, ROPE_D).transpose(0, 2, 1, 3)
            q_rope = _rope(q_rope, cos, sin)
            q = jnp.concatenate([q_nope, q_rope], axis=-1)
            gate = jax.nn.softmax((x @ w_gate).mean(axis=1), axis=-1)
            ckv = _rms(x @ w_ckv, g_kvnorm)
            k_nope = (ckv @ w_dk_nope).reshape(B, T, N_HEAD, NOPE).transpose(0, 2, 1, 3)
            v1 = (ckv @ w_dv).reshape(B, T, N_HEAD, V_HEAD).transpose(0, 2, 1, 3)
            k_rope = (x @ w_krope).reshape(B, T, 1, ROPE_D).transpose(0, 2, 1, 3) / N_HEAD
            k_rope = _rope(k_rope, cos, sin)
            k1 = jnp.concatenate([k_nope, jnp.broadcast_to(k_rope, (B, N_HEAD, T, ROPE_D))], axis=-1)
            scores = (x @ w_imp)[..., 0]
            _, idx = jax.lax.top_k(scores, KEEP)
            idx = jnp.sort(idx, axis=1)
            sel = jnp.take_along_axis(x, idx[:, :, None], axis=1)
            ks = (sel @ w_selk).reshape(B, KEEP, N_HEAD, NOPE + ROPE_D).transpose(0, 2, 1, 3)
            vs = (sel @ w_selv).reshape(B, KEEP, N_HEAD, V_HEAD).transpose(0, 2, 1, 3)
            ks = jnp.concatenate([ks[..., :NOPE], _rope(ks[..., NOPE:], cos, sin)], axis=-1)
            kw = (x @ w_wink).reshape(B, T, N_HEAD, NOPE + ROPE_D).transpose(0, 2, 1, 3)
            vw = (x @ w_winv).reshape(B, T, N_HEAD, V_HEAD).transpose(0, 2, 1, 3)
            kw = jnp.concatenate([kw[..., :NOPE], _rope(kw[..., NOPE:], cos, sin)], axis=-1)
            a1 = _attn(q, k1, v1, causal=True)
            a2 = _attn(q, ks, vs, causal=False)
            a3 = _attn(q, kw, vw, causal=True)
            g = gate[:, :, None, None, None]
            out = g[:, 0] * a1 + g[:, 1] * a2 + g[:, 2] * a3
            out = out.transpose(0, 2, 1, 3).reshape(B, T, N_HEAD * V_HEAD)
            return out @ w_proj
        return _forward(x, w_cq, g_qnorm, w_dq_nope, w_dq_rope, w_ckv, g_kvnorm, w_dk_nope, w_dv, w_krope, w_imp, w_selk, w_selv, w_wink, w_winv, w_gate, w_proj)

    def _L0_ffn_ref(x, Wr, W1, W2):
        import jax, jax.numpy as jnp
        import numpy as np
        N_EXPERTS = 8
        CAP_FACTOR = 1.25
        BATCH, SEQ, DMODEL, DFF = (4, 512, 256, 1024)
        B, S, D = x.shape
        E = W1.shape[0]
        cap = int(CAP_FACTOR * B * S / E)
        t = x.reshape(-1, D)
        probs = jax.nn.softmax(t @ Wr, axis=-1)
        idx = jnp.argmax(probs, axis=-1)
        pmax = jnp.max(probs, axis=-1)
        onehot = jax.nn.one_hot(idx, E, dtype=jnp.int32)
        pos = jnp.sum(jnp.cumsum(onehot, axis=0) * onehot, axis=-1) - 1
        kept = pos < cap
        flat = idx * cap + jnp.minimum(pos, cap - 1)
        disp = jnp.zeros((E * cap, D), t.dtype).at[flat].add(t * kept[:, None].astype(t.dtype))
        ein = disp.reshape(E, cap, D)
        h = jax.nn.relu(jnp.einsum('ecd,edf->ecf', ein, W1))
        eout = jnp.einsum('ecf,efd->ecd', h, W2).reshape(E * cap, D)
        comb = jnp.where(kept[:, None], eout[flat], t)
        factor = jnp.where(kept, pmax, jnp.ones_like(pmax))
        out = (comb * factor[:, None]).reshape(B, S, D)
        return out
    x = L0_attn_x
    x = x + 0.5 * _L0_ffn_ref(_layernorm(x, axis=-1), L0_ffn_Wr, L0_ffn_W1, L0_ffn_W2)
    x = x + _L0_attn_ref(_layernorm(x, axis=-1), L0_attn_w_cq, L0_attn_g_qnorm, L0_attn_w_dq_nope, L0_attn_w_dq_rope, L0_attn_w_ckv, L0_attn_g_kvnorm, L0_attn_w_dk_nope, L0_attn_w_dv, L0_attn_w_krope, L0_attn_w_imp, L0_attn_w_selk, L0_attn_w_selv, L0_attn_w_wink, L0_attn_w_winv, L0_attn_w_gate, L0_attn_w_proj)
    x = x + 0.5 * _L0_ffn_ref(_layernorm(x, axis=-1), L0_ffn_Wr, L0_ffn_W1, L0_ffn_W2)
    return x

_drawn_inputs = setup_inputs


def setup_inputs(seed=0):
    import zlib

    import numpy as np

    out = dict(_drawn_inputs(seed))
    spreads = {'L0_attn_g_qnorm': (1.0, 0.6), 'L0_attn_g_kvnorm': (1.0, 0.6)}
    factors = {'L0_attn_w_cq': 8.0,
     'L0_attn_w_dq_nope': 8.0,
     'L0_attn_w_dq_rope': 8.0,
     'L0_attn_w_ckv': 8.0,
     'L0_attn_w_dk_nope': 8.0,
     'L0_attn_w_dv': 8.0,
     'L0_attn_w_krope': 27.204,
     'L0_attn_w_imp': 7.29,
     'L0_attn_w_selk': 8.0,
     'L0_attn_w_selv': 6.816,
     'L0_attn_w_wink': 8.0,
     'L0_attn_w_winv': 8.0,
     'L0_attn_w_gate': 8.0,
     'L0_attn_w_proj': 6.257}
    for name, (base, spread) in spreads.items():
        noise = np.random.default_rng([zlib.crc32(name.encode()), seed]).standard_normal(out[name].shape)
        drawn = base * np.exp(spread * noise) if base else spread * noise
        out[name] = jnp.asarray(drawn.astype(out[name].dtype))
    for name, factor in factors.items():
        out[name] = (out[name] * factor).astype(out[name].dtype)
    return out
```

```python
from contextlib import ExitStack

import numpy as np

import concourse.bass as bass
from concourse import mybir

F32 = mybir.dt.float32
F16 = mybir.dt.float16
I32 = mybir.dt.int32
ALU = mybir.AluOpType
ACT = mybir.ActivationFunctionType
AX = mybir.AxisListType.X

P = 128
B, T, C = 4, 1024, 256
N = B * T
NT = N // P
GT = T // P
CK = C // P
E, CAP, F = 8, 640, 1024
SLOTS = E * CAP
ST = CAP // P
FT = F // P
H, HG = 16, 4
G = H // HG
D, NOPE, ROPE, DV = 96, 32, 64, 32
HALF = ROPE // 2
QL, KL = 96, 32
KEEP = 64
LAT = QL + KL + ROPE + 1 + 3
LN_EPS, RMS_EPS = 1e-5, 1e-6
HL = 2

XSC, WSC, QSC = 16.0, 64.0, 16.0
FXSC = 4.0
SHIFT = 256.0
EXP_SCALE = 1.0 / (QSC * QSC * float(np.sqrt(D)))
HIHI, HILO, LOHI = (0, 0), (0, 1), (1, 0)
PRODUCTS = (HIHI, HILO, LOHI)

W_WIN, W_SEL = 0, HL * CK * 3 * P
W_WINV = 2 * HL * CK * 3 * P
W_SELV = W_WINV + HL * CK * P
W_Q = W_SELV + HL * CK * P
W_DK = W_Q + HL * 3 * P
W_DV = W_DK + HL * P
W_COLS = W_DV + HL * P


class Steps:

    def __init__(self, engine, sem, base=0):
        self.engine, self.sem, self.base, self.n = engine, sem, base, 0

    def done(self, ins):
        ins.then_inc(self.sem, 1)
        self.n += 1

    def wait(self):
        self.engine.wait_ge(self.sem, self.base + self.n)

    def one(self, ins):
        self.done(ins)
        self.wait()


def bcast(ap, n):
    return ap.unsqueeze(2).broadcast_to([ap.shape[0], ap.shape[1], n])


def constants():
    ident = np.eye(P, dtype=np.float32)
    upto = np.triu(np.ones((P, P), np.float32))
    inv = (1.0 / np.power(10000.0, np.arange(0, ROPE, 2) / ROPE)).astype(np.float32)
    angle = np.outer(np.arange(T, dtype=np.float32), inv)
    cos, sin = np.cos(angle), np.sin(angle)
    big = (32768.0 * ident).astype(np.float16)
    hide_s = np.where(np.arange(P)[:, None] > np.arange(P)[None, :], -65504.0, 0.0).astype(np.float16)
    return {
        "c_ident": ident,
        "c_upto": upto,
        "c_expert": np.tile(np.arange(E, dtype=np.float32), (P, NT)),
        "c_keep": np.tile(np.arange(KEEP, dtype=np.float32), (P, 1)),
        "c_cosT": np.tile(cos.T, (HG, 1)).astype(np.float32),
        "c_sinT": np.tile(sin.T, (HG, 1)).astype(np.float32),
        "c_cos": cos.astype(np.float32),
        "c_sin": sin.astype(np.float32),
        "c_shift": np.stack([np.stack([np.full((HG, T), SHIFT if r == k else 0.0, np.float16) for r in range(3)])
                             for k in range(3)]),
        "c_mask": np.concatenate([big, hide_s, hide_s.T], axis=1),
    }


def normalize_batch(dve, b, stats_done, steps, eps_added, rstd_done, x_tiles, stats, moments, rstd, out, ready):
    for k in range(GT):
        dve.bn_stats(stats[:, k, :], x_tiles(k)).then_inc(stats_done, 1)
    dve.wait_ge(stats_done, b * GT + GT)
    mean, diff, squares = moments[:, 0, :], moments[:, 1, :], moments[:, 2, :]
    steps.done(dve.tensor_tensor(mean, stats[:, :, 1], stats[:, :, 4], ALU.add))
    steps.done(dve.tensor_tensor(diff, stats[:, :, 1], stats[:, :, 4], ALU.subtract))
    steps.one(dve.tensor_tensor(squares, stats[:, :, 2], stats[:, :, 5], ALU.add))
    steps.done(dve.tensor_scalar(mean, mean, 0.5, None, ALU.mult))
    steps.done(dve.tensor_scalar(squares, squares, 1.0 / C, LN_EPS, ALU.mult, ALU.add))
    steps.one(dve.scalar_tensor_tensor(diff, diff, 0.25, diff, ALU.mult, ALU.mult))
    dve.tensor_tensor(rstd[:, :], squares, diff, ALU.add).then_inc(eps_added, 1)
    dve.wait_ge(rstd_done, b + 1)
    for k in range(GT):
        ready(k, dve.tensor_scalar(out[:, k, :], x_tiles(k), mean[:, k:k + 1], rstd[:, k:k + 1],
                                   ALU.subtract, ALU.mult))


NORM_STEPS = 6


def inverse_deviation(pool, b, eps_added, rstd_done, rstd, minus_half):
    pool.wait_ge(eps_added, b + 1)
    pool.tensor_tensor(rstd[:, :], rstd[:, :], minus_half[:, 0:GT], ALU.pow).then_inc(rstd_done, 1)


def ffn(nc, name, X, dram, consts, xin, xout):
    disp, eout = dram["disp" + name], dram["eout" + name]
    with ExitStack() as ctx:
        def sb(n, shape, dt=F32):
            return ctx.enter_context(nc.sbuf_tensor(name + n, shape, dt))

        XN = sb("XN", [P, NT, C])
        w_kept = sb("w_kept", [P, NT])
        w_lost = sb("w_lost", [P, NT])
        take = sb("take", [P, NT], I32)
        put = sb("put", [P, NT], I32)
        route_tokens(nc, name, X, XN, w_kept, w_lost, take, put, disp, dram, consts, xin)
        run_experts(nc, name, disp, eout, dram, consts)
        combine(nc, name, X, XN, w_kept, w_lost, take, eout, xout)


def route_tokens(nc, name, X, XN, w_kept, w_lost, take, put, disp, dram, consts, xin):
    with ExitStack() as ctx:
        def sb(n, shape, dt=F32):
            return ctx.enter_context(nc.sbuf_tensor(name + n, shape, dt))

        def pb(n, shape, dt=F32):
            return ctx.enter_context(nc.psum_tensor(name + n, shape, dt))

        def sem(n):
            return nc.alloc_semaphore(name + n)

        ident, upto, ones, expert = (sb(n, s) for n, s in (
            ("ident", [P, P]), ("upto", [P, P]), ("ones", [P, P]), ("expert", [P, NT, E])))
        minus_half = sb("minus_half", [P, GT])
        half_set = sem("half_set")
        wr = sb("wr", [P, CK, E])
        zeros = sb("zeros", [P, 10 * C])
        stats, moments, rstd = sb("stats", [P, GT, 6]), sb("moments", [P, 3, GT]), sb("rstd", [P, GT])
        XS = sb("XS", [P, GT, C])
        XT = sb("XT", [P, 2, C])
        logit = sb("logit", [P, NT, E])
        top, sume, idx, used, kept, slot, tmp = (sb(n, [P, NT]) for n in
                                                 ("top", "sume", "idx", "used", "kept", "slot", "tmp"))
        d8, e8, eq, cand, onehot, run, pos = (sb(n, [P, NT, E]) for n in
                                              ("d8", "e8", "eq", "cand", "onehot", "run", "pos"))
        psT, psL = pb("psT", [P, 2, 512]), pb("psL", [P, 2, 512])
        psC = pb("psC", [P, 2, NT, E])

        loaded, const_in, zeroed, zero_set, ones_set = (sem(n) for n in
                                              ("loaded", "const_in", "zeroed", "zero_set", "ones_set"))
        norm_ready, kept_copy, step = sem("norm_ready"), sem("kept_copy"), sem("step")
        stats_done, eps_added, rstd_done = (sem(n) for n in ("stats_done", "eps_added", "rstd_done"))
        turned, xt_ready, logits_mm, logits_out = (sem(n) for n in
                                                   ("turned", "xt_ready", "logits_mm", "logits_out"))
        shifted, expd, hot, counted, routed, sent = (sem(n) for n in
                                                     ("shifted", "expd", "hot", "counted", "routed", "sent"))
        block = ctx.enter_context(nc.Block())

        @block.sync
        def _(sp):
            if xin is not None:
                for b in range(B):
                    sp.dma_start(X[:, b * GT:(b + 1) * GT, :],
                                 xin.rearrange("(i p) c -> p i c", p=P)[:, b * GT:(b + 1) * GT, :]).then_inc(loaded, 16)
            sp.dma_start(ident[:, :], consts["c_ident"]).then_inc(const_in, 16)
            sp.dma_start(upto[:, :], consts["c_upto"]).then_inc(const_in, 16)
            sp.dma_start(expert[:, :, :], consts["c_expert"].rearrange("p (i e) -> p i e", e=E)).then_inc(const_in, 16)
            sp.dma_start(wr[:, :, :], dram["Wr"].rearrange("(k p) e -> p k e", p=P)).then_inc(const_in, 16)
            sp.wait_ge(zero_set, 1)
            for q in range(SLOTS // (10 * P)):
                sp.dma_start(disp.rearrange("(q p i) c -> q p (i c)", p=P, i=10)[q], zeros[:, :]).then_inc(zeroed, 16)

        @block.gpsimd
        def _(pool):
            pool.memset(zeros[:, :], 0.0).then_inc(zero_set, 1)
            pool.memset(ones[:, :], 1.0).then_inc(ones_set, 1)
            pool.memset(minus_half[:, :], -0.5).then_inc(half_set, 1)
            pool.wait_ge(half_set, 1)
            with pool.Fori(0, B) as b:
                inverse_deviation(pool, b, eps_added, rstd_done, rstd, minus_half)
                for k in range(GT):
                    pool.wait_ge(norm_ready, b * GT + (k + 1))
                    pool.wait_ge(norm_ready, 1)
                    pool.tensor_copy(XN[:, bass.ds(b * GT + k, 1), :].rearrange("p a c -> p (a c)"), XS[:, k, :]).then_inc(kept_copy, 1)
            pool.wait_ge(kept_copy, NT)
            pool.wait_ge(zeroed, 16 * (SLOTS // (10 * P)))
            pool.wait_ge(routed, 2)
            for i in range(NT):
                pool.indirect_dma_start(
                    out=disp, out_offset=bass.IndirectOffsetOnAxis(ap=put[:, i:i + 1], axis=0),
                    in_=XN[:, i, :], in_offset=None, bounds_check=SLOTS - 1, oob_is_err=False).then_inc(sent, 16)
            pool.wait_ge(sent, 16 * NT)

        @block.vector
        def _(dve):
            if xin is not None:
                dve.wait_ge(loaded, 16 * B)
            with dve.Fori(0, B) as b:
                dve.wait_ge(turned, b * GT)
                dve.wait_ge(kept_copy, b * GT)
                normalize_batch(dve, b, stats_done, Steps(dve, step, b * NORM_STEPS), eps_added, rstd_done, lambda k: X[:, bass.ds(b * GT + k, 1), :].rearrange("p a c -> p (a c)"),
                                stats, moments, rstd, XS, lambda k, ins: ins.then_inc(norm_ready, 1))
            steps = Steps(dve, step, B * NORM_STEPS)
            dve.wait_ge(logits_out, B)
            steps.one(dve.tensor_reduce(top[:, :], logit[:, :, :], AX, ALU.max))
            dve.tensor_tensor(d8[:, :, :], logit[:, :, :], bcast(top[:, :], E), ALU.subtract).then_inc(shifted, 1)
            dve.wait_ge(shifted, 1)
            steps.one(dve.tensor_scalar(eq[:, :, :], d8[:, :, :], 0.0, -float(E), ALU.is_ge, ALU.mult))
            dve.wait_ge(const_in, 64)
            steps.one(dve.scalar_tensor_tensor(cand[:, :, :], eq[:, :, :], float(E), expert[:, :, :], ALU.add, ALU.add))
            steps.one(dve.tensor_reduce(idx[:, :], cand[:, :, :], AX, ALU.min))
            dve.tensor_tensor(onehot[:, :, :], expert[:, :, :], bcast(idx[:, :], E), ALU.is_equal).then_inc(hot, 1)
            dve.wait_ge(expd, 1)
            steps.one(dve.tensor_reduce(sume[:, :], e8[:, :, :], AX, ALU.add))
            steps.one(dve.reciprocal(top[:, :], sume[:, :]))
            dve.wait_ge(counted, 1)
            for e in range(E):
                steps.done(dve.tensor_tensor_scan(run[:, :, e], ones[:, 0:NT], psC[:, 1, :, e], 0.0, ALU.mult, ALU.add))
            steps.wait()
            steps.one(dve.tensor_tensor(run[:, :, :], run[:, :, :], psC[:, 1, :, :], ALU.subtract))
            steps.one(dve.tensor_tensor(run[:, :, :], run[:, :, :], psC[:, 0, :, :], ALU.add))
            steps.one(dve.tensor_tensor(pos[:, :, :], run[:, :, :], onehot[:, :, :], ALU.mult))
            steps.one(dve.tensor_reduce(used[:, :], pos[:, :, :], AX, ALU.add))
            steps.one(dve.tensor_scalar(kept[:, :], used[:, :], float(CAP), None, ALU.is_le))
            steps.one(dve.scalar_tensor_tensor(w_kept[:, :], top[:, :], 0.5, kept[:, :], ALU.mult, ALU.mult))
            steps.one(dve.tensor_scalar(w_lost[:, :], kept[:, :], -0.5, 0.5, ALU.mult, ALU.add))
            steps.one(dve.tensor_scalar(tmp[:, :], used[:, :], float(CAP), -1.0, ALU.min, ALU.add))
            steps.one(dve.scalar_tensor_tensor(slot[:, :], idx[:, :], float(CAP), tmp[:, :], ALU.mult, ALU.add))
            dve.tensor_copy(take[:, :], slot[:, :]).then_inc(routed, 1)
            steps.one(dve.scalar_tensor_tensor(tmp[:, :], w_lost[:, :], float(4 * SLOTS), slot[:, :], ALU.mult, ALU.add))
            dve.tensor_copy(put[:, :], tmp[:, :]).then_inc(routed, 1)

        @block.scalar
        def _(act):
            with act.Fori(0, B) as b:
                for k in range(GT):
                    act.wait_ge(turned, b * GT + (k + 1))
                    act.activation(XT[:, k % 2, :], psT[:, k % 2, 0:C], ACT.Copy).then_inc(xt_ready, 1)
                act.wait_ge(logits_mm, b * GT + GT)
                act.activation(logit[:, bass.ds(b * GT, GT), :], psL[:, 0, 0:GT * E], ACT.Copy).then_inc(logits_out, 1)
            act.wait_ge(shifted, 1)
            act.activation(e8[:, :, :], d8[:, :, :], ACT.Exp).then_inc(expd, 1)

        @block.tensor
        def _(pe):
            pe.wait_ge(const_in, 64)

            def turn(b, k):
                pe.wait_ge(norm_ready, b * GT + (k + 1))
                if k >= 2:
                    pe.wait_ge(logits_mm, b * GT + (k - 1))
                for c in range(CK):
                    last = pe.transpose(psT[:, k % 2, c * P:(c + 1) * P], XS[:, k, c * P:(c + 1) * P], ident[:, :])
                last.then_inc(turned, 1)

            def router(b, k):
                pe.wait_ge(xt_ready, b * GT + (k + 1))
                if k == 0:
                    pe.wait_ge(logits_out, b)
                for c in range(CK):
                    last = pe.matmul(psL[:, 0, k * E:(k + 1) * E], XT[:, k % 2, c * P:(c + 1) * P], wr[:, c, :],
                                     start=(c == 0), stop=(c == CK - 1))
                last.then_inc(logits_mm, 1)

            with pe.Fori(0, B) as b:
                pe.wait_ge(logits_out, b)
                turn(b, 0)
                for k in range(GT):
                    if k + 1 < GT:
                        turn(b, k + 1)
                    router(b, k)
            pe.wait_ge(hot, 1)
            pe.wait_ge(ones_set, 1)
            flat = onehot[:, :, :].rearrange("p i e -> p (i e)")
            pe.matmul(psC[:, 0, :, :].rearrange("p i e -> p (i e)"), upto[:, :], flat, start=True, stop=True)
            pe.matmul(psC[:, 1, :, :].rearrange("p i e -> p (i e)"), ones[:, :], flat, start=True, stop=True).then_inc(counted, 1)


def run_experts(nc, name, disp, eout, dram, consts):
    PAIR = 2
    with ExitStack() as ctx:
        def sb(n, shape, dt=F32):
            return ctx.enter_context(nc.sbuf_tensor(name + n, shape, dt))

        def pb(n, shape, dt=F32):
            return ctx.enter_context(nc.psum_tensor(name + n, shape, dt))

        def sem(n):
            return nc.alloc_semaphore(name + n)

        ident = sb("ident2", [P, P])
        rows = sb("rows", [P, PAIR, ST, C])
        w1, w2 = sb("w1", [P, PAIR, CK, F]), sb("w2", [P, PAIR, FT, C])
        w1s, w2s = sb("w1s", [P, PAIR, HL, CK, F], F16), sb("w2s", [P, PAIR, HL, FT, C], F16)
        xT = sb("xT", [P, PAIR, HL, CK, CAP], F16)
        hT = sb("hT", [P, PAIR, HL, FT, CAP], F16)
        res = sb("res", [P, PAIR, ST, C])
        psT = pb("psTe", [P, 2, 512])
        psH = pb("psH", [P, 2, 2, 512])
        psO = pb("psO", [P, 2, 512])
        HC = CAP // 2

        ident_in = sem("ident_in")
        rows_in = [sem(f"rows_in{e}") for e in range(PAIR)]
        w_in = [sem(f"w_in{e}") for e in range(PAIR)]
        w_hi, w_lo = sem("w_hi"), sem("w_lo")
        turned, x_hi, x_lo = sem("turned2"), sem("x_hi"), sem("x_lo")
        hidden, h_hi, h_lo = sem("hidden"), sem("h_hi"), sem("h_lo")
        summed, res_ready = sem("summed"), sem("res_ready")
        stored = [sem(f"stored{e}") for e in range(PAIR)]
        blocks = [(c, s) for c in range(CK) for s in range(ST)]
        jobs = [blocks[j:j + 4] for j in range(0, len(blocks), 4)]
        NJ = len(jobs)
        block = ctx.enter_context(nc.Block())

        @block.sync
        def _(sp):
            sp.dma_start(ident[:, :], consts["c_ident"]).then_inc(ident_in, 16)
            with sp.Fori(0, E // PAIR) as t:
                for e in range(PAIR):
                    sp.wait_ge(turned, t * (PAIR * NJ))
                    sp.dma_start(rows[:, e, :, :],
                                 disp.rearrange("(x s p) c -> x p s c", s=ST, p=P)[bass.ds(t * PAIR + e, 1)].rearrange("x p s c -> p (x s) c")).then_inc(rows_in[e], 16)
                    sp.wait_ge(w_lo, t * (2 * PAIR))
                    sp.dma_start(w1[:, e, :, :], dram["W1"].rearrange("x (k p) f -> x p k f", p=P)[bass.ds(t * PAIR + e, 1)].rearrange("x p k f -> p (x k) f")).then_inc(w_in[e], 16)
                    sp.dma_start(w2[:, e, :, :], dram["W2"].rearrange("x (k p) c -> x p k c", p=P)[bass.ds(t * PAIR + e, 1)].rearrange("x p k c -> p (x k) c")).then_inc(w_in[e], 16)

        @block.gpsimd
        def _(pool):
            with pool.Fori(0, E // PAIR) as t:
                for e in range(PAIR):
                    pool.wait_ge(res_ready, t * (PAIR * ST) + ST * (e + 1))
                    pool.dma_start(eout.rearrange("(x s p) c -> x p s c", s=ST, p=P)[bass.ds(t * PAIR + e, 1)].rearrange("x p s c -> p (x s) c"), res[:, e, :, :]).then_inc(stored[e], 16)
            for e in range(PAIR):
                pool.wait_ge(stored[e], 16 * (E // PAIR))

        @block.scalar
        def _(act):
            with act.Fori(0, E // PAIR) as t:
                for e in range(PAIR):
                    act.wait_ge(w_in[e], t * 32 + 32)
                    act.wait_ge(summed, t * (PAIR * ST))
                    act.activation(w1s[:, e, 0, :, :], w1[:, e, :, :], ACT.Copy, scale=WSC).then_inc(w_hi, 1)
                    act.activation(w2s[:, e, 0, :, :], w2[:, e, :, :], ACT.Copy, scale=WSC).then_inc(w_hi, 1)
                    for j, job in enumerate(jobs):
                        if j == 0:
                            act.wait_ge(hidden, t * (PAIR * FT))
                        act.wait_ge(turned, t * (PAIR * NJ) + (e * NJ + j + 1))
                        o = j * 4 * P
                        n = len(job) * P
                        act.activation(xT[:, e, 0, :, :].rearrange("p k s -> p (k s)")[:, o:o + n],
                                       psT[:, (e * NJ + j) % 2, 0:n], ACT.Copy, scale=FXSC).then_inc(x_hi, 1)
                for e in range(PAIR):
                    for f in range(FT):
                        if f == 0:
                            act.wait_ge(summed, t * (PAIR * ST))
                        act.wait_ge(hidden, t * (PAIR * FT) + (e * FT + f + 1))
                        act.activation(hT[:, e, 0, f, :].rearrange("p (n s) -> p n s", n=2), psH[:, f % 2, :, 0:HC],
                                       ACT.Relu).then_inc(h_hi, 1)
                for e in range(PAIR):
                    act.wait_ge(stored[e], t * 16)
                    for s in range(ST):
                        act.wait_ge(summed, t * (PAIR * ST) + (e * ST + s + 1))
                        act.activation(res[:, e, s, :], psO[:, (e * ST + s) % 2, 0:C], ACT.Copy,
                                       scale=1.0 / (FXSC * WSC * WSC)).then_inc(res_ready, 1)

        @block.vector
        def _(dve):
            with dve.Fori(0, E // PAIR) as t:
                for e in range(PAIR):
                    for n, (raw, split) in enumerate(((w1, w1s), (w2, w2s))):
                        dve.wait_ge(w_hi, t * (2 * PAIR) + (2 * e + n + 1))
                        dve.scalar_tensor_tensor(split[:, e, 1, :, :], raw[:, e, :, :], WSC, split[:, e, 0, :, :],
                                                 ALU.mult, ALU.subtract).then_inc(w_lo, 1)
                    for j, job in enumerate(jobs):
                        dve.wait_ge(x_hi, t * (PAIR * NJ) + (e * NJ + j + 1))
                        o = j * 4 * P
                        n = len(job) * P
                        dve.scalar_tensor_tensor(xT[:, e, 1, :, :].rearrange("p k s -> p (k s)")[:, o:o + n],
                                                 psT[:, (e * NJ + j) % 2, 0:n], FXSC,
                                                 xT[:, e, 0, :, :].rearrange("p k s -> p (k s)")[:, o:o + n],
                                                 ALU.mult, ALU.subtract).then_inc(x_lo, 1)
                for e in range(PAIR):
                    for f in range(FT):
                        dve.wait_ge(h_hi, t * (PAIR * FT) + (e * FT + f + 1))
                        dve.scalar_tensor_tensor(hT[:, e, 1, f, :].rearrange("p (n s) -> p n s", n=2), psH[:, f % 2, :, 0:HC], 0.0,
                                                 hT[:, e, 0, f, :].rearrange("p (n s) -> p n s", n=2), ALU.max, ALU.subtract).then_inc(h_lo, 1)

        @block.tensor
        def _(pe):
            pe.wait_ge(ident_in, 16)
            with pe.Fori(0, E // PAIR) as t:
                for e in range(PAIR):
                    pe.wait_ge(rows_in[e], t * 16 + 16)
                    for j, job in enumerate(jobs):
                        m = e * NJ + j - 1
                        pe.wait_ge(x_lo, t * (PAIR * NJ) + m if m > 0 else t * (PAIR * NJ))
                        for q, (c, s) in enumerate(job):
                            last = pe.transpose(psT[:, (e * NJ + j) % 2, q * P:(q + 1) * P],
                                                rows[:, e, s, c * P:(c + 1) * P], ident[:, :])
                        last.then_inc(turned, 1)
                for e in range(PAIR):
                    pe.wait_ge(x_lo, t * (PAIR * NJ) + NJ * (e + 1))
                    pe.wait_ge(w_lo, t * (2 * PAIR) + 2 * (e + 1))
                    for f in range(FT):
                        m = e * FT + f - 1
                        pe.wait_ge(h_lo, t * (PAIR * FT) + m if m > 0 else t * (PAIR * FT))
                        for c in range(CK):
                            for a, b in PRODUCTS:
                                for n in range(2):
                                    last = pe.matmul(psH[:, f % 2, n, 0:HC], w1s[:, e, a, c, f * P:(f + 1) * P],
                                                     xT[:, e, b, c, n * HC:(n + 1) * HC],
                                                     start=(c == 0 and (a, b) == HIHI),
                                                     stop=(c == CK - 1 and (a, b) == LOHI))
                        last.then_inc(hidden, 1)
                for e in range(PAIR):
                    pe.wait_ge(h_lo, t * (PAIR * FT) + FT * (e + 1))
                    for s in range(ST):
                        m = e * ST + s - 1
                        pe.wait_ge(res_ready, t * (PAIR * ST) + m if m > 0 else t * (PAIR * ST))
                        for f in range(FT):
                            for a, b in PRODUCTS:
                                last = pe.matmul(psO[:, (e * ST + s) % 2, 0:C], hT[:, e, a, f, s * P:(s + 1) * P],
                                                 w2s[:, e, b, f, :], start=(f == 0 and (a, b) == HIHI),
                                                 stop=(f == FT - 1 and (a, b) == LOHI))
                        last.then_inc(summed, 1)


def combine(nc, name, X, XN, w_kept, w_lost, take, eout, xout):
    with ExitStack() as ctx:
        R = ctx.enter_context(nc.sbuf_tensor(name + "R", [P, NT, C], F32))
        LOT = 4
        got = [nc.alloc_semaphore(f"{name}got{i}") for i in range(NT // LOT)]
        mixed, ready, stored = (nc.alloc_semaphore(name + n) for n in ("mixed", "ready", "xstored"))
        block = ctx.enter_context(nc.Block())

        @block.gpsimd
        def _(pool):
            for i in range(NT):
                pool.indirect_dma_start(
                    out=R[:, i, :], out_offset=None, in_=eout,
                    in_offset=bass.IndirectOffsetOnAxis(ap=take[:, i:i + 1], axis=0),
                    bounds_check=SLOTS - 1, oob_is_err=False).then_inc(got[i // LOT], 16)

        @block.vector
        def _(dve):
            for i in range(NT):
                dve.scalar_tensor_tensor(X[:, i, :], XN[:, i, :], w_lost[:, i:i + 1], X[:, i, :], ALU.mult, ALU.add).then_inc(mixed, 1)
            for i in range(NT):
                if i % LOT == 0:
                    dve.wait_ge(got[i // LOT], 16 * LOT)
                dve.wait_ge(mixed, i + 1)
                dve.scalar_tensor_tensor(X[:, i, :], R[:, i, :], w_kept[:, i:i + 1], X[:, i, :], ALU.mult, ALU.add).then_inc(ready, 1)

        @block.sync
        def _(sp):
            for i in range(0, NT, LOT):
                sp.wait_ge(ready, i + LOT)
                sp.dma_start(xout.rearrange("(i p) c -> p i c", p=P)[:, i:i + LOT, :], X[:, i:i + LOT, :]).then_inc(stored, 16)
            sp.wait_ge(stored, 16 * (NT // LOT))


def split_weights(nc, dram, wsplit):
    with ExitStack() as ctx:
        def sb(n, shape, dt=F32):
            return ctx.enter_context(nc.sbuf_tensor("ws_" + n, shape, dt))

        def sem(n):
            return nc.alloc_semaphore("ws_" + n)

        win, sel = sb("win", [P, CK, H * D]), sb("sel", [P, CK, H * D])
        winv, selv = sb("winv", [P, CK, H * DV]), sb("selv", [P, CK, H * DV])
        qn, qr = sb("qn", [QL, H * NOPE]), sb("qr", [QL, H * ROPE])
        dk, dv = sb("dk", [P, H * NOPE]), sb("dv", [P, H * DV])
        out = sb("out", [P, G, W_COLS], F16)
        loaded, hi_done, lo_done, stored = sem("loaded"), sem("hi_done"), sem("lo_done"), sem("stored")

        def pieces():
            for raw, at in ((win, W_WIN), (sel, W_SEL)):
                dst = out[:, :, at:at + HL * CK * 3 * P].rearrange(
                    "p g (l k y h d) -> p g l k y h d", l=HL, k=CK, y=3, h=HG)
                src = raw[:, :, :].rearrange("p k (g h y d) -> p k g h y d", g=G, h=HG, y=3)
                for k in range(CK):
                    for y in range(3):
                        yield src[:, k, :, :, y, :], dst[:, :, 0, k, y, :, :], dst[:, :, 1, k, y, :, :]
            for raw, at in ((winv, W_WINV), (selv, W_SELV)):
                dst = out[:, :, at:at + HL * CK * P].rearrange("p g (l k h d) -> p g l k h d", l=HL, k=CK, h=HG)
                src = raw[:, :, :].rearrange("p k (g h d) -> p k g h d", g=G, h=HG)
                for k in range(CK):
                    yield src[:, k], dst[:, :, 0, k], dst[:, :, 1, k]
            dst = out[0:QL, :, W_Q:W_Q + HL * 3 * P].rearrange("p g (l y h d) -> p g l y h d", l=HL, y=3, h=HG)
            yield qn[:, :].rearrange("p (g h d) -> p g h d", g=G, h=HG), dst[:, :, 0, 0], dst[:, :, 1, 0]
            src = qr[:, :].rearrange("p (g h y d) -> p g h y d", g=G, h=HG, y=2)
            for y in range(2):
                yield src[:, :, :, y, :], dst[:, :, 0, 1 + y], dst[:, :, 1, 1 + y]
            for raw, at in ((dk, W_DK), (dv, W_DV)):
                dst = out[QL:P, :, at:at + HL * P].rearrange("p g (l h d) -> p g l h d", l=HL, h=HG)
                yield raw[QL:P, :].rearrange("p (g h d) -> p g h d", g=G, h=HG), dst[:, :, 0], dst[:, :, 1]

        block = ctx.enter_context(nc.Block())

        @block.sync
        def _(sp):
            for dst, name in ((win, "w_wink"), (sel, "w_selk"), (winv, "w_winv"), (selv, "w_selv")):
                sp.dma_start(dst[:, :, :], dram[name].rearrange("(k p) n -> p k n", p=P)).then_inc(loaded, 16)
            sp.dma_start(qn[:, :], dram["w_dq_nope"]).then_inc(loaded, 16)
            sp.dma_start(qr[:, :], dram["w_dq_rope"]).then_inc(loaded, 16)
            sp.dma_start(dk[QL:P, :], dram["w_dk_nope"]).then_inc(loaded, 16)
            sp.dma_start(dv[QL:P, :], dram["w_dv"]).then_inc(loaded, 16)
            sp.wait_ge(lo_done, len(list(pieces())))
            for g in range(G):
                sp.dma_start(wsplit[g, :, 0:W_Q], out[:, g, 0:W_Q]).then_inc(stored, 16)
                sp.dma_start(wsplit[g, 0:QL, W_Q:W_DK], out[0:QL, g, W_Q:W_DK]).then_inc(stored, 16)
                sp.dma_start(wsplit[g, QL:P, W_DK:W_COLS], out[QL:P, g, W_DK:W_COLS]).then_inc(stored, 16)
            sp.wait_ge(stored, 3 * G * 16)

        @block.scalar
        def _(act):
            act.wait_ge(loaded, 8 * 16)
            for src, hi, _lo in pieces():
                act.activation(hi, src, ACT.Copy, scale=WSC).then_inc(hi_done, 1)

        @block.vector
        def _(dve):
            for n, (src, hi, lo) in enumerate(pieces()):
                dve.wait_ge(hi_done, n + 1)
                dve.scalar_tensor_tensor(lo, src, WSC, hi, ALU.mult, ALU.subtract).then_inc(lo_done, 1)


def latents(nc, X, dram, consts, s):
    with ExitStack() as ctx:
        def sb(n, shape, dt=F32):
            return ctx.enter_context(nc.sbuf_tensor("l_" + n, shape, dt))

        def pb(n, shape, dt=F32):
            return ctx.enter_context(nc.psum_tensor("l_" + n, shape, dt))

        def sem(n):
            return nc.alloc_semaphore("l_" + n)

        ident, mean_of = sb("ident", [P, P]), sb("mean_of", [P, P])
        minus_half = sb("minus_half", [P, 2 * GT])
        cos, sin = sb("cos", [P, GT, HALF]), sb("sin", [P, GT, HALF])
        gain = sb("gain", [P, 2])
        wlat = sb("wlat", [P, CK, LAT])
        stats, moments, rstd = sb("stats", [P, GT, 6]), sb("moments", [P, 3, GT]), sb("rstd", [P, GT])
        XS = sb("XS", [P, GT, C])
        XT = sb("XT", [P, 2, C])
        XB = sb("XB", [P, CK, HL, T], F16)
        lat = sb("lat", [P, GT, LAT])
        sq, ss = sb("sq", [P, GT, QL + KL]), sb("ss", [P, 2 * GT])
        nc_ = sb("normed", [P, GT, QL + KL + ROPE])
        rt = sb("rt", [P, 4, GT, HALF])
        NB, RB = sb("NB", [P, HL, T], F16), sb("RB", [ROPE, HL, T], F16)
        scores, gl = sb("scores", [P, NT]), sb("gl", [P, B, 3])
        psT, psL, psN, psG = pb("psT", [P, 2, 512]), pb("psL", [P, 2, 512]), pb("psN", [P, 2, 512]), pb("psG", [P, 512])

        const_in, set_, gained = sem("const_in"), sem("set"), sem("gained")
        stats_done, step, eps_added, rstd_done = sem("stats_done"), sem("step"), sem("eps_added"), sem("rstd_done")
        norm_ready, turned, xt_ready, x_hi, x_lo = (sem(n) for n in
                                                    ("norm_ready", "turned", "xt_ready", "x_hi", "x_lo"))
        lat_mm, lat_out, sums, rms, ready = (sem(n) for n in ("lat_mm", "lat_out", "sums", "rms", "ready"))
        turned2, n_hi, n_lo, gate_mm, gate_out = (sem(n) for n in
                                                  ("turned2", "n_hi", "n_lo", "gate_mm", "gate_out"))
        score_out, stored_x, stored_n, stored_s = sem("score_out"), sem("stored_x"), sem("stored_n"), sem("stored_s")
        STEPS = NORM_STEPS + 12
        CONSTS = 10 * 16
        block = ctx.enter_context(nc.Block())

        @block.sync
        def _(sp):
            sp.dma_start(ident[:, :], consts["c_ident"]).then_inc(const_in, 16)
            sp.dma_start(cos[:, :, :], consts["c_cos"].rearrange("(i p) d -> p i d", p=P)).then_inc(const_in, 16)
            sp.dma_start(sin[:, :, :], consts["c_sin"].rearrange("(i p) d -> p i d", p=P)).then_inc(const_in, 16)
            sp.dma_start(gain[0:QL, 0:1], dram["g_qnorm"].rearrange("(p a) -> p a", a=1)).then_inc(const_in, 16)
            sp.dma_start(gain[QL:P, 0:1], dram["g_kvnorm"].rearrange("(p a) -> p a", a=1)).then_inc(const_in, 16)
            at = 0
            for name, n in (("w_cq", QL), ("w_ckv", KL), ("w_krope", ROPE), ("w_imp", 1), ("w_gate", 3)):
                sp.dma_start(wlat[:, :, at:at + n], dram[name].rearrange("(k p) n -> p k n", p=P),
                             allow_slow_non_contiguous=(n == 1)).then_inc(const_in, 16)
                at += n
            with sp.Fori(0, B) as b:
                sp.wait_ge(norm_ready, b * GT + GT)
                sp.dma_start(s["xn"].rearrange("(b i p) c -> b p i c", p=P, i=GT)[bass.ds(b, 1)].rearrange("b p i c -> p (b i) c"), XS[:, :, :]).then_inc(stored_s, 16)
                sp.wait_ge(x_lo, b * GT + GT)
                sp.dma_start(s["xt"][bass.ds(b, 1)].rearrange("b p n -> p (b n)"),
                             XB[:, :, :, :].rearrange("p k l t -> p (k l t)")).then_inc(stored_x, 16)
                sp.wait_ge(n_lo, b * (2 * GT) + 2 * GT)
                sp.dma_start(s["kr"][bass.ds(b, 1)].rearrange("b p n -> p (b n)"),
                             RB[:, :, :].rearrange("p l t -> p (l t)")).then_inc(stored_n, 16)
                sp.dma_start(s["lat"][bass.ds(b, 1)].rearrange("b p n -> p (b n)"),
                             NB[:, :, :].rearrange("p l t -> p (l t)")).then_inc(stored_n, 16)
            sp.wait_ge(stored_x, 16 * B)
            sp.wait_ge(stored_n, 32 * B)
            sp.wait_ge(stored_s, 16 * B)
            sp.wait_ge(score_out, B)
            sp.wait_ge(gate_out, B)
            sp.dma_start(s["score_n"], scores[:, :]).then_inc(stored_x, 16)
            sp.dma_start(s["gl"], gl[:, :, :].rearrange("p b g -> p (b g)")).then_inc(stored_x, 16)
            sp.wait_ge(stored_x, 16 * B + 32)

        @block.gpsimd
        def _(pool):
            pool.memset(minus_half[:, :], -0.5).then_inc(set_, 1)
            pool.memset(mean_of[:, :], 1.0 / T).then_inc(set_, 1)
            pool.wait_ge(const_in, CONSTS)
            pool.tensor_scalar(gain[:, 1:2], gain[:, 0:1], XSC, None, ALU.mult).then_inc(gained, 1)
            pool.wait_ge(set_, 2)
            with pool.Fori(0, B) as b:
                inverse_deviation(pool, b, eps_added, rstd_done, rstd, minus_half)
                pool.wait_ge(sums, b + 1)
                pool.tensor_tensor(ss[:, :], ss[:, :], minus_half[:, :], ALU.pow).then_inc(rms, 1)

        @block.vector
        def _(dve):
            dve.wait_ge(const_in, CONSTS)
            dve.wait_ge(gained, 1)
            with dve.Fori(0, B) as b:
                steps = Steps(dve, step, b * STEPS)
                dve.wait_ge(turned, b * GT)
                dve.wait_ge(stored_s, b * 16)
                normalize_batch(dve, b, stats_done, steps, eps_added, rstd_done,
                                lambda k: X[:, bass.ds(b * GT + k, 1), :].rearrange("p a c -> p (a c)"),
                                stats, moments, rstd, XS, lambda k, ins: ins.then_inc(norm_ready, 1))
                for k in range(GT):
                    dve.wait_ge(x_hi, b * GT + (k + 1))
                    dve.scalar_tensor_tensor(XB[:, :, 1, k * P:(k + 1) * P], psT[:, k % 2, 0:C].rearrange("p (k t) -> p k t", k=CK), XSC,
                                             XB[:, :, 0, k * P:(k + 1) * P], ALU.mult, ALU.subtract).then_inc(x_lo, 1)
                dve.wait_ge(lat_out, b * GT + GT)
                steps.one(dve.tensor_tensor(sq[:, :, :], lat[:, :, 0:QL + KL], lat[:, :, 0:QL + KL], ALU.mult))
                steps.done(dve.tensor_reduce(ss[:, 0:GT], sq[:, :, 0:QL], AX, ALU.add))
                steps.one(dve.tensor_reduce(ss[:, GT:2 * GT], sq[:, :, QL:QL + KL], AX, ALU.add))
                steps.one(dve.tensor_scalar(ss[:, 0:GT], ss[:, 0:GT], 1.0 / QL, RMS_EPS, ALU.mult, ALU.add))
                dve.tensor_scalar(ss[:, GT:2 * GT], ss[:, GT:2 * GT], 1.0 / KL, RMS_EPS, ALU.mult, ALU.add).then_inc(sums, 1)
                x1, x2 = lat[:, :, QL + KL:QL + KL + HALF], lat[:, :, QL + KL + HALF:QL + KL + ROPE]
                for q, (a, m) in enumerate(((x1, cos), (x2, sin), (x1, sin), (x2, cos))):
                    steps.done(dve.scalar_tensor_tensor(rt[:, q, :, :], a, QSC / H, m[:, :, :], ALU.mult, ALU.mult))
                steps.wait()
                dve.wait_ge(turned2, b * (2 * GT))
                steps.done(dve.tensor_tensor(nc_[:, :, QL + KL:QL + KL + HALF], rt[:, 0, :, :], rt[:, 1, :, :], ALU.subtract))
                steps.done(dve.tensor_tensor(nc_[:, :, QL + KL + HALF:QL + KL + ROPE], rt[:, 2, :, :], rt[:, 3, :, :], ALU.add))
                dve.wait_ge(rms, b + 1)
                steps.done(dve.tensor_tensor(nc_[:, :, 0:QL], lat[:, :, 0:QL], bcast(ss[:, 0:GT], QL), ALU.mult))
                steps.one(dve.tensor_tensor(nc_[:, :, QL:QL + KL], lat[:, :, QL:QL + KL], bcast(ss[:, GT:2 * GT], KL), ALU.mult))
                dve.tensor_copy(scores[:, bass.ds(b * GT, GT)], lat[:, :, QL + KL + ROPE]).then_inc(score_out, 1)
                for k in range(GT):
                    dve.wait_ge(n_hi, b * (2 * GT) + 2 * (k + 1))
                    dve.scalar_tensor_tensor(NB[:, 1, k * P:(k + 1) * P], psN[:, k % 2, 0:P], gain[:, 1:2],
                                             NB[:, 0, k * P:(k + 1) * P], ALU.mult, ALU.subtract).then_inc(n_lo, 1)
                    dve.tensor_tensor(RB[:, 1, k * P:(k + 1) * P], psN[0:ROPE, k % 2, P:2 * P],
                                      RB[:, 0, k * P:(k + 1) * P], ALU.subtract).then_inc(n_lo, 1)
                assert steps.n == STEPS, steps.n

        @block.scalar
        def _(act):
            act.wait_ge(gained, 1)
            with act.Fori(0, B) as b:
                def latent(k):
                    act.wait_ge(lat_mm, b * GT + (k + 1))
                    act.activation(lat[:, k, :], psL[:, k % 2, 0:LAT], ACT.Copy).then_inc(lat_out, 1)

                act.wait_ge(stored_x, b * 16)
                act.wait_ge(score_out, b)
                act.wait_ge(gate_mm, b)
                for k in range(GT):
                    act.wait_ge(turned, b * GT + (k + 1))
                    act.activation(XT[:, k % 2, :], psT[:, k % 2, 0:C], ACT.Copy).then_inc(xt_ready, 1)
                    act.activation(XB[:, :, 0, k * P:(k + 1) * P], psT[:, k % 2, 0:C].rearrange("p (k t) -> p k t", k=CK),
                                   ACT.Copy, scale=XSC).then_inc(x_hi, 1)
                    if k:
                        latent(k - 1)
                latent(GT - 1)
                act.wait_ge(gate_mm, b + 1)
                act.activation(gl[:, bass.ds(b, 1), :].rearrange("p a g -> p (a g)"), psG[:, 0:3], ACT.Copy).then_inc(gate_out, 1)
                act.wait_ge(stored_n, b * 32)
                for k in range(GT):
                    act.wait_ge(turned2, b * (2 * GT) + 2 * (k + 1))
                    act.activation(NB[:, 0, k * P:(k + 1) * P], psN[:, k % 2, 0:P], ACT.Identity, scale=gain[:, 1:2]).then_inc(n_hi, 1)
                    act.activation(RB[:, 0, k * P:(k + 1) * P], psN[0:ROPE, k % 2, P:2 * P], ACT.Copy).then_inc(n_hi, 1)

        @block.tensor
        def _(pe):
            pe.wait_ge(const_in, CONSTS)
            pe.wait_ge(set_, 2)
            with pe.Fori(0, B) as b:
                def turn(k):
                    pe.wait_ge(norm_ready, b * GT + (k + 1))
                    pe.wait_ge(x_lo, b * GT + (k - 1) if k > 1 else b * GT)
                    pe.wait_ge(lat_mm, b * GT + (k - 1) if k > 1 else b * GT)
                    for c in range(CK):
                        last = pe.transpose(psT[:, k % 2, c * P:(c + 1) * P], XS[:, k, c * P:(c + 1) * P], ident[:, :])
                    last.then_inc(turned, 1)

                def product(k):
                    pe.wait_ge(xt_ready, b * GT + (k + 1))
                    pe.wait_ge(lat_out, b * GT + (k - 1) if k > 1 else b * GT)
                    for c in range(CK):
                        last = pe.matmul(psL[:, k % 2, 0:LAT], XT[:, k % 2, c * P:(c + 1) * P], wlat[:, c, :],
                                         start=(c == 0), stop=(c == CK - 1))
                    last.then_inc(lat_mm, 1)

                turn(0)
                for k in range(GT):
                    if k + 1 < GT:
                        turn(k + 1)
                    product(k)
                pe.wait_ge(lat_out, b * GT + GT)
                pe.wait_ge(gate_out, b)
                for k in range(GT):
                    last = pe.matmul(psG[:, 0:3], mean_of[:, :], lat[:, k, LAT - 3:LAT], start=(k == 0), stop=(k == GT - 1))
                last.then_inc(gate_mm, 1)
                pe.wait_ge(step, b * STEPS + STEPS)
                for k in range(GT):
                    pe.wait_ge(n_lo, b * (2 * GT) + 2 * (k - 1) if k > 1 else b * (2 * GT))
                    pe.transpose(psN[:, k % 2, 0:P], nc_[:, k, 0:P], ident[:, :]).then_inc(turned2, 1)
                    pe.transpose(psN[0:ROPE, k % 2, P:2 * P], nc_[:, k, P:P + ROPE], ident[:, :]).then_inc(turned2, 1)


def select_tokens(nc, dram, consts, s):
    with ExitStack() as ctx:
        def sb(n, shape, dt=F32):
            return ctx.enter_context(nc.sbuf_tensor("t_" + n, shape, dt))

        def pb(n, shape, dt=F32):
            return ctx.enter_context(nc.psum_tensor("t_" + n, shape, dt))

        def sem(n):
            return nc.alloc_semaphore("t_" + n)

        ident, keep = sb("ident", [P, P]), sb("keep", [P, KEEP])
        score_n, score_t = sb("score_n", [P, NT]), sb("score_t", [NT, P])
        score, left, chosen, rank = (sb(n, [B, T]) for n in ("score", "left", "chosen", "rank"))
        ones = sb("ones", [B, T])
        best = sb("best", [B, 8])
        rank_t, rank_n = sb("rank_t", [NT, P]), sb("rank_n", [P, NT])
        XN = sb("XN", [P, 2, GT, C])
        hot = sb("hot", [P, 2, GT, KEEP])
        SB = sb("SB", [P, 2, CK, HL, KEEP], F16)
        gl, ge, gs = sb("gl", [P, B, 3]), sb("ge", [P, B, 3]), sb("gs", [P, 2, B])
        ps1, ps2, psS = pb("ps1", [P, 512]), pb("ps2", [P, 512]), pb("psS", [P, 2, 512])
        const_in, turned, copied, moved, topped, step = (sem(n) for n in
                                                         ("const_in", "turned", "copied", "moved", "topped", "step"))
        shifted, expd, gated, gates_out = sem("shifted"), sem("expd"), sem("gated"), sem("gates_out")
        x_in = [sem(f"x_in{i}") for i in range(2)]
        hot_ready, picked, s_hi, s_lo = sem("hot_ready"), sem("picked"), sem("s_hi"), sem("s_lo")
        stored = [sem(f"stored{i}") for i in range(2)]
        block = ctx.enter_context(nc.Block())

        @block.sync
        def _(sp):
            sp.dma_start(ident[:, :], consts["c_ident"]).then_inc(const_in, 16)
            sp.dma_start(keep[:, :], consts["c_keep"]).then_inc(const_in, 16)
            sp.dma_start(score_n[:, :], s["score_n"]).then_inc(const_in, 16)
            sp.dma_start(gl[:, :, :].rearrange("p b g -> p (b g)"), s["gl"]).then_inc(const_in, 16)
            sp.wait_ge(copied, 1)
            sp.dma_start(s["score_t"].rearrange("(i p) -> i p", p=P), score_t[:, :]).then_inc(moved, 16)
            sp.wait_ge(moved, 16)
            sp.dma_start(score[:, :], s["score_t"].rearrange("(b t) -> b t", t=T)).then_inc(moved, 16)
            sp.wait_ge(topped, 1)
            sp.dma_start(s["rank_t"].rearrange("(b t) -> b t", t=T), rank[:, :]).then_inc(moved, 16)
            sp.wait_ge(moved, 48)
            sp.dma_start(rank_t[:, :], s["rank_t"].rearrange("(i p) -> i p", p=P)).then_inc(moved, 16)
            sp.wait_ge(gated, 1)
            sp.dma_start(s["gates"].rearrange("b p g -> p b g"), ge[:, :, :]).then_inc(gates_out, 16)
            with sp.Fori(0, B // 2) as t:
                for e in range(2):
                    b = sp.snap(t * 2 + e)
                    sp.wait_ge(picked, t * 2)
                    sp.dma_start(XN[:, e, :, :], s["xn"].rearrange("(b i p) c -> b p i c", p=P, i=GT)[bass.ds(b, 1)].rearrange("b p i c -> p (b i) c")).then_inc(x_in[e], 16)
                for e in range(2):
                    sp.wait_ge(s_lo, t * 2 + (e + 1))
                    sp.dma_start(s["sel"][bass.ds(t * 2 + e, 1)].rearrange("b p n -> p (b n)"),
                                 SB[:, e, :, :, :].rearrange("p k l t -> p (k l t)")).then_inc(stored[e], 16)
            for e in range(2):
                sp.wait_ge(stored[e], 16 * (B // 2))
            sp.wait_ge(gates_out, 16)

        @block.vector
        def _(dve):
            steps = Steps(dve, step)
            steps.done(dve.memset(ones[:, :], 1.0))
            dve.wait_ge(const_in, 64)
            steps.one(dve.tensor_reduce(gs[:, 0, :], gl[:, :, :], AX, ALU.max))
            dve.tensor_tensor(gl[:, :, :], gl[:, :, :], bcast(gs[:, 0, :], 3), ALU.subtract).then_inc(shifted, 1)
            dve.wait_ge(expd, 1)
            steps.one(dve.tensor_reduce(gs[:, 1, :], ge[:, :, :], AX, ALU.add))
            steps.one(dve.reciprocal(gs[:, 0, :], gs[:, 1, :]))
            dve.tensor_tensor(ge[:, :, :], ge[:, :, :], bcast(gs[:, 0, :], 3), ALU.mult).then_inc(gated, 1)
            dve.wait_ge(moved, 32)
            for r in range(KEEP // 8):
                src = score if r == 0 else left
                steps.one(dve.max(best[:, :], src[:, :]))
                steps.one(dve.match_replace(left[:, :], best[:, :], src[:, :], -3.0e38))
            steps.one(dve.tensor_tensor(chosen[:, :], score[:, :], left[:, :], ALU.not_equal))
            steps.one(dve.tensor_tensor_scan(rank[:, :], ones[:, :], chosen[:, :], 0.0, ALU.mult, ALU.add))
            steps.one(dve.tensor_tensor(rank[:, :], rank[:, :], chosen[:, :], ALU.mult))
            dve.tensor_scalar(rank[:, :], rank[:, :], 1.0, None, ALU.subtract).then_inc(topped, 1)
            with dve.Fori(0, B // 2) as t:
                dve.wait_ge(copied, 2)
                for e in range(2):
                    dve.wait_ge(picked, t * 2)
                    dve.tensor_tensor(hot[:, e, :, :], bcast(rank_n[:, bass.ds((t * 2 + e) * GT, GT)], KEEP),
                                      keep[:, :].unsqueeze(1).broadcast_to([P, GT, KEEP]), ALU.is_equal).then_inc(hot_ready, 1)
                for e in range(2):
                    dve.wait_ge(s_hi, t * 2 + (e + 1))
                    dve.scalar_tensor_tensor(SB[:, e, :, 1, :], psS[:, e, 0:CK * KEEP].rearrange("p (k t) -> p k t", k=CK),
                                             XSC, SB[:, e, :, 0, :], ALU.mult, ALU.subtract).then_inc(s_lo, 1)

        @block.scalar
        def _(act):
            act.wait_ge(turned, 1)
            act.activation(score_t[:, :], ps1[0:NT, 0:P], ACT.Copy).then_inc(copied, 1)
            act.wait_ge(shifted, 1)
            act.activation(ge[:, :, :], gl[:, :, :], ACT.Exp).then_inc(expd, 1)
            act.wait_ge(turned, 2)
            act.activation(rank_n[:, :], ps2[:, 0:NT], ACT.Copy).then_inc(copied, 1)
            with act.Fori(0, B // 2) as t:
                for e in range(2):
                    act.wait_ge(stored[e], t * 16)
                    act.wait_ge(picked, t * 2 + (e + 1))
                    act.activation(SB[:, e, :, 0, :], psS[:, e, 0:CK * KEEP].rearrange("p (k t) -> p k t", k=CK),
                                   ACT.Copy, scale=XSC).then_inc(s_hi, 1)

        @block.tensor
        def _(pe):
            pe.wait_ge(const_in, 64)
            pe.transpose(ps1[0:NT, 0:P], score_n[:, :], ident[:, :]).then_inc(turned, 1)
            pe.wait_ge(moved, 64)
            pe.transpose(ps2[:, 0:NT], rank_t[:, :], ident[0:NT, 0:NT]).then_inc(turned, 1)
            with pe.Fori(0, B // 2) as t:
                for e in range(2):
                    pe.wait_ge(x_in[e], t * 16 + 16)
                    pe.wait_ge(hot_ready, t * 2 + (e + 1))
                    pe.wait_ge(s_lo, t * 2)
                    for c in range(CK):
                        for k in range(GT):
                            last = pe.matmul(psS[:, e, c * KEEP:(c + 1) * KEEP], XN[:, e, k, c * P:(c + 1) * P], hot[:, e, k, :],
                                             start=(k == 0), stop=(k == GT - 1))
                    last.then_inc(picked, 1)


LATENT_KEYS, WINDOW_KEYS, CHOSEN_KEYS = 0, 1, 2
GATE = (0, 2, 1)
BANK = 512
HB = T // BANK
PROJECT = ([("v", k, c) for k in range(2) for c in range(HB)] + [("chosen_v",)]
           + [("plain", n, c) for n in ("k", "w", "q") for c in range(HB)] + [("chosen_k",)]
           + [("turn", n, c, y) for n in ("q", "w") for c in range(HB) for y in range(2)])
NEAR = PROJECT.index(("chosen_k",))
SPLIT = ("plain", "chosen_k")
MAXIMA = ([(k, i, c) for i in range(GT) for k in (LATENT_KEYS, WINDOW_KEYS) for c in range((i * P) // BANK + 1)]
          + [(CHOSEN_KEYS, 0, 0)])
NM = len(MAXIMA)
MAX_SHARE = 0.8


def main_steps(j):
    steps = []
    for p in range(GT):
        first = (p * P) // BANK
        for k in (LATENT_KEYS, WINDOW_KEYS):
            for c in range(first, HB):
                w = (c + 1) * BANK - max(p * P, c * BANK)
                steps.append((("S", j, k, p, c), 3 * w))
        if p:
            for c in range(((p - 1) * P) // BANK, HB):
                w = (c + 1) * BANK - max((p - 1) * P, c * BANK)
                steps.append((("PV", j, p - 1, c), 5 * w))
    for c in range(HB):
        steps.append((("S", j, CHOSEN_KEYS, 0, c), 3 * BANK))
    steps.append((("PV", j, GT - 1, HB - 1), 5 * P))
    steps.append((("OUT", j), 0))
    return steps


def spread(fill, start, end):
    return [(start + (end - start) * (n + 0.5) / len(fill), f) for n, f in enumerate(fill)] if fill else []


def group_plan():
    plan = []
    for j in range(HG):
        fill = spread([("MAX", (j + 1) % HG, n) for n in range(NM)] + [("MAXROW", (j + 1) % HG)], 0.0, MAX_SHARE)
        if j:
            fill += spread([("G", "chosen_o", j - 1)], 0.08, 0.1)
        if j == 0:
            fill += [(0.1, ("INVERT", 0)), (0.2, ("INVERT", 1)), (0.3, ("INVERT", 2)), (0.31, ("MIX",))]
            fill += spread([("G",) + g for g in PROJECT[:NEAR]], 0.12, 1.0)
        elif j == 1:
            items = []
            for g in PROJECT[NEAR:]:
                items.append(("G",) + g)
                if g[0] == "turn" and g[3] == 1:
                    items.append(("ROPE", g[1], g[2]))
                if g[0] == "chosen_k":
                    items.append(("ROPE", "chosen", 0))
            fill += spread(items, 0.12, 1.0)
        fill.sort(key=lambda f: f[0])
        main = main_steps(j)
        total = sum(w for _, w in main)
        at = 0
        for step, w in main:
            plan.append(step)
            at += w
            while fill and fill[0][0] * total <= at:
                plan.append(fill.pop(0)[1])
        plan += [f for _, f in fill]
    plan.append(("G", "chosen_o", HG - 1))
    return plan


def first_plan():
    plan = []
    for g in PROJECT:
        plan.append(("G",) + g)
        if g[0] == "turn" and g[3] == 1:
            plan.append(("ROPE", g[1], g[2]))
        if g[0] == "chosen_k":
            plan.append(("ROPE", "chosen", 0))
    return plan + [("MAX", 0, n) for n in range(NM)] + [("MAXROW", 0)]


def general_jobs(plan):
    return [s for s in plan if s[0] in ("G", "MAXROW")]


def is_split(job):
    return job[0] == "G" and job[1] in SPLIT


rope_order = [(x[1], x[2]) for x in first_plan() if x[0] == "ROPE"]
rope_buf = {r: n % 2 for n, r in enumerate(rope_order)}


def job_index(plan):
    found = {}
    for n, x in enumerate(general_jobs(plan)):
        if x[:2] == ("G", "turn") and x[4] == 1:
            found[(x[2], x[3])] = n
        if x[:2] == ("G", "chosen_k"):
            found[("chosen", 0)] = n
    return found


first_turn, turn_job = job_index(first_plan()), job_index(group_plan())


def attention(nc, consts, s):
    with ExitStack() as ctx:
        def sb(n, shape, dt=F32):
            return ctx.enter_context(nc.sbuf_tensor("a_" + n, shape, dt))

        def pb(n, shape, dt=F32):
            return ctx.enter_context(nc.psum_tensor("a_" + n, shape, dt))

        def sem(n):
            return nc.alloc_semaphore("a_" + n)

        K99 = D + 3
        ident, mask = sb("ident", [P, P]), sb("mask", [P, 3, P], F16)
        cos, sin = sb("cos", [P, T]), sb("sin", [P, T])
        W = sb("W", [P, W_COLS], F16)
        XB, NB = sb("XB", [P, CK, HL, T], F16), sb("NB", [P, HL, T], F16)
        SB = sb("SB", [P, CK, HL, KEEP], F16)
        gates = sb("gates", [P, 3])
        Qs, Ws, Ks = sb("Qs", [P, 3, HL, T], F16), sb("Ws", [P, 3, HL, T], F16), sb("Ks", [P, HL, T], F16)
        Cs = sb("Cs", [P, 3, HL, KEEP], F16)
        Vs, CVs = sb("Vs", [P, 2, GT, P]), sb("CVs", [KEEP, P])
        raw = sb("raw", [P, 2, 2, BANK])
        turned_, pool_t = sb("turned_", [P, 2, BANK]), sb("pool_t", [P, 2, BANK])
        Q, K1, KW = (sb(n, [K99, HG, HL, T], F16) for n in ("Q", "K1", "KW"))
        KC = sb("KC", [K99, HG, HL, KEEP], F16)
        V, VC = sb("V", [P, 2, HG, GT, 2 * DV]), sb("VC", [P, HG, 2 * DV])
        maxima, more = sb("maxima", [P, 3 * GT]), sb("more", [P, 2, GT // 2])
        max_rows = sb("max_rows", [3 * GT, P], F16)
        prob = sb("prob", [P, 2, 2, T])
        prob_c = sb("prob_c", [P, T])
        o_raw, oc_raw = sb("o_raw", [P, T]), sb("oc_raw", [P, BANK])
        o_val, o_sum = sb("o_val", [P, 3, T]), sb("o_sum", [P, 3, T])
        mix, zero = sb("mix", [P, HL, T], F16), sb("zero", [P, 1])
        psS, psO = pb("psS", [P, 2, T]), pb("psO", [P, T])
        psM, psG = pb("psM", [P, BANK]), pb("psG", [P, BANK])

        const_in, ones_set, w_in, gates_in = sem("const_in"), sem("ones_set"), sem("w_in"), sem("gates_in")
        g_mm, g_act, g_dve = sem("g_mm"), sem("g_act"), sem("g_dve")
        r_step, r_pool, roped = sem("r_step"), sem("r_pool"), sem("roped")
        slot_in = [sem(f"slot_in{j}") for j in range(HG)]
        m_mm, m_red, m_ready, rows_in = (sem(n) for n in ("m_mm", "m_red", "m_ready", "rows_in"))
        s_mm, exp_done, pv_mm = sem("s_mm"), sem("exp_done"), sem("pv_mm")
        v_copied, o_out, o_moved = sem("v_copied"), sem("o_out"), sem("o_moved")
        oc_moved = sem("oc_moved")
        inverse, weighed, mix_hi, mix_done, mix_stored = (sem(n) for n in
                                                          ("inverse", "weighed", "mix_hi", "mix_done", "mix_stored"))
        p_step, set_, set_sums, inverted = sem("p_step"), sem("set"), sem("set_sums"), sem("inverted")
        CONSTS = 16 * (4 + 3)

        plan, first = group_plan(), first_plan()
        jobs, first_jobs = general_jobs(plan), general_jobs(first)
        NJ, FJ = len(jobs), len(first_jobs)
        ND, FD = sum(map(is_split, jobs)), sum(map(is_split, first_jobs))
        NR = sum(1 for x in plan if x[0] == "ROPE")
        units = [x for x in plan if x[0] == "S" and x[4] == HB - 1]
        unit_of = {x[1:4]: n for n, x in enumerate(units)}
        NU = len(units)
        NPV = HG * GT
        SLOT_DMAS = 3 + 3 + 3 + 2

        row_jobs = [n + 1 for n, x in enumerate(jobs) if x[0] == "MAXROW"]
        last_project = jobs.index(("G",) + PROJECT[-1]) + 1

        def chosen_o_job(j):
            return jobs.index(("G", "chosen_o", j)) + 1

        def weights(at, rows, *dims):
            n = int(np.prod(dims)) * P
            lo = 0 if rows != KL else QL
            ap = W[lo:lo + rows, at:at + n]
            names = " ".join("abc"[:len(dims)])
            return ap.rearrange(f"p ({names} m) -> p {names} m", **dict(zip("abc", dims)))

        w_win, w_sel = weights(W_WIN, P, HL, CK, 3), weights(W_SEL, P, HL, CK, 3)
        w_winv, w_selv = weights(W_WINV, P, HL, CK), weights(W_SELV, P, HL, CK)
        w_q, w_dk, w_dv = weights(W_Q, QL, HL, 3), weights(W_DK, KL, HL), weights(W_DV, KL, HL)

        block = ctx.enter_context(nc.Block())

        @block.sync
        def _(sp):
            sp.dma_start(ident[:, :], consts["c_ident"]).then_inc(const_in, 16)
            sp.dma_start(mask[:, :, :], consts["c_mask"].rearrange("p (a q) -> p a q", a=3)).then_inc(const_in, 16)
            sp.dma_start(cos[:, :], consts["c_cosT"]).then_inc(const_in, 16)
            sp.dma_start(sin[:, :], consts["c_sinT"]).then_inc(const_in, 16)
            for k, dst in enumerate((K1, KW, KC)):
                n = dst.shape[3]
                sp.dma_start(dst[D:K99, :, 0, :], consts["c_shift"][k][:, :, 0:n]).then_inc(const_in, 16)

            def load(m):
                g, b = sp.snap(m % G), sp.snap(m // G)
                sp.dma_start(W[:, 0:W_Q], s["wsplit"][bass.ds(g, 1), :, 0:W_Q].rearrange("g p n -> p (g n)")).then_inc(w_in, 16)
                sp.dma_start(W[0:QL, W_Q:W_DK], s["wsplit"][bass.ds(g, 1), 0:QL, W_Q:W_DK].rearrange("g p n -> p (g n)")).then_inc(w_in, 16)
                sp.dma_start(W[QL:P, W_DK:W_COLS], s["wsplit"][bass.ds(g, 1), QL:P, W_DK:W_COLS].rearrange("g p n -> p (g n)")).then_inc(w_in, 16)
                sp.dma_start(XB[:, :, :, :].rearrange("p k l t -> p (k l t)"), s["xt"][bass.ds(b, 1)].rearrange("b p n -> p (b n)")).then_inc(w_in, 16)
                sp.dma_start(NB[:, :, :].rearrange("p l t -> p (l t)"), s["lat"][bass.ds(b, 1)].rearrange("b p n -> p (b n)")).then_inc(w_in, 16)
                sp.dma_start(SB[:, :, :, :].rearrange("p k l t -> p (k l t)"), s["sel"][bass.ds(b, 1)].rearrange("b p n -> p (b n)")).then_inc(w_in, 16)

            def repack(j, b):
                rows = slice(j * NOPE, (j + 1) * NOPE)
                for stage, slot in ((Qs, Q), (Ws, KW), (Cs, KC)):
                    for y in range(3):
                        sp.dma_start(slot[y * NOPE:(y + 1) * NOPE, j, :, :], stage[rows, y, :, :]).then_inc(slot_in[j], 16)
                sp.dma_start(K1[0:NOPE, j, :, :], Ks[rows, :, :]).then_inc(slot_in[j], 16)
                sp.dma_start(K1[NOPE:D, j, :, :].rearrange("p l t -> p (l t)"),
                             s["kr"][bass.ds(b, 1)].rearrange("b p n -> p (b n)")).then_inc(slot_in[j], 16)

            def move_out(n, j):
                rows = slice(j * DV, (j + 1) * DV)
                sp.wait_ge(o_out, n * HG + (j + 1))
                for k in range(2):
                    sp.dma_start(o_val[rows, k, :], o_raw[64 * k:64 * k + DV, :]).then_inc(o_moved, 16)
                    sp.dma_start(o_sum[rows, k, :], o_raw[64 * k + DV:64 * k + 2 * DV, :]).then_inc(o_moved, 16)

            def move_chosen(job, j):
                rows = slice(j * DV, (j + 1) * DV)
                sp.wait_ge(g_act, job)
                for c in range(HB):
                    cols = slice(c * BANK, (c + 1) * BANK)
                    sp.dma_start(o_val[rows, 2, cols], oc_raw[64 * c:64 * c + DV, :]).then_inc(oc_moved, 16)
                    sp.dma_start(o_sum[rows, 2, cols], oc_raw[64 * c + DV:64 * c + 2 * DV, :]).then_inc(oc_moved, 16)

            def staged(m):
                split_all, roped_all = m * ND + ND, m * NR + NR
                if not isinstance(m, int):
                    split_all, roped_all = sp.snap(split_all), sp.snap(roped_all)
                sp.wait_ge(g_dve, split_all)
                sp.wait_ge(roped, roped_all)

            def store_mix(n):
                sp.wait_ge(mix_done, n * 2 + 2)
                row = s["mixed"][n] if isinstance(n, int) else s["mixed"][bass.ds(n, 1)].rearrange("n p c -> p (n c)")
                sp.dma_start(row, mix[:, :, :].rearrange("p l t -> p (l t)")).then_inc(mix_stored, 16)

            load(0)
            staged(0)
            for j in range(HG):
                repack(j, 0)
            load(1)
            with sp.Fori(0, B * G) as n:
                nxt = sp.snap((n + 1) % (B * G))
                after = sp.snap((n + 2) % (B * G))
                here, next_batch = sp.snap(n + 0), sp.snap(nxt // G)
                batch = sp.snap(((n + (B * G - 1)) % (B * G)) // G)
                sp.dma_start(gates[:, :], s["gates"][bass.ds(batch, 1)].rearrange("b p g -> p (b g)")).then_inc(gates_in, 16)
                store_mix(here)
                move_out(here, 0)
                move_chosen(here * NJ + (FJ + chosen_o_job(0)), 0)
                staged(here + 1)
                for j in range(HG):
                    scored = sp.snap(here * NU + (unit_of[(j, CHOSEN_KEYS, 0)] + 1))
                    chosen_out = sp.snap(here * NJ + (FJ + chosen_o_job(j)))
                    if j:
                        move_out(here, j)
                        move_chosen(chosen_out, j)
                    sp.wait_ge(s_mm, scored)
                    repack(j, next_batch)
                    if j == 0:
                        load(after)
            sp.dma_start(gates[:, :], s["gates"][B - 1]).then_inc(gates_in, 16)
            store_mix(B * G)
            sp.wait_ge(mix_stored, 16 * (B * G + 1))
            sp.wait_ge(w_in, 16 * 6 * (B * G + 2))
            for j in range(HG):
                sp.wait_ge(slot_in[j], 16 * SLOT_DMAS * (B * G + 1))
            sp.wait_ge(rows_in, 16 * 3 * (B * G * HG + 1))

        @block.gpsimd
        def _(pool):
            ones = Steps(pool, ones_set)
            ones.one(pool.memset(V[:, :, :, :, :].rearrange("p k j i d -> p (k j i) d")[:, :, DV:2 * DV], 1.0))
            ones.one(pool.memset(VC[0:KEEP, :, DV:2 * DV], 1.0))
            ones.one(pool.memset(VC[KEEP:P, :, :], 0.0))
            ones.one(pool.memset(prob_c[KEEP:P, :], 0.0))
            pool.wait_ge(const_in, CONSTS)
            pool.wait_ge(ones_set, 4)
            zeros = Steps(pool, set_)
            zeros.one(pool.memset(o_val[:, :, :], 0.0))
            zeros.one(pool.memset(zero[:, :], 0.0))

            def rope(count, name, c, r):
                n = KEEP if name == "chosen" else BANK
                job = first_turn[(name, c)] if r is None else turn_job[(name, c)]
                base = 0 if r is None else FJ
                pool.wait_ge(g_act, (0 if r is None else r * NJ) + (base + job + 1))
                pool.wait_ge(roped, count)
                buf = rope_buf[(name, c)]
                cs, sn = cos[:, c * BANK:c * BANK + n], sin[:, c * BANK:c * BANK + n]
                pool.tensor_tensor(pool_t[:, 0, 0:n], raw[:, buf, 0, 0:n], sn, ALU.mult).then_inc(p_step, 1)
                pool.tensor_tensor(pool_t[:, 1, 0:n], raw[:, buf, 1, 0:n], cs, ALU.mult).then_inc(p_step, 1)
                pool.wait_ge(p_step, count * 2 + 2)
                pool.tensor_tensor(pool_t[:, 0, 0:n], pool_t[:, 0, 0:n], pool_t[:, 1, 0:n], ALU.add).then_inc(r_pool, 1)

            def copy_values(j):
                cols = slice(j * DV, (j + 1) * DV)
                pool.tensor_tensor(VC[0:KEEP, j, 0:DV], CVs[:, cols], zero[0:KEEP, :].broadcast_to([KEEP, DV]), ALU.add).then_inc(v_copied, 1)
                pool.tensor_copy(V[:, :, j, :, 0:DV], Vs[:, :, :, cols]).then_inc(v_copied, 1)

            def mix_group(n):
                for k in range(3):
                    pool.wait_ge(inverse, n * 3 + (k + 1))
                    pool.tensor_tensor(o_val[:, k, :], o_val[:, k, :], o_sum[:, k, :], ALU.mult).then_inc(weighed, 1)
                pool.wait_ge(weighed, n * 5 + 3)
                pool.tensor_tensor(o_val[:, 0, :], o_val[:, 0, :], o_val[:, 1, :], ALU.add).then_inc(weighed, 1)
                pool.wait_ge(weighed, n * 5 + 4)
                pool.tensor_tensor(o_val[:, 0, :], o_val[:, 0, :], o_val[:, 2, :], ALU.add).then_inc(weighed, 1)
                pool.wait_ge(weighed, n * 5 + 5)
                pool.wait_ge(mix_stored, n * 16)
                pool.tensor_tensor(mix[:, 0, :], o_val[:, 0, :], zero[:, :].broadcast_to([P, T]), ALU.add).then_inc(mix_done, 1)
                pool.wait_ge(mix_done, n * 2 + 1)
                pool.tensor_tensor(mix[:, 1, :], o_val[:, 0, :], mix[:, 0, :], ALU.subtract).then_inc(mix_done, 1)

            r = 0
            for x in first:
                if x[0] == "ROPE":
                    rope(r, x[1], x[2], None)
                    r += 1
            for j in range(HG):
                copy_values(j)
            with pool.Fori(0, B * G) as n:
                r = 0
                for x in plan:
                    if x[0] == "ROPE":
                        rope(n * NR + (NR + r), x[1], x[2], n)
                        r += 1
                    if x[0] == "MIX":
                        mix_group(n)
                    if x == ("OUT", 1):
                        pool.wait_ge(g_act, n * NJ + (FJ + chosen_o_job(0)))
                        copy_values(0)
                for j in range(1, HG):
                    pool.wait_ge(pv_mm, n * NPV + (j + 1) * GT)
                    pool.wait_ge(g_act, n * NJ + (FJ + chosen_o_job(j)))
                    copy_values(j)
            mix_group(B * G)

        @block.vector
        def _(dve):
            dve.wait_ge(const_in, CONSTS)

            def split_job(job, index, m):
                dve.wait_ge(g_act, index)
                scale = QSC / (XSC * WSC)
                if job[1] == "plain":
                    stage = {"q": Qs[:, 0], "w": Ws[:, 0], "k": Ks[:, :, :]}[job[2]]
                    cols = slice(job[3] * BANK, (job[3] + 1) * BANK)
                    dve.scalar_tensor_tensor(stage[:, 1, cols], psG[:, :], scale, stage[:, 0, cols],
                                             ALU.mult, ALU.subtract).then_inc(g_dve, 1)
                else:
                    dve.scalar_tensor_tensor(Cs[:, 0, 1, :], psG[:, 0:KEEP], scale, Cs[:, 0, 0, :],
                                             ALU.mult, ALU.subtract).then_inc(g_dve, 1)

            def rope(count, name, c):
                n = KEEP if name == "chosen" else BANK
                stage = {"q": Qs, "w": Ws, "chosen": Cs}[name]
                cols = slice(c * BANK, c * BANK + n)
                buf = rope_buf[(name, c)]
                steps = Steps(dve, r_step, count * 6)
                steps.wait()
                steps.done(dve.tensor_tensor(turned_[:, 0, 0:n], raw[:, buf, 0, 0:n], cos[:, c * BANK:c * BANK + n], ALU.mult))
                steps.one(dve.tensor_tensor(turned_[:, 1, 0:n], raw[:, buf, 1, 0:n], sin[:, c * BANK:c * BANK + n], ALU.mult))
                steps.one(dve.tensor_tensor(turned_[:, 0, 0:n], turned_[:, 0, 0:n], turned_[:, 1, 0:n], ALU.subtract))
                steps.done(dve.tensor_copy(stage[:, 1, 0, cols], turned_[:, 0, 0:n]))
                dve.wait_ge(r_pool, count + 1)
                steps.one(dve.tensor_copy(stage[:, 2, 0, cols], pool_t[:, 0, 0:n]))
                steps.done(dve.tensor_tensor(stage[:, 1, 1, cols], turned_[:, 0, 0:n], stage[:, 1, 0, cols], ALU.subtract))
                dve.tensor_tensor(stage[:, 2, 1, cols], pool_t[:, 0, 0:n], stage[:, 2, 0, cols], ALU.subtract).then_inc(roped, 1)

            def maxima_piece(done, n):
                k, i, c = MAXIMA[n]
                dve.wait_ge(m_mm, done + 1)
                if k == CHOSEN_KEYS:
                    ins = dve.tensor_reduce(maxima[:, 2 * GT:3 * GT], psM[:, :].rearrange("p (i k) -> p i k", k=KEEP), AX, ALU.max)
                else:
                    w = min((i + 1) * P - c * BANK, BANK)
                    dst = maxima[:, k * GT + i:k * GT + i + 1] if c == 0 else more[:, k, i - GT // 2:i - GT // 2 + 1]
                    ins = dve.tensor_reduce(dst, psM[:, 0:w], AX, ALU.max)
                ins.then_inc(m_red, 1)

            def merge(done):
                dve.wait_ge(m_red, done)
                both = maxima[:, 0:2 * GT].rearrange("p (k i) -> p k i", k=2)[:, :, GT // 2:GT]
                dve.tensor_tensor(both, both, more[:, :, :], ALU.max).then_inc(m_ready, 1)

            def invert(n, k):
                if k == 0:
                    dve.wait_ge(o_moved, n * (64 * HG))
                    dve.wait_ge(oc_moved, n * (64 * HG))
                    dve.wait_ge(gates_in, n * 16 + 16)
                steps = Steps(dve, inverted, n * 3 + k)
                steps.one(dve.reciprocal(o_sum[:, k, :], o_sum[:, k, :]))
                dve.tensor_scalar(o_sum[:, k, :], o_sum[:, k, :], gates[:, GATE[k]:GATE[k] + 1], QSC, ALU.mult, ALU.mult).then_inc(inverse, 1)

            dve.memset(o_sum[:, :, :], 1.0).then_inc(set_sums, 1)
            dve.wait_ge(set_sums, 1)
            done, q = 0, 0
            r = 0
            for x in first:
                if x[0] in ("G", "MAXROW"):
                    q += 1
                if is_split(x):
                    split_job(x, q, 0)
                if x[0] == "ROPE":
                    dve.wait_ge(g_act, first_turn[(x[1], x[2])] + 1)
                    rope(r, x[1], x[2])
                    r += 1
                if x[0] == "MAX":
                    maxima_piece(done, x[2])
                    done += 1
                if x[0] == "MAXROW":
                    merge(done)
            with dve.Fori(0, B * G) as n:
                done, q, r, heads = 0, 0, 0, 0
                for x in plan:
                    if x[0] in ("G", "MAXROW"):
                        q += 1
                    if is_split(x):
                        split_job(x, n * NJ + (FJ + q), n)
                    if x[0] == "INVERT":
                        invert(n, x[1])
                    if x[0] == "ROPE":
                        dve.wait_ge(g_act, n * NJ + (FJ + turn_job[(x[1], x[2])] + 1))
                        rope(n * NR + (NR + r), x[1], x[2])
                        r += 1
                    if x[0] == "MAX":
                        if x[2] == 0:
                            dve.wait_ge(g_mm, n * NJ + (FJ + row_jobs[heads - 1] if heads else FJ))
                        maxima_piece(n * (HG * NM) + (NM + done), x[2])
                        done += 1
                    if x[0] == "MAXROW":
                        merge(n * (HG * NM) + (NM + done))
                        heads += 1
            for k in range(3):
                invert(B * G, k)

        @block.scalar
        def _(act):
            act.wait_ge(const_in, CONSTS)

            def copy_job(job, q, m, ropes, start):
                act.wait_ge(g_mm, q)
                scale = 1.0 / (XSC * WSC)
                kind = job[1]
                if kind == "v":
                    if not start:
                        act.wait_ge(v_copied, m * (2 * HG))
                    i = job[3] * (BANK // P)
                    act.activation(Vs[:, job[2], i:i + BANK // P, :], psG[:, :].rearrange("p (i d) -> p i d", d=P),
                                   ACT.Copy, scale=scale).then_inc(g_act, 1)
                elif kind == "chosen_v":
                    act.activation(CVs[:, :], psG[0:KEEP, 0:P], ACT.Copy, scale=scale).then_inc(g_act, 1)
                elif kind == "plain":
                    if not start:
                        for j in range(HG):
                            act.wait_ge(slot_in[j], m * (16 * SLOT_DMAS))
                    stage = {"q": Qs[:, 0], "w": Ws[:, 0], "k": Ks[:, :, :]}[job[2]]
                    act.activation(stage[:, 0, job[3] * BANK:(job[3] + 1) * BANK], psG[:, :], ACT.Copy,
                                   scale=QSC * scale).then_inc(g_act, 1)
                elif kind == "chosen_k":
                    act.wait_ge(roped, ropes("chosen", 0))
                    act.activation(raw[:, rope_buf[("chosen", 0)], :, 0:KEEP],
                                   psG[:, KEEP:3 * KEEP].rearrange("p (y t) -> p y t", y=2), ACT.Copy, scale=QSC * scale)
                    act.activation(Cs[:, 0, 0, :], psG[:, 0:KEEP], ACT.Copy, scale=QSC * scale).then_inc(g_act, 1)
                elif kind == "turn":
                    act.wait_ge(roped, ropes(job[2], job[3]))
                    act.activation(raw[:, rope_buf[(job[2], job[3])], job[4], :], psG[:, :], ACT.Copy,
                                   scale=QSC * scale).then_inc(g_act, 1)

            def chosen_out(q, moved):
                act.wait_ge(g_mm, q)
                act.wait_ge(oc_moved, moved)
                act.activation(oc_raw[:, :], psG[:, :], ACT.Copy).then_inc(g_act, 1)

            def max_row(q, j, heads):
                act.wait_ge(g_mm, q)
                act.wait_ge(rows_in, heads * 48)
                act.activation(max_rows[:, :], psG[0:3 * GT, 0:P], ACT.Copy, scale=-1.0 / SHIFT).then_inc(g_act, 1)
                act.wait_ge(g_act, q)
                for k in range(3):
                    act.dma_start(Q[D + k:D + k + 1, j, 0, :], max_rows[k * GT:(k + 1) * GT, :]).then_inc(rows_in, 16)

            q = 0
            for x in first:
                if x[0] == "G":
                    q += 1
                    copy_job(x, q, 0, lambda name, c: max(rope_order.index((name, c)) - 1, 0), True)
                if x[0] == "MAXROW":
                    q += 1
                    max_row(q, 0, 0)
            with act.Fori(0, B * G) as n:
                q = u = heads = 0
                for x in plan:
                    if x[0] == "G" and x[1] == "chosen_o":
                        q += 1
                        chosen_out(n * NJ + (FJ + q), n * (64 * HG) + 64 * x[2])
                    elif x[0] == "G":
                        q += 1
                        copy_job(x, n * NJ + (FJ + q), n + 1,
                                 lambda name, c: n * NR + (NR + max(rope_order.index((name, c)) - 1, 0)), False)
                    elif x[0] == "MAXROW":
                        q += 1
                        max_row(n * NJ + (FJ + q), x[1], n * HG + (heads + 1))
                        heads += 1
                    elif x[0] == "S" and x[4] == HB - 1:
                        _s, j, k, p, _c = x
                        act.wait_ge(s_mm, n * NU + (u + 1))
                        buf = u % 2
                        if k == CHOSEN_KEYS:
                            if j == 0:
                                act.wait_ge(g_mm, n * NJ + FJ)
                            else:
                                act.wait_ge(g_mm, n * NJ + (FJ + chosen_o_job(j - 1)))
                            act.activation(prob_c[0:KEEP, :], psS[0:KEEP, buf, :], ACT.Exp, scale=EXP_SCALE).then_inc(exp_done, 1)
                        else:
                            pair = j * GT + p
                            act.wait_ge(pv_mm, n * NPV + (pair - 1) if pair > 1 else n * NPV)
                            act.activation(prob[:, pair % 2, k, p * P:T], psS[:, buf, p * P:T], ACT.Exp,
                                           scale=EXP_SCALE).then_inc(exp_done, 1)
                        u += 1
                    elif x[0] == "OUT":
                        j = x[1]
                        act.wait_ge(pv_mm, n * NPV + (j + 1) * GT)
                        act.wait_ge(o_moved, n * (64 * HG) + 64 * j)
                        act.activation(o_raw[:, :], psO[:, :], ACT.Copy).then_inc(o_out, 1)

        @block.tensor
        def _(pe):
            pe.wait_ge(const_in, CONSTS)
            pe.wait_ge(ones_set, 4)

            def three(out, left, right):
                terms = [(l[a], r[b]) for l, r in zip(left, right) for a, b in PRODUCTS]
                for i, (l, r) in enumerate(terms):
                    last = pe.matmul(out, l, r, start=(i == 0), stop=(i == len(terms) - 1))
                return last

            def project(job):
                kind = job[1]
                if kind == "v":
                    for i in range(BANK // P):
                        t = job[3] * (BANK // P) + i
                        tile = slice(t * P, (t + 1) * P)
                        out = psG[:, i * P:(i + 1) * P]
                        if job[2] == LATENT_KEYS:
                            last = three(out, [[NB[QL:P, l, tile] for l in range(HL)]], [[w_dv[:, l, :] for l in range(HL)]])
                        else:
                            last = three(out, [[XB[:, c, l, tile] for l in range(HL)] for c in range(CK)],
                                         [[w_winv[:, l, c, :] for l in range(HL)] for c in range(CK)])
                elif kind == "chosen_v":
                    last = three(psG[0:KEEP, 0:P], [[SB[:, c, l, :] for l in range(HL)] for c in range(CK)],
                                 [[w_selv[:, l, c, :] for l in range(HL)] for c in range(CK)])
                elif kind == "chosen_k":
                    for y in range(3):
                        last = three(psG[:, y * KEEP:(y + 1) * KEEP],
                                     [[w_sel[:, l, c, y, :] for l in range(HL)] for c in range(CK)],
                                     [[SB[:, c, l, :] for l in range(HL)] for c in range(CK)])
                else:
                    name, c = job[2], job[3]
                    y = 0 if kind == "plain" else 1 + job[4]
                    cols = slice(c * BANK, (c + 1) * BANK)
                    if name == "q":
                        last = three(psG[:, :], [[w_q[:, l, y, :] for l in range(HL)]], [[NB[0:QL, l, cols] for l in range(HL)]])
                    elif name == "k":
                        last = three(psG[:, :], [[w_dk[:, l, :] for l in range(HL)]], [[NB[QL:P, l, cols] for l in range(HL)]])
                    else:
                        last = three(psG[:, :], [[w_win[:, l, k, y, :] for l in range(HL)] for k in range(CK)],
                                     [[XB[:, k, l, cols] for l in range(HL)] for k in range(CK)])
                last.then_inc(g_mm, 1)

            def bank_free(before, jobs_done, split_done):
                if before is not None and is_split(before):
                    pe.wait_ge(g_dve, split_done)
                else:
                    pe.wait_ge(g_act, jobs_done)

            def maxima_piece(j, n, reduced):
                k, i, c = MAXIMA[n]
                pe.wait_ge(m_red, reduced)
                if k == CHOSEN_KEYS:
                    for t in range(GT):
                        last = pe.matmul(psM[:, t * KEEP:(t + 1) * KEEP], Q[0:D, j, 0, t * P:(t + 1) * P], KC[0:D, j, 0, :],
                                         start=True, stop=True)
                else:
                    keys = (K1, KW)[k]
                    w = min((i + 1) * P - c * BANK, BANK)
                    diagonal = (i * P) // BANK == c
                    last = pe.matmul(psM[:, 0:w], Q[0:D, j, 0, i * P:(i + 1) * P], keys[0:D, j, 0, c * BANK:c * BANK + w],
                                     start=True, stop=not diagonal)
                    if diagonal:
                        last = pe.matmul(psM[:, w - P:w], mask[:, 0, :], mask[:, 2, :], start=False, stop=True)
                last.then_inc(m_mm, 1)

            def scores(j, k, p, c, u):
                keys = (K1, KW, KC)[k]
                rows = KEEP if k == CHOSEN_KEYS else P
                a = max(p * P, c * BANK)
                out = psS[0:rows, u % 2, a:(c + 1) * BANK]
                tile = slice(p * rows, (p + 1) * rows)
                cols = slice(a, (c + 1) * BANK)
                diagonal = k != CHOSEN_KEYS and a == p * P
                pe.matmul(out, keys[:, j, 0, tile], Q[:, j, 0, cols], start=True, stop=False)
                pe.matmul(out, keys[0:D, j, 0, tile], Q[0:D, j, 1, cols], start=False, stop=False)
                last = pe.matmul(out, keys[0:D, j, 1, tile], Q[0:D, j, 0, cols], start=False, stop=not diagonal)
                if diagonal:
                    last = pe.matmul(psS[:, u % 2, a:a + P], mask[:, 0, :], mask[:, 1, :], start=False, stop=True)
                return last

            def values(j, p, c):
                a = max(p * P, c * BANK)
                for k in range(2):
                    last = pe.matmul(psO[64 * k:64 * k + 64, a:(c + 1) * BANK], V[:, k, j, p, :],
                                     prob[:, (j * GT + p) % 2, k, a:(c + 1) * BANK], start=(p == 0),
                                     stop=(p * P + P >= (c + 1) * BANK))
                return last

            pe.wait_ge(w_in, 16 * 6)
            q = d = done = 0
            before = None
            for x in first:
                if x[0] == "G":
                    if q:
                        bank_free(before, q, d)
                    project(x)
                    q += 1
                    d += is_split(x)
                    before = x
                if x[0] == "MAX":
                    if x[2] == 0:
                        pe.wait_ge(slot_in[0], 16 * SLOT_DMAS)
                    maxima_piece(0, x[2], done)
                    done += 1
                if x[0] == "MAXROW":
                    bank_free(before, q, d)
                    pe.wait_ge(m_ready, 1)
                    pe.transpose(psG[0:3 * GT, 0:P], maxima[:, :], ident[:, :]).then_inc(g_mm, 1)
                    before = x
            with pe.Fori(0, B * G) as n:
                q = d = done = u = heads = 0
                for x in plan:
                    kind = x[0]
                    if kind == "G" and x[1] != "chosen_o":
                        if x[1:] == PROJECT[0]:
                            pe.wait_ge(w_in, n * (16 * 6) + 2 * 16 * 6)
                        bank_free(before, n * NJ + (FJ + q), n * ND + (FD + d))
                        project(x)
                        q += 1
                        d += is_split(x)
                        before = x
                    elif kind == "G":
                        j = x[2]
                        pe.wait_ge(exp_done, n * NU + unit_of[(j, CHOSEN_KEYS, 0)] + 1)
                        bank_free(before, n * NJ + (FJ + q), n * ND + (FD + d))
                        for c in range(HB):
                            last = pe.matmul(psG[64 * c:64 * c + 64, :], VC[:, j, :], prob_c[:, c * BANK:(c + 1) * BANK],
                                             start=True, stop=True)
                        last.then_inc(g_mm, 1)
                        q += 1
                        before = x
                    elif kind == "MAXROW":
                        bank_free(before, n * NJ + (FJ + q), n * ND + (FD + d))
                        pe.wait_ge(m_ready, n * HG + heads + 2)
                        pe.transpose(psG[0:3 * GT, 0:P], maxima[:, :], ident[:, :]).then_inc(g_mm, 1)
                        q += 1
                        heads += 1
                        before = x
                    elif kind == "MAX":
                        if x[2] == 0:
                            pe.wait_ge(slot_in[x[1]], n * (16 * SLOT_DMAS) + (16 * SLOT_DMAS) * (2 if x[1] == 0 else 1))
                        maxima_piece(x[1], x[2], n * (HG * NM) + (NM + done))
                        done += 1
                    elif kind == "S":
                        _s, j, k, p, c = x
                        if c == (p * P) // BANK:
                            if k == LATENT_KEYS and p == 0:
                                pe.wait_ge(rows_in, n * (48 * HG) + 48 * (j + 1))
                            pe.wait_ge(exp_done, n * NU + (u - 1) if u > 1 else n * NU)
                        last = scores(j, k, p, c, u)
                        if c == HB - 1:
                            last.then_inc(s_mm, 1)
                            u += 1
                    elif kind == "PV":
                        _p, j, p, c = x
                        if c == (p * P) // BANK:
                            if p == 0:
                                pe.wait_ge(o_out, n * HG + j)
                                pe.wait_ge(v_copied, n * (2 * HG) + 2 * (j + 1))
                            pe.wait_ge(exp_done, n * NU + unit_of[(j, WINDOW_KEYS, p)] + 1)
                        last = values(j, p, c)
                        if c == HB - 1:
                            last.then_inc(pv_mm, 1)


def project_out(nc, X, dram, s):
    with ExitStack() as ctx:
        def sb(n, shape, dt=F32):
            return ctx.enter_context(nc.sbuf_tensor("o_" + n, shape, dt))

        def sem(n):
            return nc.alloc_semaphore("o_" + n)

        wp, ws = sb("wp", [P, G, C]), sb("ws", [P, HL, G, C], F16)
        O = sb("O", [P, 2, G, HL, T], F16)
        ps = ctx.enter_context(nc.psum_tensor("o_ps", [P, 4, BANK], F32))
        loaded, x_in, hi, ready, summed, added = (sem(n) for n in ("loaded", "x_in", "hi", "ready", "summed", "added"))
        o_in = [sem(f"o_in{e}") for e in range(2)]
        block = ctx.enter_context(nc.Block())

        @block.sync
        def _(sp):
            sp.dma_start(wp[:, :, :], dram["w_proj"].rearrange("(g p) c -> p g c", p=P)).then_inc(loaded, 16)
            with sp.Fori(0, B // 2) as t:
                for e in range(2):
                    b = sp.snap(t * 2 + e)
                    sp.wait_ge(summed, t * (2 * GT))
                    sp.dma_start(O[:, e, :, :, :].rearrange("p g l t -> p g (l t)"),
                                 s["mixed"][1:B * G + 1].rearrange("(b g) p c -> b p g c", g=G)[bass.ds(b, 1)].rearrange("b p g c -> p (b g) c")).then_inc(o_in[e], 16)
            sp.wait_ge(added, NT)

        @block.gpsimd
        def _(pool):
            for b in range(B):
                pool.dma_start(X[:, b * GT:(b + 1) * GT, :],
                               s["x1"].rearrange("(i p) c -> p i c", p=P)[:, b * GT:(b + 1) * GT, :]).then_inc(x_in, 16)

        @block.scalar
        def _(act):
            act.wait_ge(loaded, 16)
            act.activation(ws[:, 0, :, :], wp[:, :, :], ACT.Copy, scale=WSC).then_inc(hi, 1)

        @block.vector
        def _(dve):
            dve.wait_ge(hi, 1)
            dve.scalar_tensor_tensor(ws[:, 1, :, :], wp[:, :, :], WSC, ws[:, 0, :, :], ALU.mult, ALU.subtract).then_inc(ready, 1)
            dve.wait_ge(x_in, 16 * B)
            with dve.Fori(0, B // 2) as t:
                for e in range(2):
                    for i in range(GT):
                        dve.wait_ge(summed, t * (2 * GT) + (e * GT + i + 1))
                        x = X[:, bass.ds((t * 2 + e) * GT + i, 1), :].rearrange("p a c -> p (a c)")
                        dve.scalar_tensor_tensor(x, ps[:, i % 4, 0:C], 1.0 / (QSC * WSC), x, ALU.mult, ALU.add).then_inc(added, 1)

        @block.tensor
        def _(pe):
            pe.wait_ge(ready, 1)
            with pe.Fori(0, B // 2) as t:
                for e in range(2):
                    pe.wait_ge(o_in[e], t * 16 + 16)
                    for i in range(GT):
                        m = e * GT + i - 3
                        pe.wait_ge(added, t * (2 * GT) + m if m > 0 else t * (2 * GT))
                        for g in range(G):
                            for a, b in PRODUCTS:
                                last = pe.matmul(ps[:, i % 4, 0:C], O[:, e, g, a, i * P:(i + 1) * P], ws[:, b, g, :],
                                                 start=(g == 0 and (a, b) == HIHI), stop=(g == G - 1 and (a, b) == LOHI))
                        last.then_inc(summed, 1)


def scratch():
    return [
        ("disp1", (SLOTS, C), F32), ("eout1", (SLOTS, C), F32), ("disp2", (SLOTS, C), F32), ("eout2", (SLOTS, C), F32),
        ("x1", (N, C), F32), ("xn", (N, C), F32), ("wsplit", (G, P, W_COLS), F16), ("xt", (B, P, CK * HL * T), F16),
        ("lat", (B, P, HL * T), F16), ("kr", (B, ROPE, HL * T), F16), ("sel", (B, P, CK * HL * KEEP), F16),
        ("score_n", (P, NT), F32), ("score_t", (N,), F32), ("rank_t", (N,), F32), ("gl", (P, B * 3), F32),
        ("gates", (B, P, 3), F32), ("mixed", (B * G + 1, P, HL * T), F16),
    ]


def macaron_block(nc, x, out, dram, consts):
    s = {name: nc.dram_tensor("s_" + name, shape, dt).ap() for name, shape, dt in scratch()}
    dram = {**dram, **s}
    with nc.cleanup_on_exit(), nc.sbuf_tensor("X", [P, NT, C], F32) as X:
        ffn(nc, "1", X, dram, consts, x, s["x1"])
        split_weights(nc, dram, s["wsplit"])
        latents(nc, X, dram, consts, s)
    with nc.cleanup_on_exit():
        select_tokens(nc, dram, consts, s)
        attention(nc, consts, s)
    with nc.cleanup_on_exit(), nc.sbuf_tensor("X2", [P, NT, C], F32) as X:
        project_out(nc, X, dram, s)
        ffn(nc, "2", X, dram, consts, None, out)


_INS = ["L0_attn_x", "L0_attn_w_cq", "L0_attn_g_qnorm", "L0_attn_w_dq_nope", "L0_attn_w_dq_rope", "L0_attn_w_ckv",
        "L0_attn_g_kvnorm", "L0_attn_w_dk_nope", "L0_attn_w_dv", "L0_attn_w_krope", "L0_attn_w_imp",
        "L0_attn_w_selk", "L0_attn_w_selv", "L0_attn_w_wink", "L0_attn_w_winv", "L0_attn_w_gate",
        "L0_attn_w_proj", "L0_ffn_Wr", "L0_ffn_W1", "L0_ffn_W2"]


def kernel(**inputs):
    import numpy as _np
    import concourse.bacc as _bacc
    from concourse import mybir as _mybir
    from concourse.bass_utils import run_bass_kernel_spmd as _run

    nc = _bacc.Bacc("TRN2", target_bir_lowering=False, num_devices=1)
    arrays, dram, consts = {}, {}, {}
    for name in _INS:
        a = _np.ascontiguousarray(inputs[name])
        arrays[f"in_{name}"] = a
        short = name.replace("L0_attn_", "").replace("L0_ffn_", "")
        dram[short] = nc.dram_tensor(f"in_{name}", a.shape, _mybir.dt.from_np(a.dtype), kind="ExternalInput").ap()
    for name, a in constants().items():
        arrays[name] = a
        consts[name] = nc.dram_tensor(name, a.shape, _mybir.dt.from_np(a.dtype), kind="ExternalInput").ap()
    out = nc.dram_tensor("out_0", (N, C), _mybir.dt.float32, kind="ExternalOutput").ap()
    x = dram["x"].rearrange("b t c -> (b t) c")
    macaron_block(nc, x, out, dram, consts)
    r = _run(nc, [arrays], core_ids=[0])
    return r.results[0]["out_0"].reshape(B, T, C)
```

```python
from contextlib import ExitStack

import numpy as np

import concourse.bass as bass
from concourse import mybir

F32 = mybir.dt.float32
F16 = mybir.dt.float16
I32 = mybir.dt.int32
ALU = mybir.AluOpType
ACT = mybir.ActivationFunctionType
AX = mybir.AxisListType.X

P = 128
B, T, C = 4, 1024, 256
N = B * T
NT = N // P
GT = T // P
CK = C // P
E, CAP, F = 8, 640, 1024
SLOTS = E * CAP
ST = CAP // P
FT = F // P
H, HG = 16, 4
G = H // HG
D, NOPE, ROPE, DV = 96, 32, 64, 32
HALF = ROPE // 2
QL, KL = 96, 32
KEEP = 64
LAT = QL + KL + ROPE + 1 + 3
LN_EPS, RMS_EPS = 1e-5, 1e-6
HL = 2

XSC, WSC, QSC = 16.0, 64.0, 16.0
FXSC = 4.0
SHIFT = 256.0
EXP_SCALE = 1.0 / (QSC * QSC * float(np.sqrt(D)))
HIHI, HILO, LOHI = (0, 0), (0, 1), (1, 0)
PRODUCTS = (HIHI, HILO, LOHI)

W_WIN, W_SEL = 0, HL * CK * 3 * P
W_WINV = 2 * HL * CK * 3 * P
W_SELV = W_WINV + HL * CK * P
W_Q = W_SELV + HL * CK * P
W_DK = W_Q + HL * 3 * P
W_DV = W_DK + HL * P
W_COLS = W_DV + HL * P


class Steps:

    def __init__(self, engine, sem, base=0):
        self.engine, self.sem, self.base, self.n = engine, sem, base, 0

    def done(self, ins):
        ins.then_inc(self.sem, 1)
        self.n += 1

    def wait(self):
        self.engine.wait_ge(self.sem, self.base + self.n)

    def one(self, ins):
        self.done(ins)
        self.wait()


def bcast(ap, n):
    return ap.unsqueeze(2).broadcast_to([ap.shape[0], ap.shape[1], n])


def constants():
    ident = np.eye(P, dtype=np.float32)
    upto = np.triu(np.ones((P, P), np.float32))
    inv = (1.0 / np.power(10000.0, np.arange(0, ROPE, 2) / ROPE)).astype(np.float32)
    angle = np.outer(np.arange(T, dtype=np.float32), inv)
    cos, sin = np.cos(angle), np.sin(angle)
    big = (32768.0 * ident).astype(np.float16)
    hide_s = np.where(np.arange(P)[:, None] > np.arange(P)[None, :], -65504.0, 0.0).astype(np.float16)
    return {
        "c_ident": ident,
        "c_upto": upto,
        "c_expert": np.tile(np.arange(E, dtype=np.float32), (P, NT)),
        "c_keep": np.tile(np.arange(KEEP, dtype=np.float32), (P, 1)),
        "c_cosT": np.tile(cos.T, (HG, 1)).astype(np.float32),
        "c_sinT": np.tile(sin.T, (HG, 1)).astype(np.float32),
        "c_cos": cos.astype(np.float32),
        "c_sin": sin.astype(np.float32),
        "c_shift": np.stack([np.stack([np.full((HG, T), SHIFT if r == k else 0.0, np.float16) for r in range(3)])
                             for k in range(3)]),
        "c_mask": np.concatenate([big, hide_s, hide_s.T], axis=1),
    }


def normalize_batch(dve, b, stats_done, steps, eps_added, rstd_done, x_tiles, stats, moments, rstd, out, ready):
    for k in range(GT):
        dve.bn_stats(stats[:, k, :], x_tiles(k)).then_inc(stats_done, 1)
    dve.wait_ge(stats_done, b * GT + GT)
    mean, diff, squares = moments[:, 0, :], moments[:, 1, :], moments[:, 2, :]
    steps.done(dve.tensor_tensor(mean, stats[:, :, 1], stats[:, :, 4], ALU.add))
    steps.done(dve.tensor_tensor(diff, stats[:, :, 1], stats[:, :, 4], ALU.subtract))
    steps.one(dve.tensor_tensor(squares, stats[:, :, 2], stats[:, :, 5], ALU.add))
    steps.done(dve.tensor_scalar(mean, mean, 0.5, None, ALU.mult))
    steps.done(dve.tensor_scalar(squares, squares, 1.0 / C, LN_EPS, ALU.mult, ALU.add))
    steps.one(dve.scalar_tensor_tensor(diff, diff, 0.25, diff, ALU.mult, ALU.mult))
    dve.tensor_tensor(rstd[:, :], squares, diff, ALU.add).then_inc(eps_added, 1)
    dve.wait_ge(rstd_done, b + 1)
    for k in range(GT):
        ready(k, dve.tensor_scalar(out[:, k, :], x_tiles(k), mean[:, k:k + 1], rstd[:, k:k + 1],
                                   ALU.subtract, ALU.mult))


NORM_STEPS = 6


def inverse_deviation(pool, b, eps_added, rstd_done, rstd, minus_half):
    pool.wait_ge(eps_added, b + 1)
    pool.tensor_tensor(rstd[:, :], rstd[:, :], minus_half[:, 0:GT], ALU.pow).then_inc(rstd_done, 1)


def ffn(nc, name, X, dram, consts, xin, xout, beside=None):
    disp, eout = dram["disp" + name], dram["eout" + name]
    with ExitStack() as ctx:
        def sb(n, shape, dt=F32):
            return ctx.enter_context(nc.sbuf_tensor(name + n, shape, dt))

        XN = sb("XN", [P, NT, C])
        w_kept = sb("w_kept", [P, NT])
        w_lost = sb("w_lost", [P, NT])
        take = sb("take", [P, NT], I32)
        put = sb("put", [P, NT], I32)
        route_tokens(nc, name, X, XN, w_kept, w_lost, take, put, disp, dram, consts, xin)
        run_experts(nc, name, disp, eout, dram, consts)
        combine(nc, name, X, XN, w_kept, w_lost, take, dram, xout, beside)


def route_tokens(nc, name, X, XN, w_kept, w_lost, take, put, disp, dram, consts, xin):
    with ExitStack() as ctx:
        def sb(n, shape, dt=F32):
            return ctx.enter_context(nc.sbuf_tensor(name + n, shape, dt))

        def pb(n, shape, dt=F32):
            return ctx.enter_context(nc.psum_tensor(name + n, shape, dt))

        def sem(n):
            return nc.alloc_semaphore(name + n)

        ident, upto, ones, expert = (sb(n, s) for n, s in (
            ("ident", [P, P]), ("upto", [P, P]), ("ones", [P, P]), ("expert", [P, NT, E])))
        minus_half = sb("minus_half", [P, GT])
        half_set = sem("half_set")
        wr = sb("wr", [P, CK, E])
        zeros = sb("zeros", [P, 10 * C])
        stats, moments, rstd = sb("stats", [P, GT, 6]), sb("moments", [P, 3, GT]), sb("rstd", [P, GT])
        XS = sb("XS", [P, GT, C])
        XT = sb("XT", [P, 2, C])
        logit = sb("logit", [P, NT, E])
        top, sume, idx, used, kept, slot, tmp = (sb(n, [P, NT]) for n in
                                                 ("top", "sume", "idx", "used", "kept", "slot", "tmp"))
        d8, e8, eq, cand, onehot, run, pos = (sb(n, [P, NT, E]) for n in
                                              ("d8", "e8", "eq", "cand", "onehot", "run", "pos"))
        psT, psL = pb("psT", [P, 2, 512]), pb("psL", [P, 2, 512])
        psC = pb("psC", [P, 2, NT, E])

        loaded, const_in, zeroed, zero_set, ones_set = (sem(n) for n in
                                              ("loaded", "const_in", "zeroed", "zero_set", "ones_set"))
        norm_ready, kept_copy, step = sem("norm_ready"), sem("kept_copy"), sem("step")
        stats_done, eps_added, rstd_done = (sem(n) for n in ("stats_done", "eps_added", "rstd_done"))
        turned, xt_ready, logits_mm, logits_out = (sem(n) for n in
                                                   ("turned", "xt_ready", "logits_mm", "logits_out"))
        shifted, expd, hot, counted, routed, sent = (sem(n) for n in
                                                     ("shifted", "expd", "hot", "counted", "routed", "sent"))
        block = ctx.enter_context(nc.Block())

        @block.sync
        def _(sp):
            if xin is not None:
                for b in range(B):
                    sp.dma_start(X[:, b * GT:(b + 1) * GT, :],
                                 xin.rearrange("(i p) c -> p i c", p=P)[:, b * GT:(b + 1) * GT, :]).then_inc(loaded, 16)
            sp.dma_start(ident[:, :], consts["c_ident"]).then_inc(const_in, 16)
            sp.dma_start(upto[:, :], consts["c_upto"]).then_inc(const_in, 16)
            sp.dma_start(expert[:, :, :], consts["c_expert"].rearrange("p (i e) -> p i e", e=E)).then_inc(const_in, 16)
            sp.dma_start(wr[:, :, :], dram["Wr"].rearrange("(k p) e -> p k e", p=P)).then_inc(const_in, 16)
            sp.wait_ge(zero_set, 1)
            for q in range(SLOTS // (10 * P)):
                sp.dma_start(disp.rearrange("(q p i) c -> q p (i c)", p=P, i=10)[q], zeros[:, :]).then_inc(zeroed, 16)

        @block.gpsimd
        def _(pool):
            pool.memset(zeros[:, :], 0.0).then_inc(zero_set, 1)
            pool.memset(ones[:, :], 1.0).then_inc(ones_set, 1)
            pool.memset(minus_half[:, :], -0.5).then_inc(half_set, 1)
            pool.wait_ge(half_set, 1)
            with pool.Fori(0, B) as b:
                inverse_deviation(pool, b, eps_added, rstd_done, rstd, minus_half)
                for k in range(GT):
                    pool.wait_ge(norm_ready, b * GT + (k + 1))
                    pool.wait_ge(norm_ready, 1)
                    pool.tensor_copy(XN[:, bass.ds(b * GT + k, 1), :].rearrange("p a c -> p (a c)"), XS[:, k, :]).then_inc(kept_copy, 1)
            pool.wait_ge(kept_copy, NT)
            pool.wait_ge(zeroed, 16 * (SLOTS // (10 * P)))
            pool.wait_ge(routed, 2)
            for i in range(NT):
                pool.indirect_dma_start(
                    out=disp, out_offset=bass.IndirectOffsetOnAxis(ap=put[:, i:i + 1], axis=0),
                    in_=XN[:, i, :], in_offset=None, bounds_check=SLOTS - 1, oob_is_err=False).then_inc(sent, 16)
            pool.wait_ge(sent, 16 * NT)

        @block.vector
        def _(dve):
            if xin is not None:
                dve.wait_ge(loaded, 16 * B)
            with dve.Fori(0, B) as b:
                dve.wait_ge(turned, b * GT)
                dve.wait_ge(kept_copy, b * GT)
                normalize_batch(dve, b, stats_done, Steps(dve, step, b * NORM_STEPS), eps_added, rstd_done, lambda k: X[:, bass.ds(b * GT + k, 1), :].rearrange("p a c -> p (a c)"),
                                stats, moments, rstd, XS, lambda k, ins: ins.then_inc(norm_ready, 1))
            steps = Steps(dve, step, B * NORM_STEPS)
            dve.wait_ge(logits_out, B)
            steps.one(dve.tensor_reduce(top[:, :], logit[:, :, :], AX, ALU.max))
            dve.tensor_tensor(d8[:, :, :], logit[:, :, :], bcast(top[:, :], E), ALU.subtract).then_inc(shifted, 1)
            dve.wait_ge(shifted, 1)
            steps.one(dve.tensor_scalar(eq[:, :, :], d8[:, :, :], 0.0, -float(E), ALU.is_ge, ALU.mult))
            dve.wait_ge(const_in, 64)
            steps.one(dve.scalar_tensor_tensor(cand[:, :, :], eq[:, :, :], float(E), expert[:, :, :], ALU.add, ALU.add))
            steps.one(dve.tensor_reduce(idx[:, :], cand[:, :, :], AX, ALU.min))
            dve.tensor_tensor(onehot[:, :, :], expert[:, :, :], bcast(idx[:, :], E), ALU.is_equal).then_inc(hot, 1)
            dve.wait_ge(expd, 1)
            steps.one(dve.tensor_reduce(sume[:, :], e8[:, :, :], AX, ALU.add))
            steps.one(dve.reciprocal(top[:, :], sume[:, :]))
            dve.wait_ge(counted, 1)
            for e in range(E):
                steps.done(dve.tensor_tensor_scan(run[:, :, e], ones[:, 0:NT], psC[:, 1, :, e], 0.0, ALU.mult, ALU.add))
            steps.wait()
            steps.one(dve.tensor_tensor(run[:, :, :], run[:, :, :], psC[:, 1, :, :], ALU.subtract))
            steps.one(dve.tensor_tensor(run[:, :, :], run[:, :, :], psC[:, 0, :, :], ALU.add))
            steps.one(dve.tensor_tensor(pos[:, :, :], run[:, :, :], onehot[:, :, :], ALU.mult))
            steps.one(dve.tensor_reduce(used[:, :], pos[:, :, :], AX, ALU.add))
            steps.one(dve.tensor_scalar(kept[:, :], used[:, :], float(CAP), None, ALU.is_le))
            steps.one(dve.scalar_tensor_tensor(w_kept[:, :], top[:, :], 0.5, kept[:, :], ALU.mult, ALU.mult))
            steps.one(dve.tensor_scalar(w_lost[:, :], kept[:, :], -0.5, 0.5, ALU.mult, ALU.add))
            steps.one(dve.tensor_scalar(tmp[:, :], used[:, :], float(CAP), -1.0, ALU.min, ALU.add))
            steps.one(dve.scalar_tensor_tensor(slot[:, :], idx[:, :], float(CAP), tmp[:, :], ALU.mult, ALU.add))
            dve.tensor_copy(take[:, :], slot[:, :]).then_inc(routed, 1)
            steps.one(dve.scalar_tensor_tensor(tmp[:, :], w_lost[:, :], float(4 * SLOTS), slot[:, :], ALU.mult, ALU.add))
            dve.tensor_copy(put[:, :], tmp[:, :]).then_inc(routed, 1)

        @block.scalar
        def _(act):
            with act.Fori(0, B) as b:
                for k in range(GT):
                    act.wait_ge(turned, b * GT + (k + 1))
                    act.activation(XT[:, k % 2, :], psT[:, k % 2, 0:C], ACT.Copy).then_inc(xt_ready, 1)
                act.wait_ge(logits_mm, b * GT + GT)
                act.activation(logit[:, bass.ds(b * GT, GT), :], psL[:, 0, 0:GT * E], ACT.Copy).then_inc(logits_out, 1)
            act.wait_ge(shifted, 1)
            act.activation(e8[:, :, :], d8[:, :, :], ACT.Exp).then_inc(expd, 1)

        @block.tensor
        def _(pe):
            pe.wait_ge(const_in, 64)

            def turn(b, k):
                pe.wait_ge(norm_ready, b * GT + (k + 1))
                if k >= 2:
                    pe.wait_ge(logits_mm, b * GT + (k - 1))
                for c in range(CK):
                    last = pe.transpose(psT[:, k % 2, c * P:(c + 1) * P], XS[:, k, c * P:(c + 1) * P], ident[:, :])
                last.then_inc(turned, 1)

            def router(b, k):
                pe.wait_ge(xt_ready, b * GT + (k + 1))
                if k == 0:
                    pe.wait_ge(logits_out, b)
                for c in range(CK):
                    last = pe.matmul(psL[:, 0, k * E:(k + 1) * E], XT[:, k % 2, c * P:(c + 1) * P], wr[:, c, :],
                                     start=(c == 0), stop=(c == CK - 1))
                last.then_inc(logits_mm, 1)

            with pe.Fori(0, B) as b:
                pe.wait_ge(logits_out, b)
                turn(b, 0)
                for k in range(GT):
                    if k + 1 < GT:
                        turn(b, k + 1)
                    router(b, k)
            pe.wait_ge(hot, 1)
            pe.wait_ge(ones_set, 1)
            flat = onehot[:, :, :].rearrange("p i e -> p (i e)")
            pe.matmul(psC[:, 0, :, :].rearrange("p i e -> p (i e)"), upto[:, :], flat, start=True, stop=True)
            pe.matmul(psC[:, 1, :, :].rearrange("p i e -> p (i e)"), ones[:, :], flat, start=True, stop=True).then_inc(counted, 1)


def run_experts(nc, name, disp, eout, dram, consts):
    PAIR = 2
    with ExitStack() as ctx:
        def sb(n, shape, dt=F32):
            return ctx.enter_context(nc.sbuf_tensor(name + n, shape, dt))

        def pb(n, shape, dt=F32):
            return ctx.enter_context(nc.psum_tensor(name + n, shape, dt))

        def sem(n):
            return nc.alloc_semaphore(name + n)

        ident = sb("ident2", [P, P])
        rows = sb("rows", [P, PAIR, ST, C])
        w1, w2 = sb("w1", [P, PAIR, CK, F]), sb("w2", [P, PAIR, FT, C])
        w1s, w2s = sb("w1s", [P, PAIR, HL, CK, F], F16), sb("w2s", [P, PAIR, HL, FT, C], F16)
        xT = sb("xT", [P, PAIR, HL, CK, CAP], F16)
        hT = sb("hT", [P, PAIR, HL, FT, CAP], F16)
        res = sb("res", [P, PAIR, ST, C])
        psT = pb("psTe", [P, 2, 512])
        psH = pb("psH", [P, 2, 2, 512])
        psO = pb("psO", [P, 2, 512])
        HC = CAP // 2

        ident_in = sem("ident_in")
        rows_in = [sem(f"rows_in{e}") for e in range(PAIR)]
        w_in = [sem(f"w_in{e}") for e in range(PAIR)]
        w_hi, w_lo = sem("w_hi"), sem("w_lo")
        turned, x_hi, x_lo = sem("turned2"), sem("x_hi"), sem("x_lo")
        hidden, h_hi, h_lo = sem("hidden"), sem("h_hi"), sem("h_lo")
        summed, res_ready = sem("summed"), sem("res_ready")
        stored = [sem(f"stored{e}") for e in range(PAIR)]
        blocks = [(c, s) for c in range(CK) for s in range(ST)]
        jobs = [blocks[j:j + 4] for j in range(0, len(blocks), 4)]
        NJ = len(jobs)
        NW, WP = FT, CK * F // (FT // 2)
        block = ctx.enter_context(nc.Block())

        def weight_piece(q, buf):
            raw, split = ((w1, w1s), (w2, w2s))[q // (NW // 2)]
            cols = slice(q % (NW // 2) * WP, (q % (NW // 2) + 1) * WP)
            return (raw[:, buf].rearrange("p k n -> p (k n)")[:, cols],
                    split[:, buf, 0].rearrange("p k n -> p (k n)")[:, cols],
                    split[:, buf, 1].rearrange("p k n -> p (k n)")[:, cols])

        def turn_piece(j, buf):
            cols = slice(j * 4 * P, j * 4 * P + len(jobs[j]) * P)
            return (xT[:, buf, 0].rearrange("p k s -> p (k s)")[:, cols],
                    xT[:, buf, 1].rearrange("p k s -> p (k s)")[:, cols])

        @block.sync
        def _(sp):
            def load(x, e, turned_before, split_before):
                if turned_before is not None:
                    sp.wait_ge(turned, turned_before)
                sp.dma_start(rows[:, e, :, :],
                             disp.rearrange("(x s p) c -> x p s c", s=ST, p=P)[bass.ds(x, 1)].rearrange("x p s c -> p (x s) c")).then_inc(rows_in[e], 16)
                if split_before is not None:
                    sp.wait_ge(w_lo, split_before)
                sp.dma_start(w1[:, e, :, :], dram["W1"].rearrange("x (k p) f -> x p k f", p=P)[bass.ds(x, 1)].rearrange("x p k f -> p (x k) f")).then_inc(w_in[e], 16)
                sp.dma_start(w2[:, e, :, :], dram["W2"].rearrange("x (k p) c -> x p k c", p=P)[bass.ds(x, 1)].rearrange("x p k c -> p (x k) c")).then_inc(w_in[e], 16)

            sp.dma_start(ident[:, :], consts["c_ident"]).then_inc(ident_in, 16)
            load(0, 0, None, None)
            with sp.Fori(0, E // PAIR) as t:
                second, third = sp.snap(t * PAIR + 1), sp.snap((t * PAIR + 2) % E)
                load(second, 1, t * (PAIR * NJ), t * (PAIR * NW))
                load(third, 0, t * (PAIR * NJ) + NJ, t * (PAIR * NW) + NW)
            sp.wait_ge(rows_in[0], 16 * (E // PAIR + 1))
            sp.wait_ge(w_in[0], 32 * (E // PAIR + 1))

        @block.gpsimd
        def _(pool):
            with pool.Fori(0, E // PAIR) as t:
                for e in range(PAIR):
                    pool.wait_ge(res_ready, t * (PAIR * ST) + ST * (e + 1))
                    pool.dma_start(eout.rearrange("(x s p) c -> x p s c", s=ST, p=P)[bass.ds(t * PAIR + e, 1)].rearrange("x p s c -> p (x s) c"), res[:, e, :, :]).then_inc(stored[e], 16)
            for e in range(PAIR):
                pool.wait_ge(stored[e], 16 * (E // PAIR))

        @block.scalar
        def _(act):
            def split(q, buf):
                src, hi, _lo = weight_piece(q, buf)
                act.activation(hi, src, ACT.Copy, scale=WSC).then_inc(w_hi, 1)

            def turned_out(j, buf, bank, count):
                act.wait_ge(turned, count)
                act.activation(turn_piece(j, buf)[0], psT[:, bank, 0:len(jobs[j]) * P], ACT.Copy, scale=FXSC).then_inc(x_hi, 1)

            act.wait_ge(w_in[0], 32)
            for q in range(NW):
                split(q, 0)
            for j in range(NJ):
                turned_out(j, 0, j % 2, j + 1)
            with act.Fori(0, E // PAIR) as t:
                for e in range(PAIR):
                    nxt = (e + 1) % PAIR
                    act.wait_ge(w_in[nxt], t * 32 + (32 if nxt else 64))
                    act.wait_ge(summed, t * (PAIR * ST) + e * ST if e else t * (PAIR * ST))
                    for f in range(FT):
                        split(f, nxt)
                        act.wait_ge(hidden, t * (PAIR * FT) + (e * FT + f + 1))
                        act.activation(hT[:, e, 0, f, :].rearrange("p (n s) -> p n s", n=2), psH[:, f % 2, :, 0:HC],
                                       ACT.Relu).then_inc(h_hi, 1)
                    for j in range(NJ):
                        n = (e + 1) * NJ + j
                        turned_out(j, nxt, n % 2, t * (PAIR * NJ) + (n + 1))
                    act.wait_ge(stored[e], t * 16)
                    for s in range(ST):
                        act.wait_ge(summed, t * (PAIR * ST) + (e * ST + s + 1))
                        act.activation(res[:, e, s, :], psO[:, (e * ST + s) % 2, 0:C], ACT.Copy,
                                       scale=1.0 / (FXSC * WSC * WSC)).then_inc(res_ready, 1)

        @block.vector
        def _(dve):
            def split(q, buf, count):
                dve.wait_ge(w_hi, count)
                src, hi, lo = weight_piece(q, buf)
                dve.scalar_tensor_tensor(lo, src, WSC, hi, ALU.mult, ALU.subtract).then_inc(w_lo, 1)

            def turned_out(j, buf, bank, count):
                dve.wait_ge(x_hi, count)
                hi, lo = turn_piece(j, buf)
                dve.scalar_tensor_tensor(lo, psT[:, bank, 0:len(jobs[j]) * P], FXSC, hi, ALU.mult, ALU.subtract).then_inc(x_lo, 1)

            for q in range(NW):
                split(q, 0, q + 1)
            for j in range(NJ):
                turned_out(j, 0, j % 2, j + 1)
            with dve.Fori(0, E // PAIR) as t:
                for e in range(PAIR):
                    nxt = (e + 1) % PAIR
                    for f in range(FT):
                        split(f, nxt, t * (PAIR * NW) + ((e + 1) * NW + f + 1))
                        dve.wait_ge(h_hi, t * (PAIR * FT) + (e * FT + f + 1))
                        dve.scalar_tensor_tensor(hT[:, e, 1, f, :].rearrange("p (n s) -> p n s", n=2), psH[:, f % 2, :, 0:HC], 0.0,
                                                 hT[:, e, 0, f, :].rearrange("p (n s) -> p n s", n=2), ALU.max, ALU.subtract).then_inc(h_lo, 1)
                    for j in range(NJ):
                        n = (e + 1) * NJ + j
                        turned_out(j, nxt, n % 2, t * (PAIR * NJ) + (n + 1))

        @block.tensor
        def _(pe):
            pe.wait_ge(ident_in, 16)

            def turn(j, buf, bank, freed):
                if freed is not None:
                    pe.wait_ge(x_lo, freed)
                for q, (c, s) in enumerate(jobs[j]):
                    last = pe.transpose(psT[:, bank, q * P:(q + 1) * P], rows[:, buf, s, c * P:(c + 1) * P], ident[:, :])
                last.then_inc(turned, 1)

            pe.wait_ge(rows_in[0], 16)
            for j in range(NJ):
                turn(j, 0, j % 2, j - 1 if j > 1 else None)
            with pe.Fori(0, E // PAIR) as t:
                for e in range(PAIR):
                    nxt = (e + 1) % PAIR
                    pe.wait_ge(x_lo, t * (PAIR * NJ) + NJ * (e + 1))
                    pe.wait_ge(w_lo, t * (PAIR * NW) + NW * (e + 1))
                    for f in range(FT):
                        m = e * FT + f - 1
                        pe.wait_ge(h_lo, t * (PAIR * FT) + m if m > 0 else t * (PAIR * FT))
                        for c in range(CK):
                            for a, b in PRODUCTS:
                                for n in range(2):
                                    last = pe.matmul(psH[:, f % 2, n, 0:HC], w1s[:, e, a, c, f * P:(f + 1) * P],
                                                     xT[:, e, b, c, n * HC:(n + 1) * HC],
                                                     start=(c == 0 and (a, b) == HIHI),
                                                     stop=(c == CK - 1 and (a, b) == LOHI))
                        last.then_inc(hidden, 1)
                    pe.wait_ge(rows_in[nxt], t * 16 + (16 if nxt else 32))
                    for j in range(NJ):
                        n = (e + 1) * NJ + j
                        turn(j, nxt, n % 2, t * (PAIR * NJ) + (n - 1))
                    pe.wait_ge(h_lo, t * (PAIR * FT) + FT * (e + 1))
                    for s in range(ST):
                        m = e * ST + s - 1
                        pe.wait_ge(res_ready, t * (PAIR * ST) + m if m > 0 else t * (PAIR * ST))
                        for f in range(FT):
                            for a, b in PRODUCTS:
                                last = pe.matmul(psO[:, (e * ST + s) % 2, 0:C], hT[:, e, a, f, s * P:(s + 1) * P],
                                                 w2s[:, e, b, f, :], start=(f == 0 and (a, b) == HIHI),
                                                 stop=(f == FT - 1 and (a, b) == LOHI))
                        last.then_inc(summed, 1)


def combine(nc, name, X, XN, w_kept, w_lost, take, dram, xout, beside):
    with ExitStack() as ctx:
        R = ctx.enter_context(nc.sbuf_tensor(name + "R", [P, NT, C], F32))
        eout = dram["eout" + name]
        LOT = 4
        got = [nc.alloc_semaphore(f"{name}got{i}") for i in range(NT // LOT)]
        mixed, ready, stored = (nc.alloc_semaphore(name + n) for n in ("mixed", "ready", "xstored"))
        block = ctx.enter_context(nc.Block())
        if beside is not None:
            beside(nc, ctx, block, dram)

        @block.gpsimd
        def _(pool):
            for i in range(NT):
                pool.indirect_dma_start(
                    out=R[:, i, :], out_offset=None, in_=eout,
                    in_offset=bass.IndirectOffsetOnAxis(ap=take[:, i:i + 1], axis=0),
                    bounds_check=SLOTS - 1, oob_is_err=False).then_inc(got[i // LOT], 16)

        @block.vector
        def _(dve):
            for i in range(NT):
                dve.scalar_tensor_tensor(X[:, i, :], XN[:, i, :], w_lost[:, i:i + 1], X[:, i, :], ALU.mult, ALU.add).then_inc(mixed, 1)
            for i in range(NT):
                if i % LOT == 0:
                    dve.wait_ge(got[i // LOT], 16 * LOT)
                dve.wait_ge(mixed, i + 1)
                dve.scalar_tensor_tensor(X[:, i, :], R[:, i, :], w_kept[:, i:i + 1], X[:, i, :], ALU.mult, ALU.add).then_inc(ready, 1)

        @block.sync
        def _(sp):
            for i in range(0, NT, LOT):
                sp.wait_ge(ready, i + LOT)
                sp.dma_start(xout.rearrange("(i p) c -> p i c", p=P)[:, i:i + LOT, :], X[:, i:i + LOT, :]).then_inc(stored, 16)
            sp.wait_ge(stored, 16 * (NT // LOT))


def split_weights(nc, ctx, block, dram):
    wsplit = dram["wsplit"]

    def sb(n, shape, dt=F32):
        return ctx.enter_context(nc.sbuf_tensor("ws_" + n, shape, dt))

    def sem(n):
        return nc.alloc_semaphore("ws_" + n)

    win, sel = sb("win", [P, CK, H * D]), sb("sel", [P, CK, H * D])
    winv, selv = sb("winv", [P, CK, H * DV]), sb("selv", [P, CK, H * DV])
    qn, qr = sb("qn", [QL, H * NOPE]), sb("qr", [QL, H * ROPE])
    dk, dv = sb("dk", [P, H * NOPE]), sb("dv", [P, H * DV])
    out = sb("out", [P, G, W_COLS], F16)
    loaded, hi_done, lo_done, stored = sem("loaded"), sem("hi_done"), sem("lo_done"), sem("stored")

    def pieces():
        for raw, at in ((win, W_WIN), (sel, W_SEL)):
            dst = out[:, :, at:at + HL * CK * 3 * P].rearrange(
                "p g (l k y h d) -> p g l k y h d", l=HL, k=CK, y=3, h=HG)
            src = raw[:, :, :].rearrange("p k (g h y d) -> p k g h y d", g=G, h=HG, y=3)
            for k in range(CK):
                for y in range(3):
                    yield src[:, k, :, :, y, :], dst[:, :, 0, k, y, :, :], dst[:, :, 1, k, y, :, :]
        for raw, at in ((winv, W_WINV), (selv, W_SELV)):
            dst = out[:, :, at:at + HL * CK * P].rearrange("p g (l k h d) -> p g l k h d", l=HL, k=CK, h=HG)
            src = raw[:, :, :].rearrange("p k (g h d) -> p k g h d", g=G, h=HG)
            for k in range(CK):
                yield src[:, k], dst[:, :, 0, k], dst[:, :, 1, k]
        dst = out[0:QL, :, W_Q:W_Q + HL * 3 * P].rearrange("p g (l y h d) -> p g l y h d", l=HL, y=3, h=HG)
        yield qn[:, :].rearrange("p (g h d) -> p g h d", g=G, h=HG), dst[:, :, 0, 0], dst[:, :, 1, 0]
        src = qr[:, :].rearrange("p (g h y d) -> p g h y d", g=G, h=HG, y=2)
        for y in range(2):
            yield src[:, :, :, y, :], dst[:, :, 0, 1 + y], dst[:, :, 1, 1 + y]
        for raw, at in ((dk, W_DK), (dv, W_DV)):
            dst = out[QL:P, :, at:at + HL * P].rearrange("p g (l h d) -> p g l h d", l=HL, h=HG)
            yield raw[QL:P, :].rearrange("p (g h d) -> p g h d", g=G, h=HG), dst[:, :, 0], dst[:, :, 1]

    @block.sync
    def _(sp):
        for dst, name in ((win, "w_wink"), (sel, "w_selk"), (winv, "w_winv"), (selv, "w_selv")):
            sp.dma_start(dst[:, :, :], dram[name].rearrange("(k p) n -> p k n", p=P)).then_inc(loaded, 16)
        sp.dma_start(qn[:, :], dram["w_dq_nope"]).then_inc(loaded, 16)
        sp.dma_start(qr[:, :], dram["w_dq_rope"]).then_inc(loaded, 16)
        sp.dma_start(dk[QL:P, :], dram["w_dk_nope"]).then_inc(loaded, 16)
        sp.dma_start(dv[QL:P, :], dram["w_dv"]).then_inc(loaded, 16)
        sp.wait_ge(lo_done, len(list(pieces())))
        for g in range(G):
            sp.dma_start(wsplit[g, :, 0:W_Q], out[:, g, 0:W_Q]).then_inc(stored, 16)
            sp.dma_start(wsplit[g, 0:QL, W_Q:W_DK], out[0:QL, g, W_Q:W_DK]).then_inc(stored, 16)
            sp.dma_start(wsplit[g, QL:P, W_DK:W_COLS], out[QL:P, g, W_DK:W_COLS]).then_inc(stored, 16)
        sp.wait_ge(stored, 3 * G * 16)

    @block.scalar
    def _(act):
        act.wait_ge(loaded, 8 * 16)
        for src, hi, _lo in pieces():
            act.activation(hi, src, ACT.Copy, scale=WSC).then_inc(hi_done, 1)

    @block.vector
    def _(dve):
        for n, (src, hi, lo) in enumerate(pieces()):
            dve.wait_ge(hi_done, n + 1)
            dve.scalar_tensor_tensor(lo, src, WSC, hi, ALU.mult, ALU.subtract).then_inc(lo_done, 1)


def latents(nc, X, dram, consts, s):
    with ExitStack() as ctx:
        def sb(n, shape, dt=F32):
            return ctx.enter_context(nc.sbuf_tensor("l_" + n, shape, dt))

        def pb(n, shape, dt=F32):
            return ctx.enter_context(nc.psum_tensor("l_" + n, shape, dt))

        def sem(n):
            return nc.alloc_semaphore("l_" + n)

        ident, mean_of = sb("ident", [P, P]), sb("mean_of", [P, P])
        minus_half = sb("minus_half", [P, 2 * GT])
        cos, sin = sb("cos", [P, GT, HALF]), sb("sin", [P, GT, HALF])
        gain = sb("gain", [P, 2])
        wlat = sb("wlat", [P, CK, LAT])
        stats, moments, rstd = sb("stats", [P, GT, 6]), sb("moments", [P, 3, GT]), sb("rstd", [P, GT])
        XS = sb("XS", [P, GT, C])
        XT = sb("XT", [P, 2, C])
        XB = sb("XB", [P, CK, HL, T], F16)
        lat = sb("lat", [P, GT, LAT])
        sq, ss = sb("sq", [P, GT, QL + KL]), sb("ss", [P, 2 * GT])
        nc_ = sb("normed", [P, GT, QL + KL + ROPE])
        rt = sb("rt", [P, 4, GT, HALF])
        NB, RB = sb("NB", [P, HL, T], F16), sb("RB", [ROPE, HL, T], F16)
        scores, gl = sb("scores", [P, NT]), sb("gl", [P, B, 3])
        psT, psL, psN, psG = pb("psT", [P, 2, 512]), pb("psL", [P, 2, 512]), pb("psN", [P, 2, 512]), pb("psG", [P, 512])

        const_in, set_, gained = sem("const_in"), sem("set"), sem("gained")
        stats_done, step, eps_added, rstd_done = sem("stats_done"), sem("step"), sem("eps_added"), sem("rstd_done")
        norm_ready, turned, xt_ready, x_hi, x_lo = (sem(n) for n in
                                                    ("norm_ready", "turned", "xt_ready", "x_hi", "x_lo"))
        lat_mm, lat_out, sums, rms, ready = (sem(n) for n in ("lat_mm", "lat_out", "sums", "rms", "ready"))
        turned2, n_hi, n_lo, gate_mm, gate_out = (sem(n) for n in
                                                  ("turned2", "n_hi", "n_lo", "gate_mm", "gate_out"))
        score_out, stored_x, stored_n, stored_s = sem("score_out"), sem("stored_x"), sem("stored_n"), sem("stored_s")
        STEPS = NORM_STEPS + 12
        CONSTS = 10 * 16
        block = ctx.enter_context(nc.Block())

        @block.sync
        def _(sp):
            sp.dma_start(ident[:, :], consts["c_ident"]).then_inc(const_in, 16)
            sp.dma_start(cos[:, :, :], consts["c_cos"].rearrange("(i p) d -> p i d", p=P)).then_inc(const_in, 16)
            sp.dma_start(sin[:, :, :], consts["c_sin"].rearrange("(i p) d -> p i d", p=P)).then_inc(const_in, 16)
            sp.dma_start(gain[0:QL, 0:1], dram["g_qnorm"].rearrange("(p a) -> p a", a=1)).then_inc(const_in, 16)
            sp.dma_start(gain[QL:P, 0:1], dram["g_kvnorm"].rearrange("(p a) -> p a", a=1)).then_inc(const_in, 16)
            at = 0
            for name, n in (("w_cq", QL), ("w_ckv", KL), ("w_krope", ROPE), ("w_imp", 1), ("w_gate", 3)):
                sp.dma_start(wlat[:, :, at:at + n], dram[name].rearrange("(k p) n -> p k n", p=P),
                             allow_slow_non_contiguous=(n == 1)).then_inc(const_in, 16)
                at += n
            with sp.Fori(0, B) as b:
                sp.wait_ge(norm_ready, b * GT + GT)
                sp.dma_start(s["xn"].rearrange("(b i p) c -> b p i c", p=P, i=GT)[bass.ds(b, 1)].rearrange("b p i c -> p (b i) c"), XS[:, :, :]).then_inc(stored_s, 16)
                sp.wait_ge(x_lo, b * GT + GT)
                sp.dma_start(s["xt"][bass.ds(b, 1)].rearrange("b p n -> p (b n)"),
                             XB[:, :, :, :].rearrange("p k l t -> p (k l t)")).then_inc(stored_x, 16)
                sp.wait_ge(n_lo, b * (2 * GT) + 2 * GT)
                sp.dma_start(s["kr"][bass.ds(b, 1)].rearrange("b p n -> p (b n)"),
                             RB[:, :, :].rearrange("p l t -> p (l t)")).then_inc(stored_n, 16)
                sp.dma_start(s["lat"][bass.ds(b, 1)].rearrange("b p n -> p (b n)"),
                             NB[:, :, :].rearrange("p l t -> p (l t)")).then_inc(stored_n, 16)
            sp.wait_ge(stored_x, 16 * B)
            sp.wait_ge(stored_n, 32 * B)
            sp.wait_ge(stored_s, 16 * B)
            sp.wait_ge(score_out, B)
            sp.wait_ge(gate_out, B)
            sp.dma_start(s["score_n"], scores[:, :]).then_inc(stored_x, 16)
            sp.dma_start(s["gl"], gl[:, :, :].rearrange("p b g -> p (b g)")).then_inc(stored_x, 16)
            sp.wait_ge(stored_x, 16 * B + 32)

        @block.gpsimd
        def _(pool):
            pool.memset(minus_half[:, :], -0.5).then_inc(set_, 1)
            pool.memset(mean_of[:, :], 1.0 / T).then_inc(set_, 1)
            pool.wait_ge(const_in, CONSTS)
            pool.tensor_scalar(gain[:, 1:2], gain[:, 0:1], XSC, None, ALU.mult).then_inc(gained, 1)
            pool.wait_ge(set_, 2)
            with pool.Fori(0, B) as b:
                inverse_deviation(pool, b, eps_added, rstd_done, rstd, minus_half)
                pool.wait_ge(sums, b + 1)
                pool.tensor_tensor(ss[:, :], ss[:, :], minus_half[:, :], ALU.pow).then_inc(rms, 1)

        @block.vector
        def _(dve):
            dve.wait_ge(const_in, CONSTS)
            dve.wait_ge(gained, 1)
            with dve.Fori(0, B) as b:
                steps = Steps(dve, step, b * STEPS)
                dve.wait_ge(turned, b * GT)
                dve.wait_ge(stored_s, b * 16)
                normalize_batch(dve, b, stats_done, steps, eps_added, rstd_done,
                                lambda k: X[:, bass.ds(b * GT + k, 1), :].rearrange("p a c -> p (a c)"),
                                stats, moments, rstd, XS, lambda k, ins: ins.then_inc(norm_ready, 1))
                for k in range(GT):
                    dve.wait_ge(x_hi, b * GT + (k + 1))
                    dve.scalar_tensor_tensor(XB[:, :, 1, k * P:(k + 1) * P], psT[:, k % 2, 0:C].rearrange("p (k t) -> p k t", k=CK), XSC,
                                             XB[:, :, 0, k * P:(k + 1) * P], ALU.mult, ALU.subtract).then_inc(x_lo, 1)
                dve.wait_ge(lat_out, b * GT + GT)
                steps.one(dve.tensor_tensor(sq[:, :, :], lat[:, :, 0:QL + KL], lat[:, :, 0:QL + KL], ALU.mult))
                steps.done(dve.tensor_reduce(ss[:, 0:GT], sq[:, :, 0:QL], AX, ALU.add))
                steps.one(dve.tensor_reduce(ss[:, GT:2 * GT], sq[:, :, QL:QL + KL], AX, ALU.add))
                steps.one(dve.tensor_scalar(ss[:, 0:GT], ss[:, 0:GT], 1.0 / QL, RMS_EPS, ALU.mult, ALU.add))
                dve.tensor_scalar(ss[:, GT:2 * GT], ss[:, GT:2 * GT], 1.0 / KL, RMS_EPS, ALU.mult, ALU.add).then_inc(sums, 1)
                x1, x2 = lat[:, :, QL + KL:QL + KL + HALF], lat[:, :, QL + KL + HALF:QL + KL + ROPE]
                for q, (a, m) in enumerate(((x1, cos), (x2, sin), (x1, sin), (x2, cos))):
                    steps.done(dve.scalar_tensor_tensor(rt[:, q, :, :], a, QSC / H, m[:, :, :], ALU.mult, ALU.mult))
                steps.wait()
                dve.wait_ge(turned2, b * (2 * GT))
                steps.done(dve.tensor_tensor(nc_[:, :, QL + KL:QL + KL + HALF], rt[:, 0, :, :], rt[:, 1, :, :], ALU.subtract))
                steps.done(dve.tensor_tensor(nc_[:, :, QL + KL + HALF:QL + KL + ROPE], rt[:, 2, :, :], rt[:, 3, :, :], ALU.add))
                dve.wait_ge(rms, b + 1)
                steps.done(dve.tensor_tensor(nc_[:, :, 0:QL], lat[:, :, 0:QL], bcast(ss[:, 0:GT], QL), ALU.mult))
                steps.one(dve.tensor_tensor(nc_[:, :, QL:QL + KL], lat[:, :, QL:QL + KL], bcast(ss[:, GT:2 * GT], KL), ALU.mult))
                dve.tensor_copy(scores[:, bass.ds(b * GT, GT)], lat[:, :, QL + KL + ROPE]).then_inc(score_out, 1)
                for k in range(GT):
                    dve.wait_ge(n_hi, b * (2 * GT) + 2 * (k + 1))
                    dve.scalar_tensor_tensor(NB[:, 1, k * P:(k + 1) * P], psN[:, k % 2, 0:P], gain[:, 1:2],
                                             NB[:, 0, k * P:(k + 1) * P], ALU.mult, ALU.subtract).then_inc(n_lo, 1)
                    dve.tensor_tensor(RB[:, 1, k * P:(k + 1) * P], psN[0:ROPE, k % 2, P:2 * P],
                                      RB[:, 0, k * P:(k + 1) * P], ALU.subtract).then_inc(n_lo, 1)
                assert steps.n == STEPS, steps.n

        @block.scalar
        def _(act):
            act.wait_ge(gained, 1)
            with act.Fori(0, B) as b:
                def latent(k):
                    act.wait_ge(lat_mm, b * GT + (k + 1))
                    act.activation(lat[:, k, :], psL[:, k % 2, 0:LAT], ACT.Copy).then_inc(lat_out, 1)

                act.wait_ge(stored_x, b * 16)
                act.wait_ge(score_out, b)
                act.wait_ge(gate_mm, b)
                for k in range(GT):
                    act.wait_ge(turned, b * GT + (k + 1))
                    act.activation(XT[:, k % 2, :], psT[:, k % 2, 0:C], ACT.Copy).then_inc(xt_ready, 1)
                    act.activation(XB[:, :, 0, k * P:(k + 1) * P], psT[:, k % 2, 0:C].rearrange("p (k t) -> p k t", k=CK),
                                   ACT.Copy, scale=XSC).then_inc(x_hi, 1)
                    if k:
                        latent(k - 1)
                latent(GT - 1)
                act.wait_ge(gate_mm, b + 1)
                act.activation(gl[:, bass.ds(b, 1), :].rearrange("p a g -> p (a g)"), psG[:, 0:3], ACT.Copy).then_inc(gate_out, 1)
                act.wait_ge(stored_n, b * 32)
                for k in range(GT):
                    act.wait_ge(turned2, b * (2 * GT) + 2 * (k + 1))
                    act.activation(NB[:, 0, k * P:(k + 1) * P], psN[:, k % 2, 0:P], ACT.Identity, scale=gain[:, 1:2]).then_inc(n_hi, 1)
                    act.activation(RB[:, 0, k * P:(k + 1) * P], psN[0:ROPE, k % 2, P:2 * P], ACT.Copy).then_inc(n_hi, 1)

        @block.tensor
        def _(pe):
            pe.wait_ge(const_in, CONSTS)
            pe.wait_ge(set_, 2)
            with pe.Fori(0, B) as b:
                def turn(k):
                    pe.wait_ge(norm_ready, b * GT + (k + 1))
                    pe.wait_ge(x_lo, b * GT + (k - 1) if k > 1 else b * GT)
                    pe.wait_ge(lat_mm, b * GT + (k - 1) if k > 1 else b * GT)
                    for c in range(CK):
                        last = pe.transpose(psT[:, k % 2, c * P:(c + 1) * P], XS[:, k, c * P:(c + 1) * P], ident[:, :])
                    last.then_inc(turned, 1)

                def product(k):
                    pe.wait_ge(xt_ready, b * GT + (k + 1))
                    pe.wait_ge(lat_out, b * GT + (k - 1) if k > 1 else b * GT)
                    for c in range(CK):
                        last = pe.matmul(psL[:, k % 2, 0:LAT], XT[:, k % 2, c * P:(c + 1) * P], wlat[:, c, :],
                                         start=(c == 0), stop=(c == CK - 1))
                    last.then_inc(lat_mm, 1)

                turn(0)
                for k in range(GT):
                    if k + 1 < GT:
                        turn(k + 1)
                    product(k)
                pe.wait_ge(lat_out, b * GT + GT)
                pe.wait_ge(gate_out, b)
                for k in range(GT):
                    last = pe.matmul(psG[:, 0:3], mean_of[:, :], lat[:, k, LAT - 3:LAT], start=(k == 0), stop=(k == GT - 1))
                last.then_inc(gate_mm, 1)
                pe.wait_ge(step, b * STEPS + STEPS)
                for k in range(GT):
                    pe.wait_ge(n_lo, b * (2 * GT) + 2 * (k - 1) if k > 1 else b * (2 * GT))
                    pe.transpose(psN[:, k % 2, 0:P], nc_[:, k, 0:P], ident[:, :]).then_inc(turned2, 1)
                    pe.transpose(psN[0:ROPE, k % 2, P:2 * P], nc_[:, k, P:P + ROPE], ident[:, :]).then_inc(turned2, 1)


def select_tokens(nc, dram, consts, s):
    with ExitStack() as ctx:
        def sb(n, shape, dt=F32):
            return ctx.enter_context(nc.sbuf_tensor("t_" + n, shape, dt))

        def pb(n, shape, dt=F32):
            return ctx.enter_context(nc.psum_tensor("t_" + n, shape, dt))

        def sem(n):
            return nc.alloc_semaphore("t_" + n)

        ident, keep = sb("ident", [P, P]), sb("keep", [P, KEEP])
        score_n, score_t = sb("score_n", [P, NT]), sb("score_t", [NT, P])
        score, left, chosen, rank = (sb(n, [B, T]) for n in ("score", "left", "chosen", "rank"))
        ones = sb("ones", [B, T])
        best = sb("best", [B, 8])
        rank_t, rank_n = sb("rank_t", [NT, P]), sb("rank_n", [P, NT])
        XN = sb("XN", [P, 2, GT, C])
        hot = sb("hot", [P, 2, GT, KEEP])
        SB = sb("SB", [P, 2, CK, HL, KEEP], F16)
        gl, ge, gs = sb("gl", [P, B, 3]), sb("ge", [P, B, 3]), sb("gs", [P, 2, B])
        ps1, ps2, psS = pb("ps1", [P, 512]), pb("ps2", [P, 512]), pb("psS", [P, 2, 512])
        const_in, turned, copied, moved, topped, step = (sem(n) for n in
                                                         ("const_in", "turned", "copied", "moved", "topped", "step"))
        shifted, expd, gated, gates_out = sem("shifted"), sem("expd"), sem("gated"), sem("gates_out")
        x_in = [sem(f"x_in{i}") for i in range(2)]
        hot_ready, picked, s_hi, s_lo = sem("hot_ready"), sem("picked"), sem("s_hi"), sem("s_lo")
        stored = [sem(f"stored{i}") for i in range(2)]
        block = ctx.enter_context(nc.Block())

        @block.sync
        def _(sp):
            sp.dma_start(ident[:, :], consts["c_ident"]).then_inc(const_in, 16)
            sp.dma_start(keep[:, :], consts["c_keep"]).then_inc(const_in, 16)
            sp.dma_start(score_n[:, :], s["score_n"]).then_inc(const_in, 16)
            sp.dma_start(gl[:, :, :].rearrange("p b g -> p (b g)"), s["gl"]).then_inc(const_in, 16)
            sp.wait_ge(copied, 1)
            sp.dma_start(s["score_t"].rearrange("(i p) -> i p", p=P), score_t[:, :]).then_inc(moved, 16)
            sp.wait_ge(moved, 16)
            sp.dma_start(score[:, :], s["score_t"].rearrange("(b t) -> b t", t=T)).then_inc(moved, 16)
            sp.wait_ge(topped, 1)
            sp.dma_start(s["rank_t"].rearrange("(b t) -> b t", t=T), rank[:, :]).then_inc(moved, 16)
            sp.wait_ge(moved, 48)
            sp.dma_start(rank_t[:, :], s["rank_t"].rearrange("(i p) -> i p", p=P)).then_inc(moved, 16)
            sp.wait_ge(gated, 1)
            sp.dma_start(s["gates"].rearrange("b p g -> p b g"), ge[:, :, :]).then_inc(gates_out, 16)
            with sp.Fori(0, B // 2) as t:
                for e in range(2):
                    b = sp.snap(t * 2 + e)
                    sp.wait_ge(picked, t * 2)
                    sp.dma_start(XN[:, e, :, :], s["xn"].rearrange("(b i p) c -> b p i c", p=P, i=GT)[bass.ds(b, 1)].rearrange("b p i c -> p (b i) c")).then_inc(x_in[e], 16)
                for e in range(2):
                    sp.wait_ge(s_lo, t * 2 + (e + 1))
                    sp.dma_start(s["sel"][bass.ds(t * 2 + e, 1)].rearrange("b p n -> p (b n)"),
                                 SB[:, e, :, :, :].rearrange("p k l t -> p (k l t)")).then_inc(stored[e], 16)
            for e in range(2):
                sp.wait_ge(stored[e], 16 * (B // 2))
            sp.wait_ge(gates_out, 16)

        @block.vector
        def _(dve):
            steps = Steps(dve, step)
            steps.done(dve.memset(ones[:, :], 1.0))
            dve.wait_ge(const_in, 64)
            steps.one(dve.tensor_reduce(gs[:, 0, :], gl[:, :, :], AX, ALU.max))
            dve.tensor_tensor(gl[:, :, :], gl[:, :, :], bcast(gs[:, 0, :], 3), ALU.subtract).then_inc(shifted, 1)
            dve.wait_ge(expd, 1)
            steps.one(dve.tensor_reduce(gs[:, 1, :], ge[:, :, :], AX, ALU.add))
            steps.one(dve.reciprocal(gs[:, 0, :], gs[:, 1, :]))
            dve.tensor_tensor(ge[:, :, :], ge[:, :, :], bcast(gs[:, 0, :], 3), ALU.mult).then_inc(gated, 1)
            dve.wait_ge(moved, 32)
            for r in range(KEEP // 8):
                src = score if r == 0 else left
                steps.one(dve.max(best[:, :], src[:, :]))
                steps.one(dve.match_replace(left[:, :], best[:, :], src[:, :], -3.0e38))
            steps.one(dve.tensor_tensor(chosen[:, :], score[:, :], left[:, :], ALU.not_equal))
            steps.one(dve.tensor_tensor_scan(rank[:, :], ones[:, :], chosen[:, :], 0.0, ALU.mult, ALU.add))
            steps.one(dve.tensor_tensor(rank[:, :], rank[:, :], chosen[:, :], ALU.mult))
            dve.tensor_scalar(rank[:, :], rank[:, :], 1.0, None, ALU.subtract).then_inc(topped, 1)
            with dve.Fori(0, B // 2) as t:
                dve.wait_ge(copied, 2)
                for e in range(2):
                    dve.wait_ge(picked, t * 2)
                    dve.tensor_tensor(hot[:, e, :, :], bcast(rank_n[:, bass.ds((t * 2 + e) * GT, GT)], KEEP),
                                      keep[:, :].unsqueeze(1).broadcast_to([P, GT, KEEP]), ALU.is_equal).then_inc(hot_ready, 1)
                for e in range(2):
                    dve.wait_ge(s_hi, t * 2 + (e + 1))
                    dve.scalar_tensor_tensor(SB[:, e, :, 1, :], psS[:, e, 0:CK * KEEP].rearrange("p (k t) -> p k t", k=CK),
                                             XSC, SB[:, e, :, 0, :], ALU.mult, ALU.subtract).then_inc(s_lo, 1)

        @block.scalar
        def _(act):
            act.wait_ge(turned, 1)
            act.activation(score_t[:, :], ps1[0:NT, 0:P], ACT.Copy).then_inc(copied, 1)
            act.wait_ge(shifted, 1)
            act.activation(ge[:, :, :], gl[:, :, :], ACT.Exp).then_inc(expd, 1)
            act.wait_ge(turned, 2)
            act.activation(rank_n[:, :], ps2[:, 0:NT], ACT.Copy).then_inc(copied, 1)
            with act.Fori(0, B // 2) as t:
                for e in range(2):
                    act.wait_ge(stored[e], t * 16)
                    act.wait_ge(picked, t * 2 + (e + 1))
                    act.activation(SB[:, e, :, 0, :], psS[:, e, 0:CK * KEEP].rearrange("p (k t) -> p k t", k=CK),
                                   ACT.Copy, scale=XSC).then_inc(s_hi, 1)

        @block.tensor
        def _(pe):
            pe.wait_ge(const_in, 64)
            pe.transpose(ps1[0:NT, 0:P], score_n[:, :], ident[:, :]).then_inc(turned, 1)
            pe.wait_ge(moved, 64)
            pe.transpose(ps2[:, 0:NT], rank_t[:, :], ident[0:NT, 0:NT]).then_inc(turned, 1)
            with pe.Fori(0, B // 2) as t:
                for e in range(2):
                    pe.wait_ge(x_in[e], t * 16 + 16)
                    pe.wait_ge(hot_ready, t * 2 + (e + 1))
                    pe.wait_ge(s_lo, t * 2)
                    for c in range(CK):
                        for k in range(GT):
                            last = pe.matmul(psS[:, e, c * KEEP:(c + 1) * KEEP], XN[:, e, k, c * P:(c + 1) * P], hot[:, e, k, :],
                                             start=(k == 0), stop=(k == GT - 1))
                    last.then_inc(picked, 1)


LATENT_KEYS, WINDOW_KEYS, CHOSEN_KEYS = 0, 1, 2
GATE = (0, 2, 1)
BANK = 512
HB = T // BANK
PROJECT = ([("v", k, c) for k in range(2) for c in range(HB)] + [("chosen_v",)]
           + [("plain", n, c) for n in ("k", "w", "q") for c in range(HB)] + [("chosen_k",)]
           + [("turn", n, c, y) for n in ("q", "w") for c in range(HB) for y in range(2)])
NEAR = PROJECT.index(("chosen_k",))
SPLIT = ("plain", "chosen_k")
MAXIMA = ([(k, i, c) for i in range(GT) for k in (LATENT_KEYS, WINDOW_KEYS) for c in range((i * P) // BANK + 1)]
          + [(CHOSEN_KEYS, 0, 0)])
NM = len(MAXIMA)
RING = 3
MAX_SHARE, ROW_AT = 0.8, 0.86
SR = 3 * HG * GT


def main_steps(j):
    steps = []
    for p in range(GT):
        first = (p * P) // BANK
        for k in (LATENT_KEYS, WINDOW_KEYS):
            for c in range(first, HB):
                w = (c + 1) * BANK - max(p * P, c * BANK)
                steps.append((("S", j, k, p, c), 3 * w))
        if p:
            for c in range(((p - 1) * P) // BANK, HB):
                w = (c + 1) * BANK - max((p - 1) * P, c * BANK)
                steps.append((("PV", j, p - 1, c), 5 * w))
    for c in range(HB):
        steps.append((("S", j, CHOSEN_KEYS, 0, c), 3 * BANK))
    steps.append((("PV", j, GT - 1, HB - 1), 5 * P))
    steps.append((("OUT", j), 0))
    return steps


def spread(fill, start, end):
    return [(start + (end - start) * (n + 0.5) / len(fill), f) for n, f in enumerate(fill)] if fill else []


def with_ropes(projections, apart):
    items, joins = [], []
    for g in projections:
        items.append(("G",) + g)
        joins = [(left - 1, join) for left, join in joins]
        items += [join for left, join in joins if left <= 0]
        joins = [x for x in joins if x[0] > 0]
        if (g[0] == "turn" and g[3] == 1) or g[0] == "chosen_k":
            rope = (g[1], g[2]) if g[0] == "turn" else ("chosen", 0)
            items.append(("ROPE",) + rope)
            if apart:
                joins.append((apart, ("JOIN",) + rope))
            else:
                items.append(("JOIN",) + rope)
    return items + [join for _, join in joins]


def group_plan():
    plan = []
    for j in range(HG):
        fill = spread([("MAX", (j + 1) % HG, n) for n in range(NM)], 0.0, MAX_SHARE) 
        fill += [(MAX_SHARE, ("MERGE", (j + 1) % HG)), (ROW_AT, ("MAXROW", (j + 1) % HG))]
        if j:
            fill += spread([("G", "chosen_o", j - 1)], 0.08, 0.1)
        if j == 0:
            fill += [(0.45, ("INVERT",)), (0.9, ("MIX",))]
            fill += spread([("G",) + g for g in PROJECT[:NEAR]], 0.12, 1.0)
        elif j == 1:
            fill += spread(with_ropes(PROJECT[NEAR:], 1), 0.12, 1.0)
        fill.sort(key=lambda f: f[0])
        main = main_steps(j)
        total = sum(w for _, w in main)
        at = 0
        for step, w in main:
            plan.append(step)
            at += w
            while fill and fill[0][0] * total <= at:
                plan.append(fill.pop(0)[1])
        plan += [f for _, f in fill]
    plan.append(("G", "chosen_o", HG - 1))
    return plan


def first_plan():
    return with_ropes(PROJECT, 0) + [("MAX", 0, n) for n in range(NM)] + [("MERGE", 0), ("MAXROW", 0)]


def general_jobs(plan):
    return [s for s in plan if s[0] in ("G", "MAXROW")]


def is_split(job):
    return job[0] == "G" and job[1] in SPLIT


rope_order = [(x[1], x[2]) for x in first_plan() if x[0] == "ROPE"]
rope_buf = {r: n % 2 for n, r in enumerate(rope_order)}


def job_index(plan):
    found = {}
    for n, x in enumerate(general_jobs(plan)):
        if x[:2] == ("G", "turn") and x[4] == 1:
            found[(x[2], x[3])] = n
        if x[:2] == ("G", "chosen_k"):
            found[("chosen", 0)] = n
    return found


first_turn, turn_job = job_index(first_plan()), job_index(group_plan())


def attention(nc, consts, s):
    with ExitStack() as ctx:
        def sb(n, shape, dt=F32):
            return ctx.enter_context(nc.sbuf_tensor("a_" + n, shape, dt))

        def pb(n, shape, dt=F32):
            return ctx.enter_context(nc.psum_tensor("a_" + n, shape, dt))

        def sem(n):
            return nc.alloc_semaphore("a_" + n)

        K99 = D + 3
        ident, mask = sb("ident", [P, P]), sb("mask", [P, 3, P], F16)
        cos, sin = sb("cos", [P, T]), sb("sin", [P, T])
        W = sb("W", [P, W_COLS], F16)
        XB, NB = sb("XB", [P, CK, HL, T], F16), sb("NB", [P, HL, T], F16)
        SB = sb("SB", [P, CK, HL, KEEP], F16)
        gates = sb("gates", [SR, 1])
        Qs, Ws, Ks = sb("Qs", [P, 3, HL, T], F16), sb("Ws", [P, 3, HL, T], F16), sb("Ks", [P, HL, T], F16)
        Cs = sb("Cs", [P, 3, HL, KEEP], F16)
        Vs, CVs = sb("Vs", [P, 2, GT, P]), sb("CVs", [KEEP, P])
        raw = sb("raw", [P, 2, 2, BANK])
        turned_, pool_t = sb("turned_", [P, 2, BANK]), sb("pool_t", [P, 2, BANK])
        Q, K1, KW = (sb(n, [K99, HG, HL, T], F16) for n in ("Q", "K1", "KW"))
        KC = sb("KC", [K99, HG, HL, KEEP], F16)
        V, VC = sb("V", [P, 2, HG, GT, 2 * DV]), sb("VC", [P, HG, 2 * DV])
        maxima, parts = sb("maxima", [P, 3 * GT]), sb("parts", [P, 2, HB, GT])
        max_rows = sb("max_rows", [3 * GT, P], F16)
        prob = sb("prob", [P, 2, 2, T])
        prob_c = sb("prob_c", [P, T])
        o_raw, oc_raw = sb("o_raw", [P, T]), sb("oc_raw", [P, BANK])
        o_val, o_inv = sb("o_val", [P, 3, T]), sb("o_inv", [P, 3, T])
        sums = sb("sums", [SR, P])
        mix, zero = sb("mix", [P, HL, T], F16), sb("zero", [P, 1])
        psS, psO = pb("psS", [P, RING, BANK]), pb("psO", [P, T])
        psM, psG = pb("psM", [P, 2, BANK]), pb("psG", [P, BANK])

        const_in, ones_set, w_in, gates_in = sem("const_in"), sem("ones_set"), sem("w_in"), sem("gates_in")
        g_mm, g_act, g_dve = sem("g_mm"), sem("g_act"), sem("g_dve")
        r_step, r_pool, roped = sem("r_step"), sem("r_pool"), sem("roped")
        slot_in = [sem(f"slot_in{j}") for j in range(HG)]
        m_mm, m_red, m_ready, rows_in = (sem(n) for n in ("m_mm", "m_red", "m_ready", "rows_in"))
        s_mm, exp_done, pv_mm = sem("s_mm"), sem("exp_done"), sem("pv_mm")
        v_copied, o_out, o_moved = sem("v_copied"), sem("o_out"), sem("o_moved")
        oc_moved = sem("oc_moved")
        sums_in, inverse, inverse_out, inverse_in, weighed, mix_hi, mix_done, mix_stored = (sem(n) for n in
                                                          ("sums_in", "inverse", "inverse_out", "inverse_in", "weighed", "mix_hi", "mix_done", "mix_stored"))
        p_step, set_, set_sums, inverted = sem("p_step"), sem("set"), sem("set_sums"), sem("inverted")
        CONSTS = 16 * (4 + 3)

        plan, first = group_plan(), first_plan()
        jobs, first_jobs = general_jobs(plan), general_jobs(first)
        NJ, FJ = len(jobs), len(first_jobs)
        ND, FD = sum(map(is_split, jobs)), sum(map(is_split, first_jobs))
        NR = sum(1 for x in plan if x[0] == "ROPE")
        units = [x for x in plan if x[0] == "S"]
        unit_of = {x[1:]: n for n, x in enumerate(units)}
        NU = len(units)
        NPV = HG * GT
        SLOT_DMAS = 3 + 3 + 3 + 2

        row_jobs = [n + 1 for n, x in enumerate(jobs) if x[0] == "MAXROW"]
        last_project = jobs.index(("G",) + PROJECT[-1]) + 1

        def chosen_o_job(j):
            return jobs.index(("G", "chosen_o", j)) + 1

        def weights(at, rows, *dims):
            n = int(np.prod(dims)) * P
            lo = 0 if rows != KL else QL
            ap = W[lo:lo + rows, at:at + n]
            names = " ".join("abc"[:len(dims)])
            return ap.rearrange(f"p ({names} m) -> p {names} m", **dict(zip("abc", dims)))

        w_win, w_sel = weights(W_WIN, P, HL, CK, 3), weights(W_SEL, P, HL, CK, 3)
        w_winv, w_selv = weights(W_WINV, P, HL, CK), weights(W_SELV, P, HL, CK)
        w_q, w_dk, w_dv = weights(W_Q, QL, HL, 3), weights(W_DK, KL, HL), weights(W_DV, KL, HL)

        block = ctx.enter_context(nc.Block())

        @block.sync
        def _(sp):
            sp.dma_start(ident[:, :], consts["c_ident"]).then_inc(const_in, 16)
            sp.dma_start(mask[:, :, :], consts["c_mask"].rearrange("p (a q) -> p a q", a=3)).then_inc(const_in, 16)
            sp.dma_start(cos[:, :], consts["c_cosT"]).then_inc(const_in, 16)
            sp.dma_start(sin[:, :], consts["c_sinT"]).then_inc(const_in, 16)
            for k, dst in enumerate((K1, KW, KC)):
                n = dst.shape[3]
                sp.dma_start(dst[D:K99, :, 0, :], consts["c_shift"][k][:, :, 0:n]).then_inc(const_in, 16)

            def load(m):
                g, b = sp.snap(m % G), sp.snap(m // G)
                sp.dma_start(W[:, 0:W_Q], s["wsplit"][bass.ds(g, 1), :, 0:W_Q].rearrange("g p n -> p (g n)")).then_inc(w_in, 16)
                sp.dma_start(W[0:QL, W_Q:W_DK], s["wsplit"][bass.ds(g, 1), 0:QL, W_Q:W_DK].rearrange("g p n -> p (g n)")).then_inc(w_in, 16)
                sp.dma_start(W[QL:P, W_DK:W_COLS], s["wsplit"][bass.ds(g, 1), QL:P, W_DK:W_COLS].rearrange("g p n -> p (g n)")).then_inc(w_in, 16)
                sp.dma_start(XB[:, :, :, :].rearrange("p k l t -> p (k l t)"), s["xt"][bass.ds(b, 1)].rearrange("b p n -> p (b n)")).then_inc(w_in, 16)
                sp.dma_start(NB[:, :, :].rearrange("p l t -> p (l t)"), s["lat"][bass.ds(b, 1)].rearrange("b p n -> p (b n)")).then_inc(w_in, 16)
                sp.dma_start(SB[:, :, :, :].rearrange("p k l t -> p (k l t)"), s["sel"][bass.ds(b, 1)].rearrange("b p n -> p (b n)")).then_inc(w_in, 16)

            def repack(j, b):
                rows = slice(j * NOPE, (j + 1) * NOPE)
                for stage, slot in ((Qs, Q), (Ws, KW), (Cs, KC)):
                    for y in range(3):
                        sp.dma_start(slot[y * NOPE:(y + 1) * NOPE, j, :, :], stage[rows, y, :, :]).then_inc(slot_in[j], 16)
                sp.dma_start(K1[0:NOPE, j, :, :], Ks[rows, :, :]).then_inc(slot_in[j], 16)
                sp.dma_start(K1[NOPE:D, j, :, :].rearrange("p l t -> p (l t)"),
                             s["kr"][bass.ds(b, 1)].rearrange("b p n -> p (b n)")).then_inc(slot_in[j], 16)

            def move_out(n, j):
                rows = slice(j * DV, (j + 1) * DV)
                sp.wait_ge(o_out, n * HG + (j + 1))
                for k in range(2):
                    sp.dma_start(o_val[rows, k, :], o_raw[64 * k:64 * k + DV, :]).then_inc(o_moved, 16)
                    sp.dma_start(s["sums"][GATE[k], j:j + 1, :], o_raw[64 * k + DV:64 * k + DV + 1, :]).then_inc(o_moved, 16)

            def move_chosen(job, j):
                rows = slice(j * DV, (j + 1) * DV)
                sp.wait_ge(g_act, job)
                for c in range(HB):
                    cols = slice(c * BANK, (c + 1) * BANK)
                    sp.dma_start(o_val[rows, 2, cols], oc_raw[64 * c:64 * c + DV, :]).then_inc(oc_moved, 16)
                    sp.dma_start(s["sums"][GATE[CHOSEN_KEYS], j:j + 1, cols], oc_raw[64 * c + DV:64 * c + DV + 1, :]).then_inc(oc_moved, 16)

            def staged(m):
                split_all, roped_all = m * ND + ND, m * NR + NR
                if not isinstance(m, int):
                    split_all, roped_all = sp.snap(split_all), sp.snap(roped_all)
                sp.wait_ge(g_dve, split_all)
                sp.wait_ge(roped, roped_all)

            def store_mix(n):
                sp.wait_ge(mix_done, n * 2 + 2)
                row = s["mixed"][n] if isinstance(n, int) else s["mixed"][bass.ds(n, 1)].rearrange("n p c -> p (n c)")
                sp.dma_start(row, mix[:, :, :].rearrange("p l t -> p (l t)")).then_inc(mix_stored, 16)

            def turn_sums(moved, earlier, used):
                sp.wait_ge(o_moved, moved)
                sp.wait_ge(oc_moved, moved)
                sp.dma_start(sums[:, :], s["sums"].rearrange("k h (c t) -> (k h c) t", t=P)).then_inc(sums_in, 16)
                sp.wait_ge(inverse, earlier + 1)
                sp.dma_start(s["inverses"].rearrange("k h (c t) -> (k h c) t", t=P), sums[:, :]).then_inc(inverse_out, 16)
                sp.wait_ge(weighed, used)
                sp.wait_ge(inverse_out, earlier * 16 + 16)
                for k in range(3):
                    sp.dma_start(o_inv[:, k, :], s["inverses"][GATE[k]].unsqueeze(1).broadcast_to([HG, DV, T])).then_inc(inverse_in, 16)

            sp.wait_ge(set_sums, 1)
            sp.dma_start(s["sums"].rearrange("k h (c t) -> (k h c) t", t=P), sums[:, :]).then_inc(sums_in, 16)
            sp.wait_ge(sums_in, 16)
            load(0)
            staged(0)
            for j in range(HG):
                repack(j, 0)
            load(1)
            with sp.Fori(0, B * G) as n:
                nxt = sp.snap((n + 1) % (B * G))
                after = sp.snap((n + 2) % (B * G))
                here, next_batch = sp.snap(n + 0), sp.snap(nxt // G)
                batch = sp.snap(((n + (B * G - 1)) % (B * G)) // G)
                moved, used = sp.snap(here * (64 * HG)), sp.snap(here * 5)
                sp.dma_start(gates[:, :], s["gates"][bass.ds(batch, 1), 0:HG * GT, :].rearrange("b p g -> (b g) p").unsqueeze(2),
                             allow_slow_non_contiguous=True).then_inc(gates_in, 16)
                turn_sums(moved, here, used)
                store_mix(here)
                move_out(here, 0)
                move_chosen(here * NJ + (FJ + chosen_o_job(0)), 0)
                staged(here + 1)
                for j in range(HG):
                    scored = sp.snap(here * NU + (unit_of[(j, CHOSEN_KEYS, 0, HB - 1)] + 1))
                    chosen_out = sp.snap(here * NJ + (FJ + chosen_o_job(j)))
                    if j:
                        move_out(here, j)
                        move_chosen(chosen_out, j)
                    sp.wait_ge(s_mm, scored)
                    repack(j, next_batch)
                    if j == 0:
                        load(after)
            sp.dma_start(gates[:, :], s["gates"][B - 1, 0:HG * GT, :].rearrange("p g -> g p").unsqueeze(2), allow_slow_non_contiguous=True).then_inc(gates_in, 16)
            turn_sums(B * G * 64 * HG, B * G, B * G * 5)
            store_mix(B * G)
            sp.wait_ge(mix_stored, 16 * (B * G + 1))
            sp.wait_ge(w_in, 16 * 6 * (B * G + 2))
            for j in range(HG):
                sp.wait_ge(slot_in[j], 16 * SLOT_DMAS * (B * G + 1))
            sp.wait_ge(rows_in, 16 * (B * G * HG + 1))

        @block.gpsimd
        def _(pool):
            ones = Steps(pool, ones_set)
            ones.one(pool.memset(V[:, :, :, :, :].rearrange("p k j i d -> p (k j i) d")[:, :, DV:2 * DV], 1.0))
            ones.one(pool.memset(VC[0:KEEP, :, DV:2 * DV], 1.0))
            ones.one(pool.memset(VC[KEEP:P, :, :], 0.0))
            ones.one(pool.memset(prob_c[KEEP:P, :], 0.0))
            pool.wait_ge(const_in, CONSTS)
            pool.wait_ge(ones_set, 4)
            zeros = Steps(pool, set_)
            zeros.one(pool.memset(o_val[:, :, :], 0.0))
            zeros.one(pool.memset(zero[:, :], 0.0))

            def rope(count, name, c, r):
                n = KEEP if name == "chosen" else BANK
                job = first_turn[(name, c)] if r is None else turn_job[(name, c)]
                base = 0 if r is None else FJ
                pool.wait_ge(g_act, (0 if r is None else r * NJ) + (base + job + 1))
                pool.wait_ge(roped, count)
                buf = rope_buf[(name, c)]
                cs, sn = cos[:, c * BANK:c * BANK + n], sin[:, c * BANK:c * BANK + n]
                pool.tensor_tensor(pool_t[:, 0, 0:n], raw[:, buf, 0, 0:n], sn, ALU.mult).then_inc(p_step, 1)
                pool.tensor_tensor(pool_t[:, 1, 0:n], raw[:, buf, 1, 0:n], cs, ALU.mult).then_inc(p_step, 1)
                pool.wait_ge(p_step, count * 2 + 2)
                pool.tensor_tensor(pool_t[:, 0, 0:n], pool_t[:, 0, 0:n], pool_t[:, 1, 0:n], ALU.add).then_inc(r_pool, 1)

            def copy_values(j):
                cols = slice(j * DV, (j + 1) * DV)
                pool.tensor_tensor(VC[0:KEEP, j, 0:DV], CVs[:, cols], zero[0:KEEP, :].broadcast_to([KEEP, DV]), ALU.add).then_inc(v_copied, 1)
                pool.tensor_copy(V[:, :, j, :, 0:DV], Vs[:, :, :, cols]).then_inc(v_copied, 1)

            def mix_group(n):
                pool.wait_ge(inverse_in, n * 48 + 48)
                for k in range(3):
                    pool.tensor_tensor(o_val[:, k, :], o_val[:, k, :], o_inv[:, k, :], ALU.mult).then_inc(weighed, 1)
                pool.wait_ge(weighed, n * 5 + 3)
                pool.tensor_tensor(o_val[:, 0, :], o_val[:, 0, :], o_val[:, 1, :], ALU.add).then_inc(weighed, 1)
                pool.wait_ge(weighed, n * 5 + 4)
                pool.tensor_tensor(o_val[:, 0, :], o_val[:, 0, :], o_val[:, 2, :], ALU.add).then_inc(weighed, 1)
                pool.wait_ge(weighed, n * 5 + 5)
                pool.wait_ge(mix_stored, n * 16)
                pool.tensor_tensor(mix[:, 0, :], o_val[:, 0, :], zero[:, :].broadcast_to([P, T]), ALU.add).then_inc(mix_done, 1)
                pool.wait_ge(mix_done, n * 2 + 1)
                pool.tensor_tensor(mix[:, 1, :], o_val[:, 0, :], mix[:, 0, :], ALU.subtract).then_inc(mix_done, 1)

            r = 0
            for x in first:
                if x[0] == "ROPE":
                    rope(r, x[1], x[2], None)
                    r += 1
            for j in range(HG):
                copy_values(j)
            with pool.Fori(0, B * G) as n:
                r = 0
                for x in plan:
                    if x[0] == "ROPE":
                        rope(n * NR + (NR + r), x[1], x[2], n)
                        r += 1
                    if x[0] == "MIX":
                        mix_group(n)
                    if x == ("OUT", 1):
                        pool.wait_ge(g_act, n * NJ + (FJ + chosen_o_job(0)))
                        copy_values(0)
                for j in range(1, HG):
                    pool.wait_ge(pv_mm, n * NPV + (j + 1) * GT)
                    pool.wait_ge(g_act, n * NJ + (FJ + chosen_o_job(j)))
                    copy_values(j)
            mix_group(B * G)

        @block.vector
        def _(dve):
            dve.wait_ge(const_in, CONSTS)

            def split_job(job, index, m):
                dve.wait_ge(g_act, index)
                scale = QSC / (XSC * WSC)
                if job[1] == "plain":
                    stage = {"q": Qs[:, 0], "w": Ws[:, 0], "k": Ks[:, :, :]}[job[2]]
                    cols = slice(job[3] * BANK, (job[3] + 1) * BANK)
                    dve.scalar_tensor_tensor(stage[:, 1, cols], psG[:, :], scale, stage[:, 0, cols],
                                             ALU.mult, ALU.subtract).then_inc(g_dve, 1)
                else:
                    dve.scalar_tensor_tensor(Cs[:, 0, 1, :], psG[:, 0:KEEP], scale, Cs[:, 0, 0, :],
                                             ALU.mult, ALU.subtract).then_inc(g_dve, 1)

            def rope(count, name, c):
                n = KEEP if name == "chosen" else BANK
                stage = {"q": Qs, "w": Ws, "chosen": Cs}[name]
                cols = slice(c * BANK, c * BANK + n)
                buf = rope_buf[(name, c)]
                steps = Steps(dve, r_step, count * 6)
                steps.wait()
                steps.done(dve.tensor_tensor(turned_[:, 0, 0:n], raw[:, buf, 0, 0:n], cos[:, c * BANK:c * BANK + n], ALU.mult))
                steps.one(dve.tensor_tensor(turned_[:, 1, 0:n], raw[:, buf, 1, 0:n], sin[:, c * BANK:c * BANK + n], ALU.mult))
                steps.one(dve.tensor_tensor(turned_[:, 0, 0:n], turned_[:, 0, 0:n], turned_[:, 1, 0:n], ALU.subtract))
                steps.one(dve.tensor_copy(stage[:, 1, 0, cols], turned_[:, 0, 0:n]))
                steps.done(dve.tensor_tensor(stage[:, 1, 1, cols], turned_[:, 0, 0:n], stage[:, 1, 0, cols], ALU.subtract))

            def join(count, name, c):
                n = KEEP if name == "chosen" else BANK
                stage = {"q": Qs, "w": Ws, "chosen": Cs}[name]
                cols = slice(c * BANK, c * BANK + n)
                steps = Steps(dve, r_step, count * 6 + 5)
                dve.wait_ge(r_pool, count + 1)
                steps.one(dve.tensor_copy(stage[:, 2, 0, cols], pool_t[:, 0, 0:n]))
                dve.tensor_tensor(stage[:, 2, 1, cols], pool_t[:, 0, 0:n], stage[:, 2, 0, cols], ALU.subtract).then_inc(roped, 1)

            def maxima_piece(turns, before, n):
                k, i, c = MAXIMA[n]
                dve.wait_ge(m_mm, turns + (before + 1))
                if k == CHOSEN_KEYS:
                    ins = dve.tensor_reduce(maxima[:, 2 * GT:3 * GT], psM[:, before % 2, :].rearrange("p (i k) -> p i k", k=KEEP), AX, ALU.max)
                else:
                    w = min((i + 1) * P - c * BANK, BANK)
                    ins = dve.tensor_reduce(parts[:, k, c, i:i + 1], psM[:, before % 2, 0:w], AX, ALU.max)
                ins.then_inc(m_red, 1)

            def merge(done):
                dve.wait_ge(m_red, done)
                dve.tensor_reduce(maxima[:, 0:2 * GT].rearrange("p (k i) -> p k i", k=2),
                                  parts[:, :, :, :].rearrange("p k c i -> p k i c"), AX, ALU.max).then_inc(m_ready, 1)

            def invert(n):
                dve.wait_ge(sums_in, n * 16 + 32)
                dve.wait_ge(gates_in, n * 16 + 16)
                steps = Steps(dve, inverted, n)
                steps.one(dve.reciprocal(sums[:, :], sums[:, :]))
                dve.tensor_scalar(sums[:, :], sums[:, :], gates[:, 0:1], QSC, ALU.mult, ALU.mult).then_inc(inverse, 1)

            dve.memset(sums[:, :], 1.0).then_inc(set_sums, 1)
            dve.memset(parts[:, :, :, :], -3.0e38).then_inc(set_sums, 1)
            dve.wait_ge(set_sums, 2)
            done, q = 0, 0
            r = 0
            for x in first:
                if x[0] in ("G", "MAXROW"):
                    q += 1
                if is_split(x):
                    split_job(x, q, 0)
                if x[0] == "ROPE":
                    dve.wait_ge(g_act, first_turn[(x[1], x[2])] + 1)
                    rope(r, x[1], x[2])
                if x[0] == "JOIN":
                    join(r, x[1], x[2])
                    r += 1
                if x[0] == "MAX":
                    maxima_piece(0, done, x[2])
                    done += 1
                if x[0] == "MERGE":
                    merge(done)
            with dve.Fori(0, B * G) as n:
                done, q, r, heads = 0, 0, 0, 0
                for x in plan:
                    if x[0] in ("G", "MAXROW"):
                        q += 1
                    if is_split(x):
                        split_job(x, n * NJ + (FJ + q), n)
                    if x[0] == "OUT":
                        j = x[1]
                        dve.wait_ge(pv_mm, n * NPV + (j + 1) * GT)
                        dve.wait_ge(o_moved, n * (64 * HG) + 64 * j)
                        dve.tensor_copy(o_raw[:, :], psO[:, :]).then_inc(o_out, 1)
                    if x[0] == "INVERT":
                        invert(n)
                    if x[0] == "ROPE":
                        dve.wait_ge(g_act, n * NJ + (FJ + turn_job[(x[1], x[2])] + 1))
                        rope(n * NR + (NR + r), x[1], x[2])
                    if x[0] == "JOIN":
                        join(n * NR + (NR + r), x[1], x[2])
                        r += 1
                    if x[0] == "MAX":
                        if x[2] == 0:
                            dve.wait_ge(g_mm, n * NJ + (FJ + row_jobs[heads - 1] if heads else FJ))
                        maxima_piece(n * (HG * NM), NM + done, x[2])
                        done += 1
                    if x[0] == "MERGE":
                        merge(n * (HG * NM) + (NM + done))
                        heads += 1
            invert(B * G)

        @block.scalar
        def _(act):
            act.wait_ge(const_in, CONSTS)

            def copy_job(job, q, m, ropes, start):
                act.wait_ge(g_mm, q)
                scale = 1.0 / (XSC * WSC)
                kind = job[1]
                if kind == "v":
                    if not start:
                        act.wait_ge(v_copied, m * (2 * HG))
                    i = job[3] * (BANK // P)
                    act.activation(Vs[:, job[2], i:i + BANK // P, :], psG[:, :].rearrange("p (i d) -> p i d", d=P),
                                   ACT.Copy, scale=scale).then_inc(g_act, 1)
                elif kind == "chosen_v":
                    act.activation(CVs[:, :], psG[0:KEEP, 0:P], ACT.Copy, scale=scale).then_inc(g_act, 1)
                elif kind == "plain":
                    if not start:
                        for j in range(HG):
                            act.wait_ge(slot_in[j], m * (16 * SLOT_DMAS))
                    stage = {"q": Qs[:, 0], "w": Ws[:, 0], "k": Ks[:, :, :]}[job[2]]
                    act.activation(stage[:, 0, job[3] * BANK:(job[3] + 1) * BANK], psG[:, :], ACT.Copy,
                                   scale=QSC * scale).then_inc(g_act, 1)
                elif kind == "chosen_k":
                    act.wait_ge(roped, ropes("chosen", 0))
                    act.activation(raw[:, rope_buf[("chosen", 0)], :, 0:KEEP],
                                   psG[:, KEEP:3 * KEEP].rearrange("p (y t) -> p y t", y=2), ACT.Copy, scale=QSC * scale)
                    act.activation(Cs[:, 0, 0, :], psG[:, 0:KEEP], ACT.Copy, scale=QSC * scale).then_inc(g_act, 1)
                elif kind == "turn":
                    act.wait_ge(roped, ropes(job[2], job[3]))
                    act.activation(raw[:, rope_buf[(job[2], job[3])], job[4], :], psG[:, :], ACT.Copy,
                                   scale=QSC * scale).then_inc(g_act, 1)

            def chosen_out(q, moved):
                act.wait_ge(g_mm, q)
                act.wait_ge(oc_moved, moved)
                act.activation(oc_raw[:, :], psG[:, :], ACT.Copy).then_inc(g_act, 1)

            def max_row(q, j, heads):
                act.wait_ge(g_mm, q)
                act.wait_ge(rows_in, heads * 16)
                act.activation(max_rows[:, :], psG[0:3 * GT, 0:P], ACT.Copy, scale=-1.0 / SHIFT).then_inc(g_act, 1)
                act.wait_ge(g_act, q)
                act.dma_start(Q[D:K99, j, 0, :].rearrange("k (i t) -> k i t", t=P), max_rows[:, :]).then_inc(rows_in, 16)

            q = 0
            for x in first:
                if x[0] == "G":
                    q += 1
                    copy_job(x, q, 0, lambda name, c: max(rope_order.index((name, c)) - 1, 0), True)
                if x[0] == "MAXROW":
                    q += 1
                    max_row(q, 0, 0)
            with act.Fori(0, B * G) as n:
                q = u = heads = 0
                for x in plan:
                    if x[0] == "G" and x[1] == "chosen_o":
                        q += 1
                        chosen_out(n * NJ + (FJ + q), n * (64 * HG) + 64 * x[2])
                    elif x[0] == "G":
                        q += 1
                        copy_job(x, n * NJ + (FJ + q), n + 1,
                                 lambda name, c: n * NR + (NR + max(rope_order.index((name, c)) - 1, 0)), False)
                    elif x[0] == "MAXROW":
                        q += 1
                        max_row(n * NJ + (FJ + q), x[1], n * HG + (heads + 1))
                        heads += 1
                    elif x[0] == "S":
                        _s, j, k, p, c = x
                        act.wait_ge(s_mm, n * NU + (u + 1))
                        a, end = max(p * P, c * BANK), (c + 1) * BANK
                        tile = psS[:, u % RING, a - c * BANK:BANK]
                        if k == CHOSEN_KEYS:
                            if j == 0:
                                act.wait_ge(g_mm, n * NJ + FJ)
                            else:
                                act.wait_ge(g_mm, n * NJ + (FJ + chosen_o_job(j - 1)))
                            act.activation(prob_c[0:KEEP, a:end], tile[0:KEEP, :], ACT.Exp, scale=EXP_SCALE).then_inc(exp_done, 1)
                        else:
                            pair = j * GT + p
                            if c == (p * P) // BANK:
                                act.wait_ge(pv_mm, n * NPV + (pair - 1) if pair > 1 else n * NPV)
                            act.activation(prob[:, pair % 2, k, a:end], tile, ACT.Exp, scale=EXP_SCALE).then_inc(exp_done, 1)
                        u += 1

        @block.tensor
        def _(pe):
            pe.wait_ge(const_in, CONSTS)
            pe.wait_ge(ones_set, 4)

            def three(out, left, right):
                terms = [(l[a], r[b]) for l, r in zip(left, right) for a, b in PRODUCTS]
                for i, (l, r) in enumerate(terms):
                    last = pe.matmul(out, l, r, start=(i == 0), stop=(i == len(terms) - 1))
                return last

            def project(job):
                kind = job[1]
                if kind == "v":
                    for i in range(BANK // P):
                        t = job[3] * (BANK // P) + i
                        tile = slice(t * P, (t + 1) * P)
                        out = psG[:, i * P:(i + 1) * P]
                        if job[2] == LATENT_KEYS:
                            last = three(out, [[NB[QL:P, l, tile] for l in range(HL)]], [[w_dv[:, l, :] for l in range(HL)]])
                        else:
                            last = three(out, [[XB[:, c, l, tile] for l in range(HL)] for c in range(CK)],
                                         [[w_winv[:, l, c, :] for l in range(HL)] for c in range(CK)])
                elif kind == "chosen_v":
                    last = three(psG[0:KEEP, 0:P], [[SB[:, c, l, :] for l in range(HL)] for c in range(CK)],
                                 [[w_selv[:, l, c, :] for l in range(HL)] for c in range(CK)])
                elif kind == "chosen_k":
                    for y in range(3):
                        last = three(psG[:, y * KEEP:(y + 1) * KEEP],
                                     [[w_sel[:, l, c, y, :] for l in range(HL)] for c in range(CK)],
                                     [[SB[:, c, l, :] for l in range(HL)] for c in range(CK)])
                else:
                    name, c = job[2], job[3]
                    y = 0 if kind == "plain" else 1 + job[4]
                    cols = slice(c * BANK, (c + 1) * BANK)
                    if name == "q":
                        last = three(psG[:, :], [[w_q[:, l, y, :] for l in range(HL)]], [[NB[0:QL, l, cols] for l in range(HL)]])
                    elif name == "k":
                        last = three(psG[:, :], [[w_dk[:, l, :] for l in range(HL)]], [[NB[QL:P, l, cols] for l in range(HL)]])
                    else:
                        last = three(psG[:, :], [[w_win[:, l, k, y, :] for l in range(HL)] for k in range(CK)],
                                     [[XB[:, k, l, cols] for l in range(HL)] for k in range(CK)])
                last.then_inc(g_mm, 1)

            def bank_free(before, jobs_done, split_done):
                if before is not None and is_split(before):
                    pe.wait_ge(g_dve, split_done)
                else:
                    pe.wait_ge(g_act, jobs_done)

            def maxima_piece(j, n, turns, before):
                k, i, c = MAXIMA[n]
                buf = before % 2
                if before > 1:
                    pe.wait_ge(m_red, turns + (before - 1))
                if k == CHOSEN_KEYS:
                    for t in range(GT):
                        last = pe.matmul(psM[:, buf, t * KEEP:(t + 1) * KEEP], Q[0:D, j, 0, t * P:(t + 1) * P], KC[0:D, j, 0, :],
                                         start=True, stop=True)
                else:
                    keys = (K1, KW)[k]
                    w = min((i + 1) * P - c * BANK, BANK)
                    diagonal = (i * P) // BANK == c
                    last = pe.matmul(psM[:, buf, 0:w], Q[0:D, j, 0, i * P:(i + 1) * P],
                                     keys[0:D, j, 0, c * BANK:c * BANK + w], start=True, stop=not diagonal)
                    if diagonal:
                        last = pe.matmul(psM[:, buf, w - P:w], mask[:, 0, :], mask[:, 2, :], start=False, stop=True)
                last.then_inc(m_mm, 1)

            def scores(j, k, p, c, u):
                keys = (K1, KW, KC)[k]
                rows = KEEP if k == CHOSEN_KEYS else P
                a = max(p * P, c * BANK)
                out = psS[0:rows, u % RING, a - c * BANK:BANK]
                tile = slice(p * rows, (p + 1) * rows)
                cols = slice(a, (c + 1) * BANK)
                diagonal = k != CHOSEN_KEYS and a == p * P
                pe.matmul(out, keys[:, j, 0, tile], Q[:, j, 0, cols], start=True, stop=False)
                pe.matmul(out, keys[0:D, j, 0, tile], Q[0:D, j, 1, cols], start=False, stop=False)
                last = pe.matmul(out, keys[0:D, j, 1, tile], Q[0:D, j, 0, cols], start=False, stop=not diagonal)
                if diagonal:
                    last = pe.matmul(out[:, 0:P], mask[:, 0, :], mask[:, 1, :], start=False, stop=True)
                return last

            def values(j, p, c):
                a = max(p * P, c * BANK)
                for k in range(2):
                    last = pe.matmul(psO[64 * k:64 * k + 64, a:(c + 1) * BANK], V[:, k, j, p, :],
                                     prob[:, (j * GT + p) % 2, k, a:(c + 1) * BANK], start=(p == 0),
                                     stop=(p * P + P >= (c + 1) * BANK))
                return last

            pe.wait_ge(w_in, 16 * 6)
            q = d = done = 0
            before = None
            for x in first:
                if x[0] == "G":
                    if q:
                        bank_free(before, q, d)
                    project(x)
                    q += 1
                    d += is_split(x)
                    before = x
                if x[0] == "MAX":
                    if x[2] == 0:
                        pe.wait_ge(slot_in[0], 16 * SLOT_DMAS)
                    maxima_piece(0, x[2], 0, done)
                    done += 1
                if x[0] == "MAXROW":
                    bank_free(before, q, d)
                    pe.wait_ge(m_ready, 1)
                    pe.transpose(psG[0:3 * GT, 0:P], maxima[:, :], ident[:, :]).then_inc(g_mm, 1)
                    before = x
            with pe.Fori(0, B * G) as n:
                q = d = done = u = heads = 0
                for x in plan:
                    kind = x[0]
                    if kind == "G" and x[1] != "chosen_o":
                        if x[1:] == PROJECT[0]:
                            pe.wait_ge(w_in, n * (16 * 6) + 2 * 16 * 6)
                        bank_free(before, n * NJ + (FJ + q), n * ND + (FD + d))
                        project(x)
                        q += 1
                        d += is_split(x)
                        before = x
                    elif kind == "G":
                        j = x[2]
                        pe.wait_ge(exp_done, n * NU + unit_of[(j, CHOSEN_KEYS, 0, HB - 1)] + 1)
                        bank_free(before, n * NJ + (FJ + q), n * ND + (FD + d))
                        for c in range(HB):
                            last = pe.matmul(psG[64 * c:64 * c + 64, :], VC[:, j, :], prob_c[:, c * BANK:(c + 1) * BANK],
                                             start=True, stop=True)
                        last.then_inc(g_mm, 1)
                        q += 1
                        before = x
                    elif kind == "MAXROW":
                        bank_free(before, n * NJ + (FJ + q), n * ND + (FD + d))
                        pe.wait_ge(m_ready, n * HG + heads + 2)
                        pe.transpose(psG[0:3 * GT, 0:P], maxima[:, :], ident[:, :]).then_inc(g_mm, 1)
                        q += 1
                        heads += 1
                        before = x
                    elif kind == "MAX":
                        if x[2] == 0:
                            pe.wait_ge(slot_in[x[1]], n * (16 * SLOT_DMAS) + (16 * SLOT_DMAS) * (2 if x[1] == 0 else 1))
                        maxima_piece(x[1], x[2], n * (HG * NM), NM + done)
                        done += 1
                    elif kind == "S":
                        _s, j, k, p, c = x
                        if k == LATENT_KEYS and p == 0 and c == 0:
                            pe.wait_ge(rows_in, n * (16 * HG) + 16 * (j + 1))
                        pe.wait_ge(exp_done, n * NU + (u + 1 - RING) if u >= RING else n * NU)
                        scores(j, k, p, c, u).then_inc(s_mm, 1)
                        u += 1
                    elif kind == "PV":
                        _p, j, p, c = x
                        if p == 0 and c == 0:
                            pe.wait_ge(o_out, n * HG + j)
                            pe.wait_ge(v_copied, n * (2 * HG) + 2 * (j + 1))
                        pe.wait_ge(exp_done, n * NU + unit_of[(j, WINDOW_KEYS, p, c)] + 1)
                        last = values(j, p, c)
                        if c == HB - 1:
                            last.then_inc(pv_mm, 1)


def project_out(nc, X, dram, s):
    with ExitStack() as ctx:
        def sb(n, shape, dt=F32):
            return ctx.enter_context(nc.sbuf_tensor("o_" + n, shape, dt))

        def sem(n):
            return nc.alloc_semaphore("o_" + n)

        wp, ws = sb("wp", [P, G, C]), sb("ws", [P, HL, G, C], F16)
        O = sb("O", [P, 2, G, HL, T], F16)
        ps = ctx.enter_context(nc.psum_tensor("o_ps", [P, 4, BANK], F32))
        loaded, x_in, hi, ready, summed, added = (sem(n) for n in ("loaded", "x_in", "hi", "ready", "summed", "added"))
        o_in = [sem(f"o_in{e}") for e in range(2)]
        block = ctx.enter_context(nc.Block())

        @block.sync
        def _(sp):
            sp.dma_start(wp[:, :, :], dram["w_proj"].rearrange("(g p) c -> p g c", p=P)).then_inc(loaded, 16)
            with sp.Fori(0, B // 2) as t:
                for e in range(2):
                    b = sp.snap(t * 2 + e)
                    sp.wait_ge(summed, t * (2 * GT))
                    sp.dma_start(O[:, e, :, :, :].rearrange("p g l t -> p g (l t)"),
                                 s["mixed"][1:B * G + 1].rearrange("(b g) p c -> b p g c", g=G)[bass.ds(b, 1)].rearrange("b p g c -> p (b g) c")).then_inc(o_in[e], 16)
            sp.wait_ge(added, NT)

        @block.gpsimd
        def _(pool):
            for b in range(B):
                pool.dma_start(X[:, b * GT:(b + 1) * GT, :],
                               s["x1"].rearrange("(i p) c -> p i c", p=P)[:, b * GT:(b + 1) * GT, :]).then_inc(x_in, 16)

        @block.scalar
        def _(act):
            act.wait_ge(loaded, 16)
            act.activation(ws[:, 0, :, :], wp[:, :, :], ACT.Copy, scale=WSC).then_inc(hi, 1)

        @block.vector
        def _(dve):
            dve.wait_ge(hi, 1)
            dve.scalar_tensor_tensor(ws[:, 1, :, :], wp[:, :, :], WSC, ws[:, 0, :, :], ALU.mult, ALU.subtract).then_inc(ready, 1)
            dve.wait_ge(x_in, 16 * B)
            with dve.Fori(0, B // 2) as t:
                for e in range(2):
                    for i in range(GT):
                        dve.wait_ge(summed, t * (2 * GT) + (e * GT + i + 1))
                        x = X[:, bass.ds((t * 2 + e) * GT + i, 1), :].rearrange("p a c -> p (a c)")
                        dve.scalar_tensor_tensor(x, ps[:, i % 4, 0:C], 1.0 / (QSC * WSC), x, ALU.mult, ALU.add).then_inc(added, 1)

        @block.tensor
        def _(pe):
            pe.wait_ge(ready, 1)
            with pe.Fori(0, B // 2) as t:
                for e in range(2):
                    pe.wait_ge(o_in[e], t * 16 + 16)
                    for i in range(GT):
                        m = e * GT + i - 3
                        pe.wait_ge(added, t * (2 * GT) + m if m > 0 else t * (2 * GT))
                        for g in range(G):
                            for a, b in PRODUCTS:
                                last = pe.matmul(ps[:, i % 4, 0:C], O[:, e, g, a, i * P:(i + 1) * P], ws[:, b, g, :],
                                                 start=(g == 0 and (a, b) == HIHI), stop=(g == G - 1 and (a, b) == LOHI))
                        last.then_inc(summed, 1)


def scratch():
    return [
        ("disp1", (SLOTS, C), F32), ("eout1", (SLOTS, C), F32), ("disp2", (SLOTS, C), F32), ("eout2", (SLOTS, C), F32),
        ("x1", (N, C), F32), ("xn", (N, C), F32), ("wsplit", (G, P, W_COLS), F16), ("xt", (B, P, CK * HL * T), F16),
        ("lat", (B, P, HL * T), F16), ("kr", (B, ROPE, HL * T), F16), ("sel", (B, P, CK * HL * KEEP), F16),
        ("score_n", (P, NT), F32), ("score_t", (N,), F32), ("rank_t", (N,), F32), ("gl", (P, B * 3), F32),
        ("gates", (B, P, 3), F32), ("mixed", (B * G + 1, P, HL * T), F16), ("sums", (3, HG, T), F32), ("inverses", (3, HG, T), F32),
    ]


def macaron_block(nc, x, out, dram, consts):
    s = {name: nc.dram_tensor("s_" + name, shape, dt).ap() for name, shape, dt in scratch()}
    dram = {**dram, **s}
    with nc.cleanup_on_exit(), nc.sbuf_tensor("X", [P, NT, C], F32) as X:
        ffn(nc, "1", X, dram, consts, x, s["x1"], beside=split_weights)
        latents(nc, X, dram, consts, s)
    with nc.cleanup_on_exit():
        select_tokens(nc, dram, consts, s)
        attention(nc, consts, s)
    with nc.cleanup_on_exit(), nc.sbuf_tensor("X2", [P, NT, C], F32) as X:
        project_out(nc, X, dram, s)
        ffn(nc, "2", X, dram, consts, None, out)


_INS = ["L0_attn_x", "L0_attn_w_cq", "L0_attn_g_qnorm", "L0_attn_w_dq_nope", "L0_attn_w_dq_rope", "L0_attn_w_ckv",
        "L0_attn_g_kvnorm", "L0_attn_w_dk_nope", "L0_attn_w_dv", "L0_attn_w_krope", "L0_attn_w_imp",
        "L0_attn_w_selk", "L0_attn_w_selv", "L0_attn_w_wink", "L0_attn_w_winv", "L0_attn_w_gate",
        "L0_attn_w_proj", "L0_ffn_Wr", "L0_ffn_W1", "L0_ffn_W2"]


def kernel(**inputs):
    import numpy as _np
    import concourse.bacc as _bacc
    from concourse import mybir as _mybir
    from concourse.bass_utils import run_bass_kernel_spmd as _run

    nc = _bacc.Bacc("TRN2", target_bir_lowering=False, num_devices=1)
    arrays, dram, consts = {}, {}, {}
    for name in _INS:
        a = _np.ascontiguousarray(inputs[name])
        arrays[f"in_{name}"] = a
        short = name.replace("L0_attn_", "").replace("L0_ffn_", "")
        dram[short] = nc.dram_tensor(f"in_{name}", a.shape, _mybir.dt.from_np(a.dtype), kind="ExternalInput").ap()
    for name, a in constants().items():
        arrays[name] = a
        consts[name] = nc.dram_tensor(name, a.shape, _mybir.dt.from_np(a.dtype), kind="ExternalInput").ap()
    out = nc.dram_tensor("out_0", (N, C), _mybir.dt.float32, kind="ExternalOutput").ap()
    x = dram["x"].rearrange("b t c -> (b t) c")
    macaron_block(nc, x, out, dram, consts)
    r = _run(nc, [arrays], core_ids=[0])
    return r.results[0]["out_0"].reshape(B, T, C)
```

```python
from contextlib import ExitStack

import numpy as np

import concourse.bass as bass
from concourse import mybir

F32 = mybir.dt.float32
F16 = mybir.dt.float16
I32 = mybir.dt.int32
ALU = mybir.AluOpType
ACT = mybir.ActivationFunctionType
AX = mybir.AxisListType.X

P = 128
B, T, C = 4, 1024, 256
N = B * T
NT = N // P
GT = T // P
CK = C // P
E, CAP, F = 8, 640, 1024
SLOTS = E * CAP
ST = CAP // P
FT = F // P
H, HG = 16, 4
G = H // HG
D, NOPE, ROPE, DV = 96, 32, 64, 32
HALF = ROPE // 2
QL, KL = 96, 32
KEEP = 64
LAT = QL + KL + ROPE + 1 + 3
LN_EPS, RMS_EPS = 1e-5, 1e-6
HL = 2

XSC, WSC, QSC = 16.0, 64.0, 16.0
FXSC = 4.0
SHIFT = 256.0
EXP_SCALE = 1.0 / (QSC * QSC * float(np.sqrt(D)))
HIHI, HILO, LOHI = (0, 0), (0, 1), (1, 0)
PRODUCTS = (HIHI, HILO, LOHI)

W_WIN, W_SEL = 0, HL * CK * 3 * P
W_WINV = 2 * HL * CK * 3 * P
W_SELV = W_WINV + HL * CK * P
W_Q = W_SELV + HL * CK * P
W_DK = W_Q + HL * 3 * P
W_DV = W_DK + HL * P
W_COLS = W_DV + HL * P


class Steps:

    def __init__(self, engine, sem, base=0):
        self.engine, self.sem, self.base, self.n = engine, sem, base, 0

    def done(self, ins):
        ins.then_inc(self.sem, 1)
        self.n += 1

    def wait(self):
        self.engine.wait_ge(self.sem, self.base + self.n)

    def one(self, ins):
        self.done(ins)
        self.wait()


def tile_of(X, i):
    return X[:, bass.ds(i, 1), :].rearrange("p a c -> p (a c)")


def batch_of(ap, b, order):
    return ap[bass.ds(b, 1)].rearrange(order)


def after(engine, sem, count):
    if not isinstance(count, int) or count > 0:
        engine.wait_ge(sem, count)


def bcast(ap, n):
    return ap.unsqueeze(2).broadcast_to([ap.shape[0], ap.shape[1], n])


def constants():
    ident = np.eye(P, dtype=np.float32)
    upto = np.triu(np.ones((P, P), np.float32))
    inv = (1.0 / np.power(10000.0, np.arange(0, ROPE, 2) / ROPE)).astype(np.float32)
    angle = np.outer(np.arange(T, dtype=np.float32), inv)
    cos, sin = np.cos(angle), np.sin(angle)
    big = (32768.0 * ident).astype(np.float16)
    later = np.arange(P)[:, None] < np.arange(P)[None, :]
    hide = np.where(later, -65504.0, 0.0).astype(np.float16)
    return {
        "c_ident": ident,
        "c_upto": upto,
        "c_expert": np.tile(np.arange(E, dtype=np.float32), (P, GT)),
        "c_keep": np.tile(np.arange(KEEP, dtype=np.float32), (P, 1)),
        "c_cosT": np.tile(cos.T, (HG, 1)).astype(np.float32),
        "c_sinT": np.tile(sin.T, (HG, 1)).astype(np.float32),
        "c_cos": cos.astype(np.float32),
        "c_sin": sin.astype(np.float32),
        "c_shift": np.stack([np.stack([np.full((HG, T), SHIFT if r == k else 0.0, np.float16) for r in range(3)])
                             for k in range(3)]),
        "c_mask": np.concatenate([big, hide], axis=1),
        "c_least": np.where(later.T, 0.0, 3.0e38).astype(np.float32),
    }


def normalize_batch(dve, b, stats_done, steps, eps_added, rstd_done, x_tiles, stats, moments, rstd, out, ready):
    for k in range(GT):
        dve.bn_stats(stats[:, k, :], x_tiles(k)).then_inc(stats_done, 1)
    dve.wait_ge(stats_done, b * GT + GT)
    mean, diff, squares = moments[:, 0, :], moments[:, 1, :], moments[:, 2, :]
    steps.done(dve.tensor_tensor(mean, stats[:, :, 1], stats[:, :, 4], ALU.add))
    steps.done(dve.tensor_tensor(diff, stats[:, :, 1], stats[:, :, 4], ALU.subtract))
    steps.one(dve.tensor_tensor(squares, stats[:, :, 2], stats[:, :, 5], ALU.add))
    steps.done(dve.tensor_scalar(mean, mean, 0.5, None, ALU.mult))
    steps.done(dve.tensor_scalar(squares, squares, 1.0 / C, LN_EPS, ALU.mult, ALU.add))
    steps.one(dve.scalar_tensor_tensor(diff, diff, 0.25, diff, ALU.mult, ALU.mult))
    dve.tensor_tensor(rstd[:, :], squares, diff, ALU.add).then_inc(eps_added, 1)
    dve.wait_ge(rstd_done, b + 1)
    for k in range(GT):
        ready(k, dve.tensor_scalar(out(k), x_tiles(k), mean[:, k:k + 1], rstd[:, k:k + 1],
                                   ALU.subtract, ALU.mult))


NORM_STEPS = 6


def inverse_deviation(pool, b, eps_added, rstd_done, rstd, minus_half):
    pool.wait_ge(eps_added, b + 1)
    pool.tensor_tensor(rstd[:, :], rstd[:, :], minus_half[:, 0:GT], ALU.pow).then_inc(rstd_done, 1)


def ffn(nc, name, X, dram, consts, xin, xout, beside=None):
    disp, eout = dram["disp" + name], dram["eout" + name]
    with ExitStack() as ctx:
        def sb(n, shape, dt=F32):
            return ctx.enter_context(nc.sbuf_tensor(name + n, shape, dt))

        XN = sb("XN", [P, NT, C])
        w_kept = sb("w_kept", [P, NT])
        w_lost = sb("w_lost", [P, NT])
        take = sb("take", [P, NT], I32)
        put = sb("put", [P, NT], I32)
        route_tokens(nc, name, X, XN, w_kept, w_lost, take, put, disp, dram, consts, xin)
        run_experts(nc, name, disp, eout, dram, consts)
        combine(nc, name, X, XN, w_kept, w_lost, take, dram, xout, beside)


def route_tokens(nc, name, X, XN, w_kept, w_lost, take, put, disp, dram, consts, xin):
    with ExitStack() as ctx:
        def sb(n, shape, dt=F32):
            return ctx.enter_context(nc.sbuf_tensor(name + n, shape, dt))

        def pb(n, shape, dt=F32):
            return ctx.enter_context(nc.psum_tensor(name + n, shape, dt))

        def sem(n):
            return nc.alloc_semaphore(name + n)

        ident, upto, ones, expert = (sb(n, s) for n, s in (
            ("ident", [P, P]), ("upto", [P, P]), ("ones", [P, P]), ("expert", [P, GT, E])))
        minus_half = sb("minus_half", [P, GT])
        half_set = sem("half_set")
        wr = sb("wr", [P, CK, E])
        zeros = sb("zeros", [P, 10 * C])
        stats, moments, rstd = sb("stats", [P, GT, 6]), sb("moments", [P, 3, GT]), sb("rstd", [P, GT])
        RING = 4
        XT = sb("XT", [P, RING, C])
        logit = sb("logit", [P, GT, E])
        top, sume, idx, used, kept, lost, slot, tmp = (sb(n, [P, GT]) for n in
                                                       ("top", "sume", "idx", "used", "kept", "lost", "slot", "tmp"))
        d8, e8, eq, cand, onehot, run, pos = (sb(n, [P, GT, E]) for n in
                                              ("d8", "e8", "eq", "cand", "onehot", "run", "pos"))
        base, total = sb("base", [P, E]), sb("total", [P, E])
        psT, psL = pb("psT", [P, RING, 512]), pb("psL", [P, 512])
        psC = pb("psC", [P, 2, GT, E])

        loaded, const_in, zeroed, zero_set, ones_set = (sem(n) for n in
                                              ("loaded", "const_in", "zeroed", "zero_set", "ones_set"))
        norm_ready, step, base_set = sem("norm_ready"), sem("step"), sem("base_set")
        stats_done, eps_added, rstd_done = (sem(n) for n in ("stats_done", "eps_added", "rstd_done"))
        turned, xt_ready, logits_mm, logits_out = (sem(n) for n in
                                                   ("turned", "xt_ready", "logits_mm", "logits_out"))
        shifted, expd, hot, counted, routed, sent = (sem(n) for n in
                                                     ("shifted", "expd", "hot", "counted", "routed", "sent"))
        slot_step = sem("slot_step")
        SLOT_STEPS = E + 19
        block = ctx.enter_context(nc.Block())

        @block.sync
        def _(sp):
            if xin is not None:
                for b in range(B):
                    sp.dma_start(X[:, b * GT:(b + 1) * GT, :],
                                 xin.rearrange("(i p) c -> p i c", p=P)[:, b * GT:(b + 1) * GT, :]).then_inc(loaded, 16)
            sp.dma_start(ident[:, :], consts["c_ident"]).then_inc(const_in, 16)
            sp.dma_start(upto[:, :], consts["c_upto"]).then_inc(const_in, 16)
            sp.dma_start(expert[:, :, :], consts["c_expert"].rearrange("p (i e) -> p i e", e=E)).then_inc(const_in, 16)
            sp.dma_start(wr[:, :, :], dram["Wr"].rearrange("(k p) e -> p k e", p=P)).then_inc(const_in, 16)
            sp.wait_ge(zero_set, 1)
            for q in range(SLOTS // (10 * P)):
                sp.dma_start(disp.rearrange("(q p i) c -> q p (i c)", p=P, i=10)[q], zeros[:, :]).then_inc(zeroed, 16)

        @block.gpsimd
        def _(pool):
            pool.memset(zeros[:, :], 0.0).then_inc(zero_set, 1)
            pool.memset(ones[:, :], 1.0).then_inc(ones_set, 1)
            pool.memset(base[:, :], 0.0).then_inc(base_set, 1)
            pool.memset(minus_half[:, :], -0.5).then_inc(half_set, 1)
            pool.wait_ge(half_set, 1)
            inverse_deviation(pool, 0, eps_added, rstd_done, rstd, minus_half)
            inverse_deviation(pool, 1, eps_added, rstd_done, rstd, minus_half)
            for b in range(B):
                if b == 0:
                    pool.wait_ge(zeroed, 16 * (SLOTS // (10 * P)))
                pool.wait_ge(routed, 2 * (b + 1))
                for i in range(b * GT, (b + 1) * GT):
                    if i == b * GT + 3 and b + 2 < B:
                        inverse_deviation(pool, b + 2, eps_added, rstd_done, rstd, minus_half)
                    pool.indirect_dma_start(
                        out=disp, out_offset=bass.IndirectOffsetOnAxis(ap=put[:, i:i + 1], axis=0),
                        in_=XN[:, i, :], in_offset=None, bounds_check=SLOTS - 1, oob_is_err=False).then_inc(sent, 16)
            pool.wait_ge(sent, 16 * NT)

        @block.vector
        def _(dve):
            def normalize(b):
                after(dve, norm_ready, b * GT)
                normalize_batch(dve, b, stats_done, Steps(dve, step, b * NORM_STEPS), eps_added, rstd_done,
                                lambda k: tile_of(X, b * GT + k), stats, moments, rstd,
                                lambda k: tile_of(XN, b * GT + k), lambda k, ins: ins.then_inc(norm_ready, 1))

            def find_slots(b):
                tiles = bass.ds(b * GT, GT)
                steps = Steps(dve, slot_step, b * SLOT_STEPS)
                dve.wait_ge(logits_out, b + 1)
                steps.one(dve.tensor_reduce(top[:, :], logit[:, :, :], AX, ALU.max))
                dve.tensor_tensor(d8[:, :, :], logit[:, :, :], bcast(top[:, :], E), ALU.subtract).then_inc(shifted, 1)
                dve.wait_ge(shifted, b + 1)
                steps.one(dve.tensor_scalar(eq[:, :, :], d8[:, :, :], 0.0, -float(E), ALU.is_ge, ALU.mult))
                steps.one(dve.scalar_tensor_tensor(cand[:, :, :], eq[:, :, :], float(E), expert[:, :, :], ALU.add, ALU.add))
                steps.one(dve.tensor_reduce(idx[:, :], cand[:, :, :], AX, ALU.min))
                dve.tensor_tensor(onehot[:, :, :], expert[:, :, :], bcast(idx[:, :], E), ALU.is_equal).then_inc(hot, 1)
                dve.wait_ge(expd, b + 1)
                steps.one(dve.tensor_reduce(sume[:, :], e8[:, :, :], AX, ALU.add))
                steps.one(dve.reciprocal(top[:, :], sume[:, :]))
                dve.wait_ge(counted, b + 1)
                for e in range(E):
                    steps.done(dve.tensor_tensor_scan(run[:, :, e], ones[:, 0:GT], psC[:, 1, :, e], 0.0, ALU.mult, ALU.add))
                steps.wait()
                steps.one(dve.tensor_copy(total[:, :], run[:, GT - 1, :]))
                steps.one(dve.tensor_tensor(run[:, :, :], run[:, :, :], psC[:, 1, :, :], ALU.subtract))
                steps.one(dve.tensor_tensor(run[:, :, :], run[:, :, :], psC[:, 0, :, :], ALU.add))
                steps.one(dve.tensor_tensor(run[:, :, :], run[:, :, :], base[:, :].unsqueeze(1).broadcast_to([P, GT, E]), ALU.add))
                steps.done(dve.tensor_tensor(base[:, :], base[:, :], total[:, :], ALU.add))
                steps.one(dve.tensor_tensor(pos[:, :, :], run[:, :, :], onehot[:, :, :], ALU.mult))
                steps.one(dve.tensor_reduce(used[:, :], pos[:, :, :], AX, ALU.add))
                steps.one(dve.tensor_scalar(kept[:, :], used[:, :], float(CAP), None, ALU.is_le))
                steps.done(dve.scalar_tensor_tensor(w_kept[:, tiles], top[:, :], 0.5, kept[:, :], ALU.mult, ALU.mult))
                steps.one(dve.tensor_scalar(lost[:, :], kept[:, :], -0.5, 0.5, ALU.mult, ALU.add))
                steps.done(dve.tensor_copy(w_lost[:, tiles], lost[:, :]))
                steps.one(dve.tensor_scalar(tmp[:, :], used[:, :], float(CAP), -1.0, ALU.min, ALU.add))
                steps.one(dve.scalar_tensor_tensor(slot[:, :], idx[:, :], float(CAP), tmp[:, :], ALU.mult, ALU.add))
                dve.tensor_copy(take[:, tiles], slot[:, :]).then_inc(routed, 1)
                dve.scalar_tensor_tensor(put[:, tiles], lost[:, :], float(4 * SLOTS), slot[:, :], ALU.mult, ALU.add).then_inc(routed, 1)
                assert steps.n == SLOT_STEPS, steps.n

            if xin is not None:
                dve.wait_ge(loaded, 16 * B)
            dve.wait_ge(const_in, 64)
            dve.wait_ge(base_set, 1)
            normalize(0)
            with dve.Fori(0, B - 1) as b:
                normalize(b + 1)
                find_slots(b)
            find_slots(B - 1)

        @block.scalar
        def _(act):
            def batch(b, middle):
                for k in range(GT):
                    after(act, turned, b * GT + (k + 1))
                    after(act, logits_mm, b * GT + (k - RING + 1) if k >= RING else b * GT)
                    act.activation(XT[:, k % RING, :], psT[:, k % RING, 0:C], ACT.Copy).then_inc(xt_ready, 1)
                    if k == 2:
                        middle()
                after(act, logits_mm, b * GT + GT)
                act.activation(logit[:, :, :].rearrange("p i e -> p (i e)"), psL[:, 0:GT * E], ACT.Copy).then_inc(logits_out, 1)

            def exponentials(b):
                after(act, shifted, b + 1)
                act.activation(e8[:, :, :], d8[:, :, :], ACT.Exp).then_inc(expd, 1)

            batch(0, lambda: None)
            with act.Fori(0, B - 1) as b:
                batch(b + 1, lambda: exponentials(b))
            exponentials(B - 1)

        @block.tensor
        def _(pe):
            pe.wait_ge(const_in, 64)
            pe.wait_ge(ones_set, 1)

            def turn(b, k):
                after(pe, norm_ready, b * GT + (k + 1))
                after(pe, xt_ready, b * GT + (k - RING + 1) if k >= RING else b * GT)
                for c in range(CK):
                    last = pe.transpose(psT[:, k % RING, c * P:(c + 1) * P],
                                        XN[:, b * GT + k, c * P:(c + 1) * P], ident[:, :])
                last.then_inc(turned, 1)

            def router(b, k):
                after(pe, xt_ready, b * GT + (k + 1))
                if k == 0:
                    after(pe, logits_out, b)
                for c in range(CK):
                    last = pe.matmul(psL[:, k * E:(k + 1) * E], XT[:, k % RING, c * P:(c + 1) * P], wr[:, c, :],
                                     start=(c == 0), stop=(c == CK - 1))
                last.then_inc(logits_mm, 1)

            def batch(b, middle):
                turn(b, 0)
                turn(b, 1)
                for k in range(GT):
                    if k + 2 < GT:
                        turn(b, k + 2)
                    router(b, k)
                    if k == 2:
                        middle()

            def count(b):
                after(pe, hot, b + 1)
                flat = onehot[:, :, :].rearrange("p i e -> p (i e)")
                pe.matmul(psC[:, 0, :, :].rearrange("p i e -> p (i e)"), upto[:, :], flat, start=True, stop=True)
                pe.matmul(psC[:, 1, :, :].rearrange("p i e -> p (i e)"), ones[:, :], flat, start=True, stop=True).then_inc(counted, 1)

            batch(0, lambda: None)
            for b in range(B - 1):
                batch(b + 1, lambda: count(b))
            count(B - 1)


def run_experts(nc, name, disp, eout, dram, consts):
    PAIR = 2
    with ExitStack() as ctx:
        def sb(n, shape, dt=F32):
            return ctx.enter_context(nc.sbuf_tensor(name + n, shape, dt))

        def pb(n, shape, dt=F32):
            return ctx.enter_context(nc.psum_tensor(name + n, shape, dt))

        def sem(n):
            return nc.alloc_semaphore(name + n)

        ident = sb("ident2", [P, P])
        rows = sb("rows", [P, PAIR, ST, C])
        w1, w2 = sb("w1", [P, PAIR, CK, F]), sb("w2", [P, PAIR, FT, C])
        w1s, w2s = sb("w1s", [P, PAIR, HL, CK, F], F16), sb("w2s", [P, PAIR, HL, FT, C], F16)
        xT = sb("xT", [P, PAIR, HL, CK, CAP], F16)
        hT = sb("hT", [P, PAIR, HL, FT, CAP], F16)
        res = sb("res", [P, PAIR, ST, C])
        psT = pb("psTe", [P, 2, 512])
        psH = pb("psH", [P, 2, 2, 512])
        psO = pb("psO", [P, 2, 512])
        HC = CAP // 2

        ident_in = sem("ident_in")
        rows_in = [sem(f"rows_in{e}") for e in range(PAIR)]
        w_in = [sem(f"w_in{e}") for e in range(PAIR)]
        w_hi, w_lo = sem("w_hi"), sem("w_lo")
        turned, x_hi, x_lo = sem("turned2"), sem("x_hi"), sem("x_lo")
        hidden, h_hi, h_lo = sem("hidden"), sem("h_hi"), sem("h_lo")
        summed, res_ready = sem("summed"), sem("res_ready")
        stored = [sem(f"stored{e}") for e in range(PAIR)]
        blocks = [(c, s) for c in range(CK) for s in range(ST)]
        jobs = [blocks[j:j + 4] for j in range(0, len(blocks), 4)]
        NJ = len(jobs)
        NW, WP = FT, CK * F // (FT // 2)
        block = ctx.enter_context(nc.Block())

        def weight_piece(q, buf):
            raw, split = ((w1, w1s), (w2, w2s))[q // (NW // 2)]
            cols = slice(q % (NW // 2) * WP, (q % (NW // 2) + 1) * WP)
            return (raw[:, buf].rearrange("p k n -> p (k n)")[:, cols],
                    split[:, buf, 0].rearrange("p k n -> p (k n)")[:, cols],
                    split[:, buf, 1].rearrange("p k n -> p (k n)")[:, cols])

        def turn_piece(j, buf):
            cols = slice(j * 4 * P, j * 4 * P + len(jobs[j]) * P)
            return (xT[:, buf, 0].rearrange("p k s -> p (k s)")[:, cols],
                    xT[:, buf, 1].rearrange("p k s -> p (k s)")[:, cols])

        @block.sync
        def _(sp):
            def load(x, e, turned_before, split_before):
                if turned_before is not None:
                    sp.wait_ge(turned, turned_before)
                sp.dma_start(rows[:, e, :, :],
                             disp.rearrange("(x s p) c -> x p s c", s=ST, p=P)[bass.ds(x, 1)].rearrange("x p s c -> p (x s) c")).then_inc(rows_in[e], 16)
                if split_before is not None:
                    sp.wait_ge(w_lo, split_before)
                sp.dma_start(w1[:, e, :, :], dram["W1"].rearrange("x (k p) f -> x p k f", p=P)[bass.ds(x, 1)].rearrange("x p k f -> p (x k) f")).then_inc(w_in[e], 16)
                sp.dma_start(w2[:, e, :, :], dram["W2"].rearrange("x (k p) c -> x p k c", p=P)[bass.ds(x, 1)].rearrange("x p k c -> p (x k) c")).then_inc(w_in[e], 16)

            sp.dma_start(ident[:, :], consts["c_ident"]).then_inc(ident_in, 16)
            load(0, 0, None, None)
            with sp.Fori(0, E // PAIR) as t:
                second, third = sp.snap(t * PAIR + 1), sp.snap((t * PAIR + 2) % E)
                load(second, 1, t * (PAIR * NJ), t * (PAIR * NW))
                load(third, 0, t * (PAIR * NJ) + NJ, t * (PAIR * NW) + NW)
            sp.wait_ge(rows_in[0], 16 * (E // PAIR + 1))
            sp.wait_ge(w_in[0], 32 * (E // PAIR + 1))

        @block.gpsimd
        def _(pool):
            with pool.Fori(0, E // PAIR) as t:
                for e in range(PAIR):
                    pool.wait_ge(res_ready, t * (PAIR * ST) + ST * (e + 1))
                    pool.dma_start(eout.rearrange("(x s p) c -> x p s c", s=ST, p=P)[bass.ds(t * PAIR + e, 1)].rearrange("x p s c -> p (x s) c"), res[:, e, :, :]).then_inc(stored[e], 16)
            for e in range(PAIR):
                pool.wait_ge(stored[e], 16 * (E // PAIR))

        @block.scalar
        def _(act):
            def split(q, buf):
                src, hi, _lo = weight_piece(q, buf)
                act.activation(hi, src, ACT.Copy, scale=WSC).then_inc(w_hi, 1)

            def turned_out(j, buf, bank, count):
                act.wait_ge(turned, count)
                act.activation(turn_piece(j, buf)[0], psT[:, bank, 0:len(jobs[j]) * P], ACT.Copy, scale=FXSC).then_inc(x_hi, 1)

            act.wait_ge(w_in[0], 32)
            for q in range(NW):
                split(q, 0)
            for j in range(NJ):
                turned_out(j, 0, j % 2, j + 1)
            with act.Fori(0, E // PAIR) as t:
                for e in range(PAIR):
                    nxt = (e + 1) % PAIR
                    act.wait_ge(w_in[nxt], t * 32 + (32 if nxt else 64))
                    act.wait_ge(summed, t * (PAIR * ST) + e * ST if e else t * (PAIR * ST))
                    for f in range(FT):
                        split(f, nxt)
                        act.wait_ge(hidden, t * (PAIR * FT) + (e * FT + f + 1))
                        act.activation(hT[:, e, 0, f, :].rearrange("p (n s) -> p n s", n=2), psH[:, f % 2, :, 0:HC],
                                       ACT.Relu).then_inc(h_hi, 1)
                    act.wait_ge(stored[e], t * 16)
                    for s in range(ST):
                        act.wait_ge(summed, t * (PAIR * ST) + (e * ST + s + 1))
                        act.activation(res[:, e, s, :], psO[:, (e * ST + s) % 2, 0:C], ACT.Copy,
                                       scale=1.0 / (FXSC * WSC * WSC)).then_inc(res_ready, 1)
                        if s < NJ:
                            n = (e + 1) * NJ + s
                            turned_out(s, nxt, n % 2, t * (PAIR * NJ) + (n + 1))

        @block.vector
        def _(dve):
            def split(q, buf, count):
                dve.wait_ge(w_hi, count)
                src, hi, lo = weight_piece(q, buf)
                dve.scalar_tensor_tensor(lo, src, WSC, hi, ALU.mult, ALU.subtract).then_inc(w_lo, 1)

            def turned_out(j, buf, bank, count):
                dve.wait_ge(x_hi, count)
                hi, lo = turn_piece(j, buf)
                dve.scalar_tensor_tensor(lo, psT[:, bank, 0:len(jobs[j]) * P], FXSC, hi, ALU.mult, ALU.subtract).then_inc(x_lo, 1)

            for q in range(NW):
                split(q, 0, q + 1)
            for j in range(NJ):
                turned_out(j, 0, j % 2, j + 1)
            with dve.Fori(0, E // PAIR) as t:
                for e in range(PAIR):
                    nxt = (e + 1) % PAIR
                    for f in range(FT):
                        split(f, nxt, t * (PAIR * NW) + ((e + 1) * NW + f + 1))
                        dve.wait_ge(h_hi, t * (PAIR * FT) + (e * FT + f + 1))
                        dve.scalar_tensor_tensor(hT[:, e, 1, f, :].rearrange("p (n s) -> p n s", n=2), psH[:, f % 2, :, 0:HC], 0.0,
                                                 hT[:, e, 0, f, :].rearrange("p (n s) -> p n s", n=2), ALU.max, ALU.subtract).then_inc(h_lo, 1)
                    for j in range(NJ):
                        n = (e + 1) * NJ + j
                        turned_out(j, nxt, n % 2, t * (PAIR * NJ) + (n + 1))

        @block.tensor
        def _(pe):
            pe.wait_ge(ident_in, 16)

            def turn(j, buf, bank, freed):
                if freed is not None:
                    pe.wait_ge(x_lo, freed)
                for q, (c, s) in enumerate(jobs[j]):
                    last = pe.transpose(psT[:, bank, q * P:(q + 1) * P], rows[:, buf, s, c * P:(c + 1) * P], ident[:, :])
                last.then_inc(turned, 1)

            pe.wait_ge(rows_in[0], 16)
            for j in range(NJ):
                turn(j, 0, j % 2, j - 1 if j > 1 else None)
            with pe.Fori(0, E // PAIR) as t:
                for e in range(PAIR):
                    nxt = (e + 1) % PAIR
                    pe.wait_ge(x_lo, t * (PAIR * NJ) + NJ * (e + 1))
                    pe.wait_ge(w_lo, t * (PAIR * NW) + NW * (e + 1))
                    for f in range(FT):
                        m = e * FT + f - 1
                        pe.wait_ge(h_lo, t * (PAIR * FT) + m if m > 0 else t * (PAIR * FT))
                        for c in range(CK):
                            for a, b in PRODUCTS:
                                for n in range(2):
                                    last = pe.matmul(psH[:, f % 2, n, 0:HC], w1s[:, e, a, c, f * P:(f + 1) * P],
                                                     xT[:, e, b, c, n * HC:(n + 1) * HC],
                                                     start=(c == 0 and (a, b) == HIHI),
                                                     stop=(c == CK - 1 and (a, b) == LOHI))
                        last.then_inc(hidden, 1)
                    for s in range(ST):
                        m = e * ST + s - 1
                        pe.wait_ge(res_ready, t * (PAIR * ST) + m if m > 0 else t * (PAIR * ST))
                        for f in range(FT):
                            if s == 0:
                                pe.wait_ge(h_lo, t * (PAIR * FT) + (FT * e + f + 1))
                            for a, b in PRODUCTS:
                                last = pe.matmul(psO[:, (e * ST + s) % 2, 0:C], hT[:, e, a, f, s * P:(s + 1) * P],
                                                 w2s[:, e, b, f, :], start=(f == 0 and (a, b) == HIHI),
                                                 stop=(f == FT - 1 and (a, b) == LOHI))
                        last.then_inc(summed, 1)
                        if s == 0:
                            pe.wait_ge(rows_in[nxt], t * 16 + (16 if nxt else 32))
                        if s < NJ:
                            n = (e + 1) * NJ + s
                            turn(s, nxt, n % 2, t * (PAIR * NJ) + (n - 1))


def combine(nc, name, X, XN, w_kept, w_lost, take, dram, xout, beside):
    with ExitStack() as ctx:
        R = ctx.enter_context(nc.sbuf_tensor(name + "R", [P, NT, C], F32))
        eout = dram["eout" + name]
        LOT = 4
        got = [nc.alloc_semaphore(f"{name}got{i}") for i in range(NT // LOT)]
        mixed, ready, stored = (nc.alloc_semaphore(name + n) for n in ("mixed", "ready", "xstored"))
        block = ctx.enter_context(nc.Block())

        @block.vector
        def _(dve):
            for i in range(NT):
                dve.scalar_tensor_tensor(X[:, i, :], XN[:, i, :], w_lost[:, i:i + 1], X[:, i, :], ALU.mult, ALU.add).then_inc(mixed, 1)

        if beside is not None:
            beside(nc, ctx, block, dram)

        @block.gpsimd
        def _(pool):
            for i in range(NT):
                pool.indirect_dma_start(
                    out=R[:, i, :], out_offset=None, in_=eout,
                    in_offset=bass.IndirectOffsetOnAxis(ap=take[:, i:i + 1], axis=0),
                    bounds_check=SLOTS - 1, oob_is_err=False).then_inc(got[i // LOT], 16)

        @block.vector
        def _(dve):
            for i in range(NT):
                if i % LOT == 0:
                    dve.wait_ge(got[i // LOT], 16 * LOT)
                dve.wait_ge(mixed, i + 1)
                dve.scalar_tensor_tensor(X[:, i, :], R[:, i, :], w_kept[:, i:i + 1], X[:, i, :], ALU.mult, ALU.add).then_inc(ready, 1)

        @block.sync
        def _(sp):
            for i in range(0, NT, LOT):
                sp.wait_ge(ready, i + LOT)
                sp.dma_start(xout.rearrange("(i p) c -> p i c", p=P)[:, i:i + LOT, :], X[:, i:i + LOT, :]).then_inc(stored, 16)
            sp.wait_ge(stored, 16 * (NT // LOT))


def split_weights(nc, ctx, block, dram):
    wsplit = dram["wsplit"]

    def sb(n, shape, dt=F32):
        return ctx.enter_context(nc.sbuf_tensor("ws_" + n, shape, dt))

    def sem(n):
        return nc.alloc_semaphore("ws_" + n)

    win, sel = sb("win", [P, CK, H * D]), sb("sel", [P, CK, H * D])
    winv, selv = sb("winv", [P, CK, H * DV]), sb("selv", [P, CK, H * DV])
    qn, qr = sb("qn", [QL, H * NOPE]), sb("qr", [QL, H * ROPE])
    dk, dv = sb("dk", [P, H * NOPE]), sb("dv", [P, H * DV])
    out = sb("out", [P, G, W_COLS], F16)
    loaded, hi_done, lo_done, stored = sem("loaded"), sem("hi_done"), sem("lo_done"), sem("stored")

    def pieces():
        for raw, at in ((win, W_WIN), (sel, W_SEL)):
            dst = out[:, :, at:at + HL * CK * 3 * P].rearrange(
                "p g (l k y h d) -> p g l k y h d", l=HL, k=CK, y=3, h=HG)
            src = raw[:, :, :].rearrange("p k (g h y d) -> p k g h y d", g=G, h=HG, y=3)
            for k in range(CK):
                for y in range(3):
                    yield src[:, k, :, :, y, :], dst[:, :, 0, k, y, :, :], dst[:, :, 1, k, y, :, :]
        for raw, at in ((winv, W_WINV), (selv, W_SELV)):
            dst = out[:, :, at:at + HL * CK * P].rearrange("p g (l k h d) -> p g l k h d", l=HL, k=CK, h=HG)
            src = raw[:, :, :].rearrange("p k (g h d) -> p k g h d", g=G, h=HG)
            for k in range(CK):
                yield src[:, k], dst[:, :, 0, k], dst[:, :, 1, k]
        dst = out[0:QL, :, W_Q:W_Q + HL * 3 * P].rearrange("p g (l y h d) -> p g l y h d", l=HL, y=3, h=HG)
        yield qn[:, :].rearrange("p (g h d) -> p g h d", g=G, h=HG), dst[:, :, 0, 0], dst[:, :, 1, 0]
        src = qr[:, :].rearrange("p (g h y d) -> p g h y d", g=G, h=HG, y=2)
        for y in range(2):
            yield src[:, :, :, y, :], dst[:, :, 0, 1 + y], dst[:, :, 1, 1 + y]
        for raw, at in ((dk, W_DK), (dv, W_DV)):
            dst = out[QL:P, :, at:at + HL * P].rearrange("p g (l h d) -> p g l h d", l=HL, h=HG)
            yield raw[QL:P, :].rearrange("p (g h d) -> p g h d", g=G, h=HG), dst[:, :, 0], dst[:, :, 1]

    @block.sync
    def _(sp):
        for dst, name in ((win, "w_wink"), (sel, "w_selk"), (winv, "w_winv"), (selv, "w_selv")):
            sp.dma_start(dst[:, :, :], dram[name].rearrange("(k p) n -> p k n", p=P)).then_inc(loaded, 16)
        sp.dma_start(qn[:, :], dram["w_dq_nope"]).then_inc(loaded, 16)
        sp.dma_start(qr[:, :], dram["w_dq_rope"]).then_inc(loaded, 16)
        sp.dma_start(dk[QL:P, :], dram["w_dk_nope"]).then_inc(loaded, 16)
        sp.dma_start(dv[QL:P, :], dram["w_dv"]).then_inc(loaded, 16)
        sp.wait_ge(lo_done, len(list(pieces())))
        for g in range(G):
            sp.dma_start(wsplit[g, :, 0:W_Q], out[:, g, 0:W_Q]).then_inc(stored, 16)
            sp.dma_start(wsplit[g, 0:QL, W_Q:W_DK], out[0:QL, g, W_Q:W_DK]).then_inc(stored, 16)
            sp.dma_start(wsplit[g, QL:P, W_DK:W_COLS], out[QL:P, g, W_DK:W_COLS]).then_inc(stored, 16)
        sp.wait_ge(stored, 3 * G * 16)

    @block.scalar
    def _(act):
        act.wait_ge(loaded, 8 * 16)
        for src, hi, _lo in pieces():
            act.activation(hi, src, ACT.Copy, scale=WSC).then_inc(hi_done, 1)

    @block.vector
    def _(dve):
        for n, (src, hi, lo) in enumerate(pieces()):
            dve.wait_ge(hi_done, n + 1)
            dve.scalar_tensor_tensor(lo, src, WSC, hi, ALU.mult, ALU.subtract).then_inc(lo_done, 1)


def latents(nc, X, dram, consts, s):
    with ExitStack() as ctx:
        def sb(n, shape, dt=F32):
            return ctx.enter_context(nc.sbuf_tensor("l_" + n, shape, dt))

        def pb(n, shape, dt=F32):
            return ctx.enter_context(nc.psum_tensor("l_" + n, shape, dt))

        def sem(n):
            return nc.alloc_semaphore("l_" + n)

        ident, mean_of = sb("ident", [P, P]), sb("mean_of", [P, P])
        minus_half = sb("minus_half", [P, 2 * GT])
        cos, sin = sb("cos", [P, GT, HALF]), sb("sin", [P, GT, HALF])
        gain = sb("gain", [P, 2])
        wlat = sb("wlat", [P, CK, LAT])
        stats, moments, rstd = sb("stats", [P, GT, 6]), sb("moments", [P, 3, GT]), sb("rstd", [P, GT])
        XS = sb("XS", [P, GT, C])
        XT = sb("XT", [P, 2, C])
        XB = sb("XB", [P, CK, HL, T], F16)
        lat = sb("lat", [P, GT, LAT])
        sq, ss = sb("sq", [P, GT, QL + KL]), sb("ss", [P, 2 * GT])
        nc_ = sb("normed", [P, GT, QL + KL + ROPE])
        rt = sb("rt", [P, 4, GT, HALF])
        NB, RB = sb("NB", [P, HL, T], F16), sb("RB", [ROPE, HL, T], F16)
        scores, gl = sb("scores", [P, NT]), sb("gl", [P, B, 3])
        psT, psL, psN, psG = pb("psT", [P, 2, 512]), pb("psL", [P, 2, 512]), pb("psN", [P, 2, 512]), pb("psG", [P, 512])

        const_in, set_, gained = sem("const_in"), sem("set"), sem("gained")
        stats_done, step, eps_added, rstd_done = sem("stats_done"), sem("step"), sem("eps_added"), sem("rstd_done")
        norm_ready, turned, xt_ready, x_hi, x_lo = (sem(n) for n in
                                                    ("norm_ready", "turned", "xt_ready", "x_hi", "x_lo"))
        lat_mm, lat_out, sums, rms = (sem(n) for n in ("lat_mm", "lat_out", "sums", "rms"))
        turned2, n_hi, n_lo, gate_mm, gate_out = (sem(n) for n in
                                                  ("turned2", "n_hi", "n_lo", "gate_mm", "gate_out"))
        score_out, stored_x, stored_n, stored_s = sem("score_out"), sem("stored_x"), sem("stored_n"), sem("stored_s")
        STEPS = NORM_STEPS + 12
        CONSTS = 10 * 16
        block = ctx.enter_context(nc.Block())

        @block.sync
        def _(sp):
            sp.dma_start(ident[:, :], consts["c_ident"]).then_inc(const_in, 16)
            sp.dma_start(cos[:, :, :], consts["c_cos"].rearrange("(i p) d -> p i d", p=P)).then_inc(const_in, 16)
            sp.dma_start(sin[:, :, :], consts["c_sin"].rearrange("(i p) d -> p i d", p=P)).then_inc(const_in, 16)
            sp.dma_start(gain[0:QL, 0:1], dram["g_qnorm"].rearrange("(p a) -> p a", a=1)).then_inc(const_in, 16)
            sp.dma_start(gain[QL:P, 0:1], dram["g_kvnorm"].rearrange("(p a) -> p a", a=1)).then_inc(const_in, 16)
            at = 0
            for name, n in (("w_cq", QL), ("w_ckv", KL), ("w_krope", ROPE), ("w_imp", 1), ("w_gate", 3)):
                sp.dma_start(wlat[:, :, at:at + n], dram[name].rearrange("(k p) n -> p k n", p=P),
                             allow_slow_non_contiguous=(n == 1)).then_inc(const_in, 16)
                at += n
            def store_norm(b):
                sp.wait_ge(norm_ready, b * GT + GT)
                sp.dma_start(batch_of(s["xn"].rearrange("(b i p) c -> b p i c", p=P, i=GT), b, "b p i c -> p (b i) c"), XS[:, :, :]).then_inc(stored_s, 16)

            def store_turned(b):
                sp.wait_ge(x_lo, b * GT + GT)
                sp.dma_start(batch_of(s["xt"], b, "b p n -> p (b n)"),
                             XB[:, :, :, :].rearrange("p k l t -> p (k l t)")).then_inc(stored_x, 16)

            def store_latents(b):
                sp.wait_ge(n_lo, b * (2 * GT) + 2 * GT)
                sp.dma_start(batch_of(s["kr"], b, "b p n -> p (b n)"),
                             RB[:, :, :].rearrange("p l t -> p (l t)")).then_inc(stored_n, 16)
                sp.dma_start(batch_of(s["lat"], b, "b p n -> p (b n)"),
                             NB[:, :, :].rearrange("p l t -> p (l t)")).then_inc(stored_n, 16)

            store_norm(0)
            store_turned(0)
            with sp.Fori(0, B - 1) as b:
                here, following = sp.snap(b + 0), sp.snap(b + 1)
                store_norm(following)
                store_latents(here)
                store_turned(following)
            store_latents(B - 1)
            sp.wait_ge(stored_x, 16 * B)
            sp.wait_ge(stored_n, 32 * B)
            sp.wait_ge(stored_s, 16 * B)
            sp.wait_ge(score_out, B)
            sp.wait_ge(gate_out, B)
            sp.dma_start(s["score_n"], scores[:, :]).then_inc(stored_x, 16)
            sp.dma_start(s["gl"], gl[:, :, :].rearrange("p b g -> p (b g)")).then_inc(stored_x, 16)
            sp.wait_ge(stored_x, 16 * B + 32)

        @block.gpsimd
        def _(pool):
            pool.memset(minus_half[:, :], -0.5).then_inc(set_, 1)
            pool.memset(mean_of[:, :], 1.0 / T).then_inc(set_, 1)
            pool.wait_ge(const_in, CONSTS)
            pool.tensor_scalar(gain[:, 1:2], gain[:, 0:1], XSC, None, ALU.mult).then_inc(gained, 1)
            pool.wait_ge(set_, 2)
            with pool.Fori(0, B) as b:
                inverse_deviation(pool, b, eps_added, rstd_done, rstd, minus_half)
                pool.wait_ge(sums, b + 1)
                pool.tensor_tensor(ss[:, :], ss[:, :], minus_half[:, :], ALU.pow).then_inc(rms, 1)

        @block.vector
        def _(dve):
            dve.wait_ge(const_in, CONSTS)
            dve.wait_ge(gained, 1)
            def normalize(b):
                after(dve, turned, b * GT)
                after(dve, stored_s, b * 16)
                normalize_batch(dve, b, stats_done, Steps(dve, step, b * STEPS), eps_added, rstd_done,
                                lambda k: tile_of(X, b * GT + k),
                                stats, moments, rstd, lambda k: XS[:, k, :], lambda k, ins: ins.then_inc(norm_ready, 1))

            def turned_lo(b, k):
                dve.wait_ge(x_hi, b * GT + (k + 1))
                dve.scalar_tensor_tensor(XB[:, :, 1, k * P:(k + 1) * P], psT[:, k % 2, 0:C].rearrange("p (k t) -> p k t", k=CK), XSC,
                                         XB[:, :, 0, k * P:(k + 1) * P], ALU.mult, ALU.subtract).then_inc(x_lo, 1)

            def latent_norms(b):
                steps = Steps(dve, step, b * STEPS + NORM_STEPS)
                dve.wait_ge(lat_out, b * GT + GT)
                steps.one(dve.tensor_tensor(sq[:, :, :], lat[:, :, 0:QL + KL], lat[:, :, 0:QL + KL], ALU.mult))
                steps.done(dve.tensor_reduce(ss[:, 0:GT], sq[:, :, 0:QL], AX, ALU.add))
                steps.one(dve.tensor_reduce(ss[:, GT:2 * GT], sq[:, :, QL:QL + KL], AX, ALU.add))
                steps.one(dve.tensor_scalar(ss[:, 0:GT], ss[:, 0:GT], 1.0 / QL, RMS_EPS, ALU.mult, ALU.add))
                dve.tensor_scalar(ss[:, GT:2 * GT], ss[:, GT:2 * GT], 1.0 / KL, RMS_EPS, ALU.mult, ALU.add).then_inc(sums, 1)
                x1, x2 = lat[:, :, QL + KL:QL + KL + HALF], lat[:, :, QL + KL + HALF:QL + KL + ROPE]
                for q, (a, m) in enumerate(((x1, cos), (x2, sin), (x1, sin), (x2, cos))):
                    steps.done(dve.scalar_tensor_tensor(rt[:, q, :, :], a, QSC / H, m[:, :, :], ALU.mult, ALU.mult))
                steps.wait()
                after(dve, turned2, b * (2 * GT))
                steps.done(dve.tensor_tensor(nc_[:, :, QL + KL:QL + KL + HALF], rt[:, 0, :, :], rt[:, 1, :, :], ALU.subtract))
                steps.done(dve.tensor_tensor(nc_[:, :, QL + KL + HALF:QL + KL + ROPE], rt[:, 2, :, :], rt[:, 3, :, :], ALU.add))
                dve.wait_ge(rms, b + 1)
                steps.done(dve.tensor_tensor(nc_[:, :, 0:QL], lat[:, :, 0:QL], bcast(ss[:, 0:GT], QL), ALU.mult))
                steps.one(dve.tensor_tensor(nc_[:, :, QL:QL + KL], lat[:, :, QL:QL + KL], bcast(ss[:, GT:2 * GT], KL), ALU.mult))
                dve.tensor_copy(scores[:, bass.ds(b * GT, GT)], lat[:, :, QL + KL + ROPE]).then_inc(score_out, 1)
                assert steps.n == STEPS - NORM_STEPS, steps.n

            def latents_lo(b, k):
                dve.wait_ge(n_hi, b * (2 * GT) + 2 * (k + 1))
                dve.scalar_tensor_tensor(NB[:, 1, k * P:(k + 1) * P], psN[:, k % 2, 0:P], gain[:, 1:2],
                                         NB[:, 0, k * P:(k + 1) * P], ALU.mult, ALU.subtract).then_inc(n_lo, 1)
                dve.tensor_tensor(RB[:, 1, k * P:(k + 1) * P], psN[0:ROPE, k % 2, P:2 * P],
                                  RB[:, 0, k * P:(k + 1) * P], ALU.subtract).then_inc(n_lo, 1)

            normalize(0)
            for k in range(GT):
                turned_lo(0, k)
            with dve.Fori(0, B - 1) as b:
                latent_norms(b)
                normalize(b + 1)
                for k in range(GT):
                    latents_lo(b, k)
                    turned_lo(b + 1, k)
            latent_norms(B - 1)
            for k in range(GT):
                latents_lo(B - 1, k)

        @block.scalar
        def _(act):
            act.wait_ge(gained, 1)
            def latent(b, k):
                act.wait_ge(lat_mm, b * GT + (k + 1))
                act.activation(lat[:, k, :], psL[:, k % 2, 0:LAT], ACT.Copy).then_inc(lat_out, 1)

            def batch(b, beside):
                after(act, stored_x, b * 16)
                after(act, score_out, b)
                after(act, gate_mm, b)
                for k in range(GT):
                    beside(k)
                    act.wait_ge(turned, b * GT + (k + 1))
                    act.activation(XT[:, k % 2, :], psT[:, k % 2, 0:C], ACT.Copy).then_inc(xt_ready, 1)
                    act.activation(XB[:, :, 0, k * P:(k + 1) * P], psT[:, k % 2, 0:C].rearrange("p (k t) -> p k t", k=CK),
                                   ACT.Copy, scale=XSC).then_inc(x_hi, 1)
                    if k:
                        latent(b, k - 1)
                latent(b, GT - 1)
                act.wait_ge(gate_mm, b + 1)
                act.activation(gl[:, bass.ds(b, 1), :].rearrange("p a g -> p (a g)"), psG[:, 0:3], ACT.Copy).then_inc(gate_out, 1)

            def latents_hi(b, k):
                if k == 0:
                    after(act, stored_n, b * 32)
                act.wait_ge(turned2, b * (2 * GT) + 2 * (k + 1))
                act.activation(NB[:, 0, k * P:(k + 1) * P], psN[:, k % 2, 0:P], ACT.Identity, scale=gain[:, 1:2]).then_inc(n_hi, 1)
                act.activation(RB[:, 0, k * P:(k + 1) * P], psN[0:ROPE, k % 2, P:2 * P], ACT.Copy).then_inc(n_hi, 1)

            batch(0, lambda k: None)
            with act.Fori(0, B - 1) as b:
                batch(b + 1, lambda k: latents_hi(b, k))
            for k in range(GT):
                latents_hi(B - 1, k)

        @block.tensor
        def _(pe):
            pe.wait_ge(const_in, CONSTS)
            pe.wait_ge(set_, 2)
            def turn(b, k):
                pe.wait_ge(norm_ready, b * GT + (k + 1))
                after(pe, x_lo, b * GT + (k - 1) if k > 1 else b * GT)
                after(pe, lat_mm, b * GT + (k - 1) if k > 1 else b * GT)
                for c in range(CK):
                    last = pe.transpose(psT[:, k % 2, c * P:(c + 1) * P], XS[:, k, c * P:(c + 1) * P], ident[:, :])
                last.then_inc(turned, 1)

            def product(b, k):
                pe.wait_ge(xt_ready, b * GT + (k + 1))
                after(pe, lat_out, b * GT + (k - 1) if k > 1 else b * GT)
                for c in range(CK):
                    last = pe.matmul(psL[:, k % 2, 0:LAT], XT[:, k % 2, c * P:(c + 1) * P], wlat[:, c, :],
                                     start=(c == 0), stop=(c == CK - 1))
                last.then_inc(lat_mm, 1)

            def batch(b, beside):
                turn(b, 0)
                for k in range(GT):
                    beside(k)
                    if k + 1 < GT:
                        turn(b, k + 1)
                    product(b, k)
                pe.wait_ge(lat_out, b * GT + GT)
                after(pe, gate_out, b)
                for k in range(GT):
                    last = pe.matmul(psG[:, 0:3], mean_of[:, :], lat[:, k, LAT - 3:LAT], start=(k == 0), stop=(k == GT - 1))
                last.then_inc(gate_mm, 1)

            def turn_latents(b, k):
                if k == 0:
                    pe.wait_ge(step, b * STEPS + STEPS)
                after(pe, n_lo, b * (2 * GT) + 2 * (k - 1) if k > 1 else b * (2 * GT))
                pe.transpose(psN[:, k % 2, 0:P], nc_[:, k, 0:P], ident[:, :]).then_inc(turned2, 1)
                pe.transpose(psN[0:ROPE, k % 2, P:2 * P], nc_[:, k, P:P + ROPE], ident[:, :]).then_inc(turned2, 1)

            batch(0, lambda k: None)
            with pe.Fori(0, B - 1) as b:
                batch(b + 1, lambda k: turn_latents(b, k))
            for k in range(GT):
                turn_latents(B - 1, k)


def select_tokens(nc, consts, s):
    with ExitStack() as ctx:
        def sb(n, shape, dt=F32):
            return ctx.enter_context(nc.sbuf_tensor("t_" + n, shape, dt))

        def pb(n, shape, dt=F32):
            return ctx.enter_context(nc.psum_tensor("t_" + n, shape, dt))

        def sem(n):
            return nc.alloc_semaphore("t_" + n)

        ident, keep = sb("ident", [P, P]), sb("keep", [P, KEEP])
        score_n, score_t = sb("score_n", [P, NT]), sb("score_t", [NT, P])
        score, left, chosen, rank = (sb(n, [B, T]) for n in ("score", "left", "chosen", "rank"))
        ones = sb("ones", [B, T])
        best = sb("best", [B, 8])
        rank_t, rank_n = sb("rank_t", [NT, P]), sb("rank_n", [P, NT])
        XN = sb("XN", [P, 2, GT, C])
        hot = sb("hot", [P, 2, GT, KEEP])
        SB = sb("SB", [P, 2, CK, HL, KEEP], F16)
        gl, ge, gs = sb("gl", [P, B, 3]), sb("ge", [P, B, 3]), sb("gs", [P, 2, B])
        ps1, ps2, psS = pb("ps1", [P, 512]), pb("ps2", [P, 512]), pb("psS", [P, 2, 512])
        const_in, turned, copied, moved, topped, step = (sem(n) for n in
                                                         ("const_in", "turned", "copied", "moved", "topped", "step"))
        shifted, expd, gated, gates_out = sem("shifted"), sem("expd"), sem("gated"), sem("gates_out")
        x_in = [sem(f"x_in{i}") for i in range(2)]
        hot_ready, picked, s_hi, s_lo = sem("hot_ready"), sem("picked"), sem("s_hi"), sem("s_lo")
        stored = [sem(f"stored{i}") for i in range(2)]
        block = ctx.enter_context(nc.Block())

        @block.sync
        def _(sp):
            sp.dma_start(ident[:, :], consts["c_ident"]).then_inc(const_in, 16)
            sp.dma_start(keep[:, :], consts["c_keep"]).then_inc(const_in, 16)
            sp.dma_start(score_n[:, :], s["score_n"]).then_inc(const_in, 16)
            sp.dma_start(gl[:, :, :].rearrange("p b g -> p (b g)"), s["gl"]).then_inc(const_in, 16)
            sp.wait_ge(copied, 1)
            sp.dma_start(s["score_t"].rearrange("(i p) -> i p", p=P), score_t[:, :]).then_inc(moved, 16)
            sp.wait_ge(moved, 16)
            sp.dma_start(score[:, :], s["score_t"].rearrange("(b t) -> b t", t=T)).then_inc(moved, 16)
            sp.wait_ge(topped, 1)
            sp.dma_start(s["rank_t"].rearrange("(b t) -> b t", t=T), rank[:, :]).then_inc(moved, 16)
            sp.wait_ge(moved, 48)
            sp.dma_start(rank_t[:, :], s["rank_t"].rearrange("(i p) -> i p", p=P)).then_inc(moved, 16)
            sp.wait_ge(gated, 1)
            sp.dma_start(s["gates"].rearrange("b p g -> p b g"), ge[:, :, :]).then_inc(gates_out, 16)
            with sp.Fori(0, B // 2) as t:
                for e in range(2):
                    b = sp.snap(t * 2 + e)
                    sp.wait_ge(picked, t * 2)
                    sp.dma_start(XN[:, e, :, :], s["xn"].rearrange("(b i p) c -> b p i c", p=P, i=GT)[bass.ds(b, 1)].rearrange("b p i c -> p (b i) c")).then_inc(x_in[e], 16)
                for e in range(2):
                    sp.wait_ge(s_lo, t * 2 + (e + 1))
                    sp.dma_start(s["sel"][bass.ds(t * 2 + e, 1)].rearrange("b p n -> p (b n)"),
                                 SB[:, e, :, :, :].rearrange("p k l t -> p (k l t)")).then_inc(stored[e], 16)
            for e in range(2):
                sp.wait_ge(stored[e], 16 * (B // 2))
            sp.wait_ge(gates_out, 16)

        @block.vector
        def _(dve):
            steps = Steps(dve, step)
            steps.done(dve.memset(ones[:, :], 1.0))
            dve.wait_ge(const_in, 64)
            steps.one(dve.tensor_reduce(gs[:, 0, :], gl[:, :, :], AX, ALU.max))
            dve.tensor_tensor(gl[:, :, :], gl[:, :, :], bcast(gs[:, 0, :], 3), ALU.subtract).then_inc(shifted, 1)
            dve.wait_ge(expd, 1)
            steps.one(dve.tensor_reduce(gs[:, 1, :], ge[:, :, :], AX, ALU.add))
            steps.one(dve.reciprocal(gs[:, 0, :], gs[:, 1, :]))
            dve.tensor_tensor(ge[:, :, :], ge[:, :, :], bcast(gs[:, 0, :], 3), ALU.mult).then_inc(gated, 1)
            dve.wait_ge(moved, 32)
            for r in range(KEEP // 8):
                src = score if r == 0 else left
                steps.one(dve.max(best[:, :], src[:, :]))
                steps.one(dve.match_replace(left[:, :], best[:, :], src[:, :], -3.0e38))
            steps.one(dve.tensor_tensor(chosen[:, :], score[:, :], left[:, :], ALU.not_equal))
            steps.one(dve.tensor_tensor_scan(rank[:, :], ones[:, :], chosen[:, :], 0.0, ALU.mult, ALU.add))
            steps.one(dve.tensor_tensor(rank[:, :], rank[:, :], chosen[:, :], ALU.mult))
            dve.tensor_scalar(rank[:, :], rank[:, :], 1.0, None, ALU.subtract).then_inc(topped, 1)
            with dve.Fori(0, B // 2) as t:
                dve.wait_ge(copied, 2)
                for e in range(2):
                    dve.wait_ge(picked, t * 2)
                    dve.tensor_tensor(hot[:, e, :, :], bcast(rank_n[:, bass.ds((t * 2 + e) * GT, GT)], KEEP),
                                      keep[:, :].unsqueeze(1).broadcast_to([P, GT, KEEP]), ALU.is_equal).then_inc(hot_ready, 1)
                for e in range(2):
                    dve.wait_ge(s_hi, t * 2 + (e + 1))
                    dve.scalar_tensor_tensor(SB[:, e, :, 1, :], psS[:, e, 0:CK * KEEP].rearrange("p (k t) -> p k t", k=CK),
                                             XSC, SB[:, e, :, 0, :], ALU.mult, ALU.subtract).then_inc(s_lo, 1)

        @block.scalar
        def _(act):
            act.wait_ge(turned, 1)
            act.activation(score_t[:, :], ps1[0:NT, 0:P], ACT.Copy).then_inc(copied, 1)
            act.wait_ge(shifted, 1)
            act.activation(ge[:, :, :], gl[:, :, :], ACT.Exp).then_inc(expd, 1)
            act.wait_ge(turned, 2)
            act.activation(rank_n[:, :], ps2[:, 0:NT], ACT.Copy).then_inc(copied, 1)
            with act.Fori(0, B // 2) as t:
                for e in range(2):
                    act.wait_ge(stored[e], t * 16)
                    act.wait_ge(picked, t * 2 + (e + 1))
                    act.activation(SB[:, e, :, 0, :], psS[:, e, 0:CK * KEEP].rearrange("p (k t) -> p k t", k=CK),
                                   ACT.Copy, scale=XSC).then_inc(s_hi, 1)

        @block.tensor
        def _(pe):
            pe.wait_ge(const_in, 64)
            pe.transpose(ps1[0:NT, 0:P], score_n[:, :], ident[:, :]).then_inc(turned, 1)
            pe.wait_ge(moved, 64)
            pe.transpose(ps2[:, 0:NT], rank_t[:, :], ident[0:NT, 0:NT]).then_inc(turned, 1)
            with pe.Fori(0, B // 2) as t:
                for e in range(2):
                    pe.wait_ge(x_in[e], t * 16 + 16)
                    pe.wait_ge(hot_ready, t * 2 + (e + 1))
                    pe.wait_ge(s_lo, t * 2)
                    for c in range(CK):
                        for k in range(GT):
                            last = pe.matmul(psS[:, e, c * KEEP:(c + 1) * KEEP], XN[:, e, k, c * P:(c + 1) * P], hot[:, e, k, :],
                                             start=(k == 0), stop=(k == GT - 1))
                    last.then_inc(picked, 1)


LATENT_KEYS, WINDOW_KEYS, CHOSEN_KEYS = 0, 1, 2
GATE = (0, 2, 1)
BANK = 512
HB = T // BANK
PROJECT = ([("v", k, c) for k in range(2) for c in range(HB)] + [("chosen_v",)]
           + [("plain", n, c) for n in ("k", "w", "q") for c in range(HB)] + [("chosen_k",)]
           + [("turn", n, c, y) for n in ("q", "w") for c in range(HB) for y in range(2)])
NEAR = PROJECT.index(("chosen_k",))
SPLIT = ("plain", "chosen_k")
MAXIMA = ([(k, i, c) for i in range(GT) for k in (LATENT_KEYS, WINDOW_KEYS) for c in range((i * P) // BANK + 1)]
          + [(CHOSEN_KEYS, 0, 0)])
NM = len(MAXIMA)
RING = 3
MAX_FROM, MAX_SHARE, ROW_AT = 0.0, 0.8, 0.86
JOBS_FROM, JOBS_TO = 0.1, 0.94
SR = 3 * HG * GT


def main_steps(j):
    steps = []
    for p in range(GT):
        first = (p * P) // BANK
        for k in (LATENT_KEYS, WINDOW_KEYS):
            for c in range(first, HB):
                w = (c + 1) * BANK - max(p * P, c * BANK)
                steps.append((("S", j, k, p, c), 3 * w))
        steps.append((("HIDE", j, p), 0))
        if p:
            for c in range(((p - 1) * P) // BANK, HB):
                w = (c + 1) * BANK - max((p - 1) * P, c * BANK)
                steps.append((("PV", j, p - 1, c), 5 * w))
    for c in range(HB):
        steps.append((("S", j, CHOSEN_KEYS, 0, c), 3 * BANK))
    steps.append((("PV", j, GT - 1, HB - 1), 5 * P))
    steps.append((("OUT", j), 0))
    return steps


def spread(fill, start, end):
    return [(start + (end - start) * (n + 0.5) / len(fill), f) for n, f in enumerate(fill)] if fill else []


def with_ropes(projections, apart):
    items, joins = [], []
    for g in projections:
        items.append(("G",) + g)
        joins = [(left - 1, join) for left, join in joins]
        items += [join for left, join in joins if left <= 0]
        joins = [x for x in joins if x[0] > 0]
        if (g[0] == "turn" and g[3] == 1) or g[0] == "chosen_k":
            rope = (g[1], g[2]) if g[0] == "turn" else ("chosen", 0)
            items.append(("ROPE",) + rope)
            if apart:
                joins.append((apart, ("JOIN",) + rope))
            else:
                items.append(("JOIN",) + rope)
    return items + [join for _, join in joins]


def group_plan():
    plan = []
    for j in range(HG):
        fill = spread([("MAX", (j + 1) % HG, n) for n in range(NM)], MAX_FROM, MAX_SHARE)
        fill += [(MAX_SHARE, ("MERGE", (j + 1) % HG)), (ROW_AT, ("MAXROW", (j + 1) % HG))]
        if j:
            fill += spread([("G", "chosen_o", j - 1)], 0.08, 0.1)
        if j == 0:
            fill += [(0.45, ("INVERT",)), (0.9, ("MIX",))]
            fill += spread([("G",) + g for g in PROJECT[:NEAR]], JOBS_FROM, JOBS_TO)
        elif j == 1:
            fill += spread(with_ropes(PROJECT[NEAR:], 1), JOBS_FROM, JOBS_TO)
        fill.sort(key=lambda f: f[0])
        main = main_steps(j)
        total = sum(w for _, w in main)
        at = 0
        for step, w in main:
            plan.append(step)
            at += w
            while fill and fill[0][0] * total <= at:
                plan.append(fill.pop(0)[1])
        plan += [f for _, f in fill]
    plan.append(("G", "chosen_o", HG - 1))
    return plan


def first_plan():
    return with_ropes(PROJECT, 0) + [("MAX", 0, n) for n in range(NM)] + [("MERGE", 0), ("MAXROW", 0)]


def general_jobs(plan):
    return [s for s in plan if s[0] in ("G", "MAXROW")]


def is_split(job):
    return job[0] == "G" and job[1] in SPLIT


rope_order = [(x[1], x[2]) for x in first_plan() if x[0] == "ROPE"]
rope_buf = {r: n % 2 for n, r in enumerate(rope_order)}


def job_index(plan):
    found = {}
    for n, x in enumerate(general_jobs(plan)):
        if x[:2] == ("G", "turn") and x[4] == 1:
            found[(x[2], x[3])] = n
        if x[:2] == ("G", "chosen_k"):
            found[("chosen", 0)] = n
    return found


first_turn, turn_job = job_index(first_plan()), job_index(group_plan())


def attention(nc, consts, s):
    with ExitStack() as ctx:
        def sb(n, shape, dt=F32):
            return ctx.enter_context(nc.sbuf_tensor("a_" + n, shape, dt))

        def pb(n, shape, dt=F32):
            return ctx.enter_context(nc.psum_tensor("a_" + n, shape, dt))

        def sem(n):
            return nc.alloc_semaphore("a_" + n)

        K99 = D + 3
        ident, mask, least = sb("ident", [P, P]), sb("mask", [P, 2, P], F16), sb("least", [P, P])
        cos, sin = sb("cos", [P, T]), sb("sin", [P, T])
        W = sb("W", [P, W_COLS], F16)
        XB, NB = sb("XB", [P, CK, HL, T], F16), sb("NB", [P, HL, T], F16)
        SB = sb("SB", [P, CK, HL, KEEP], F16)
        gates = sb("gates", [SR, 1])
        Qs, Ws, Ks = sb("Qs", [P, 3, HL, T], F16), sb("Ws", [P, 3, HL, T], F16), sb("Ks", [P, HL, T], F16)
        Cs = sb("Cs", [P, 3, HL, KEEP], F16)
        Vs, CVs = sb("Vs", [P, 2, GT, P]), sb("CVs", [KEEP, P])
        raw = sb("raw", [P, 2, 2, BANK])
        turned_, pool_t = sb("turned_", [P, 2, BANK]), sb("pool_t", [P, 2, BANK])
        Q, K1, KW = (sb(n, [K99, HG, HL, T], F16) for n in ("Q", "K1", "KW"))
        KC = sb("KC", [K99, HG, HL, KEEP], F16)
        V, VC = sb("V", [P, 2, HG, GT, 2 * DV]), sb("VC", [P, HG, 2 * DV])
        maxima, parts = sb("maxima", [P, 3 * GT]), sb("parts", [P, 2, HB, GT])
        max_rows = sb("max_rows", [3 * GT, P], F16)
        prob = sb("prob", [P, 2, 2, T])
        prob_c = sb("prob_c", [P, T])
        o_raw, oc_raw = sb("o_raw", [P, T]), sb("oc_raw", [P, BANK])
        o_val, o_inv = sb("o_val", [P, 3, T]), sb("o_inv", [P, 3, T])
        sums = sb("sums", [SR, P])
        mix, zero = sb("mix", [P, HL, T], F16), sb("zero", [P, 1])
        psS, psO = pb("psS", [P, RING, BANK]), pb("psO", [P, T])
        psM, psG = pb("psM", [P, 2, BANK]), pb("psG", [P, BANK])

        const_in, ones_set, w_in, gates_in = sem("const_in"), sem("ones_set"), sem("w_in"), sem("gates_in")
        g_mm, g_act, g_dve = sem("g_mm"), sem("g_act"), sem("g_dve")
        r_step, r_pool, roped = sem("r_step"), sem("r_pool"), sem("roped")
        slot_in = [sem(f"slot_in{j}") for j in range(HG)]
        m_mm, m_red, m_ready, rows_in = (sem(n) for n in ("m_mm", "m_red", "m_ready", "rows_in"))
        s_mm, exp_done, hidden, pv_mm = sem("s_mm"), sem("exp_done"), sem("hidden"), sem("pv_mm")
        v_copied, o_out, o_moved = sem("v_copied"), sem("o_out"), sem("o_moved")
        oc_moved = sem("oc_moved")
        sums_in, inverse, inverse_out, inverse_in = (sem(n) for n in ("sums_in", "inverse", "inverse_out", "inverse_in"))
        weighed, mix_done, mix_stored = (sem(n) for n in ("weighed", "mix_done", "mix_stored"))
        p_step, set_, set_sums, inverted = sem("p_step"), sem("set"), sem("set_sums"), sem("inverted")
        CONSTS = 16 * (5 + 3)

        plan, first = group_plan(), first_plan()
        jobs, first_jobs = general_jobs(plan), general_jobs(first)
        NJ, FJ = len(jobs), len(first_jobs)
        ND, FD = sum(map(is_split, jobs)), sum(map(is_split, first_jobs))
        NR = sum(1 for x in plan if x[0] == "ROPE")
        units = [x for x in plan if x[0] == "S"]
        unit_of = {x[1:]: n for n, x in enumerate(units)}
        NU = len(units)
        NPV = HG * GT
        SLOT_DMAS = 3 + 3 + 3 + 2

        row_jobs = [n + 1 for n, x in enumerate(jobs) if x[0] == "MAXROW"]

        def chosen_o_job(j):
            return jobs.index(("G", "chosen_o", j)) + 1

        def weights(at, rows, *dims):
            n = int(np.prod(dims)) * P
            lo = 0 if rows != KL else QL
            ap = W[lo:lo + rows, at:at + n]
            names = " ".join("abc"[:len(dims)])
            return ap.rearrange(f"p ({names} m) -> p {names} m", **dict(zip("abc", dims)))

        w_win, w_sel = weights(W_WIN, P, HL, CK, 3), weights(W_SEL, P, HL, CK, 3)
        w_winv, w_selv = weights(W_WINV, P, HL, CK), weights(W_SELV, P, HL, CK)
        w_q, w_dk, w_dv = weights(W_Q, QL, HL, 3), weights(W_DK, KL, HL), weights(W_DV, KL, HL)

        def mix_group(engine, n):
            engine.wait_ge(inverse_in, n * 48 + 48)
            for k in range(3):
                engine.tensor_tensor(o_val[:, k, :], o_val[:, k, :], o_inv[:, k, :], ALU.mult).then_inc(weighed, 1)
            engine.wait_ge(weighed, n * 5 + 3)
            engine.tensor_tensor(o_val[:, 0, :], o_val[:, 0, :], o_val[:, 1, :], ALU.add).then_inc(weighed, 1)
            engine.wait_ge(weighed, n * 5 + 4)
            engine.tensor_tensor(o_val[:, 0, :], o_val[:, 0, :], o_val[:, 2, :], ALU.add).then_inc(weighed, 1)
            engine.wait_ge(weighed, n * 5 + 5)
            engine.wait_ge(mix_stored, n * 16)
            engine.tensor_tensor(mix[:, 0, :], o_val[:, 0, :], zero[:, :].broadcast_to([P, T]), ALU.add).then_inc(mix_done, 1)
            engine.wait_ge(mix_done, n * 2 + 1)
            engine.tensor_tensor(mix[:, 1, :], o_val[:, 0, :], mix[:, 0, :], ALU.subtract).then_inc(mix_done, 1)

        block = ctx.enter_context(nc.Block())

        @block.sync
        def _(sp):
            sp.dma_start(ident[:, :], consts["c_ident"]).then_inc(const_in, 16)
            sp.dma_start(mask[:, :, :], consts["c_mask"].rearrange("p (a q) -> p a q", a=2)).then_inc(const_in, 16)
            sp.dma_start(least[:, :], consts["c_least"]).then_inc(const_in, 16)
            sp.dma_start(cos[:, :], consts["c_cosT"]).then_inc(const_in, 16)
            sp.dma_start(sin[:, :], consts["c_sinT"]).then_inc(const_in, 16)
            for k, dst in enumerate((K1, KW, KC)):
                n = dst.shape[3]
                sp.dma_start(dst[D:K99, :, 0, :], consts["c_shift"][k][:, :, 0:n]).then_inc(const_in, 16)

            def load(m):
                g, b = sp.snap(m % G), sp.snap(m // G)
                sp.dma_start(W[:, 0:W_Q], s["wsplit"][bass.ds(g, 1), :, 0:W_Q].rearrange("g p n -> p (g n)")).then_inc(w_in, 16)
                sp.dma_start(W[0:QL, W_Q:W_DK], s["wsplit"][bass.ds(g, 1), 0:QL, W_Q:W_DK].rearrange("g p n -> p (g n)")).then_inc(w_in, 16)
                sp.dma_start(W[QL:P, W_DK:W_COLS], s["wsplit"][bass.ds(g, 1), QL:P, W_DK:W_COLS].rearrange("g p n -> p (g n)")).then_inc(w_in, 16)
                sp.dma_start(XB[:, :, :, :].rearrange("p k l t -> p (k l t)"), s["xt"][bass.ds(b, 1)].rearrange("b p n -> p (b n)")).then_inc(w_in, 16)
                sp.dma_start(NB[:, :, :].rearrange("p l t -> p (l t)"), s["lat"][bass.ds(b, 1)].rearrange("b p n -> p (b n)")).then_inc(w_in, 16)
                sp.dma_start(SB[:, :, :, :].rearrange("p k l t -> p (k l t)"), s["sel"][bass.ds(b, 1)].rearrange("b p n -> p (b n)")).then_inc(w_in, 16)

            def repack(j, b):
                rows = slice(j * NOPE, (j + 1) * NOPE)
                for stage, slot in ((Qs, Q), (Ws, KW), (Cs, KC)):
                    for y in range(3):
                        sp.dma_start(slot[y * NOPE:(y + 1) * NOPE, j, :, :], stage[rows, y, :, :]).then_inc(slot_in[j], 16)
                sp.dma_start(K1[0:NOPE, j, :, :], Ks[rows, :, :]).then_inc(slot_in[j], 16)
                sp.dma_start(K1[NOPE:D, j, :, :].rearrange("p l t -> p (l t)"),
                             s["kr"][bass.ds(b, 1)].rearrange("b p n -> p (b n)")).then_inc(slot_in[j], 16)

            def move_out(n, j):
                rows = slice(j * DV, (j + 1) * DV)
                sp.wait_ge(o_out, n * HG + (j + 1))
                for k in range(2):
                    sp.dma_start(o_val[rows, k, :], o_raw[64 * k:64 * k + DV, :]).then_inc(o_moved, 16)
                    sp.dma_start(s["sums"][GATE[k], j:j + 1, :], o_raw[64 * k + DV:64 * k + DV + 1, :]).then_inc(o_moved, 16)

            def move_chosen(job, j):
                rows = slice(j * DV, (j + 1) * DV)
                sp.wait_ge(g_act, job)
                for c in range(HB):
                    cols = slice(c * BANK, (c + 1) * BANK)
                    sp.dma_start(o_val[rows, 2, cols], oc_raw[64 * c:64 * c + DV, :]).then_inc(oc_moved, 16)
                    sp.dma_start(s["sums"][GATE[CHOSEN_KEYS], j:j + 1, cols], oc_raw[64 * c + DV:64 * c + DV + 1, :]).then_inc(oc_moved, 16)

            def staged(m):
                split_all, roped_all = m * ND + ND, m * NR + NR
                if not isinstance(m, int):
                    split_all, roped_all = sp.snap(split_all), sp.snap(roped_all)
                sp.wait_ge(g_dve, split_all)
                sp.wait_ge(roped, roped_all)

            def store_mix(n):
                sp.wait_ge(mix_done, n * 2 + 2)
                row = s["mixed"][n] if isinstance(n, int) else s["mixed"][bass.ds(n, 1)].rearrange("n p c -> p (n c)")
                sp.dma_start(row, mix[:, :, :].rearrange("p l t -> p (l t)")).then_inc(mix_stored, 16)

            def turn_sums(moved, earlier, used):
                sp.wait_ge(o_moved, moved)
                sp.wait_ge(oc_moved, moved)
                sp.dma_start(sums[:, :], s["sums"].rearrange("k h (c t) -> (k h c) t", t=P)).then_inc(sums_in, 16)
                sp.wait_ge(inverse, earlier + 1)
                sp.dma_start(s["inverses"].rearrange("k h (c t) -> (k h c) t", t=P), sums[:, :]).then_inc(inverse_out, 16)
                sp.wait_ge(weighed, used)
                sp.wait_ge(inverse_out, earlier * 16 + 16)
                for k in range(3):
                    sp.dma_start(o_inv[:, k, :], s["inverses"][GATE[k]].unsqueeze(1).broadcast_to([HG, DV, T])).then_inc(inverse_in, 16)

            sp.wait_ge(set_sums, 1)
            sp.dma_start(s["sums"].rearrange("k h (c t) -> (k h c) t", t=P), sums[:, :]).then_inc(sums_in, 16)
            sp.wait_ge(sums_in, 16)
            load(0)
            staged(0)
            for j in range(HG):
                repack(j, 0)
            load(1)
            with sp.Fori(0, B * G) as n:
                nxt = sp.snap((n + 1) % (B * G))
                after = sp.snap((n + 2) % (B * G))
                here, next_batch = sp.snap(n + 0), sp.snap(nxt // G)
                batch = sp.snap(((n + (B * G - 1)) % (B * G)) // G)
                moved, used = sp.snap(here * (64 * HG)), sp.snap(here * 5)
                sp.dma_start(gates[:, :], s["gates"][bass.ds(batch, 1), 0:HG * GT, :].rearrange("b p g -> (b g) p").unsqueeze(2),
                             allow_slow_non_contiguous=True).then_inc(gates_in, 16)
                turn_sums(moved, here, used)
                store_mix(here)
                move_out(here, 0)
                move_chosen(here * NJ + (FJ + chosen_o_job(0)), 0)
                staged(here + 1)
                for j in range(HG):
                    scored = sp.snap(here * NU + (unit_of[(j, CHOSEN_KEYS, 0, HB - 1)] + 1))
                    chosen_out = sp.snap(here * NJ + (FJ + chosen_o_job(j)))
                    if j:
                        move_out(here, j)
                        move_chosen(chosen_out, j)
                    sp.wait_ge(s_mm, scored)
                    repack(j, next_batch)
                    if j == 0:
                        load(after)
            sp.dma_start(gates[:, :], s["gates"][B - 1, 0:HG * GT, :].rearrange("p g -> g p").unsqueeze(2), allow_slow_non_contiguous=True).then_inc(gates_in, 16)
            turn_sums(B * G * 64 * HG, B * G, B * G * 5)
            store_mix(B * G)
            sp.wait_ge(mix_stored, 16 * (B * G + 1))
            sp.wait_ge(w_in, 16 * 6 * (B * G + 2))
            for j in range(HG):
                sp.wait_ge(slot_in[j], 16 * SLOT_DMAS * (B * G + 1))
            sp.wait_ge(rows_in, 16 * (B * G * HG + 1))

        @block.gpsimd
        def _(pool):
            ones = Steps(pool, ones_set)
            ones.one(pool.memset(V[:, :, :, :, :].rearrange("p k j i d -> p (k j i) d")[:, :, DV:2 * DV], 1.0))
            ones.one(pool.memset(VC[0:KEEP, :, DV:2 * DV], 1.0))
            ones.one(pool.memset(VC[KEEP:P, :, :], 0.0))
            ones.one(pool.memset(prob_c[KEEP:P, :], 0.0))
            pool.wait_ge(const_in, CONSTS)
            pool.wait_ge(ones_set, 4)
            zeros = Steps(pool, set_)
            zeros.one(pool.memset(o_val[:, :, :], 0.0))
            zeros.one(pool.memset(zero[:, :], 0.0))

            def rope(count, name, c, r):
                n = KEEP if name == "chosen" else BANK
                job = first_turn[(name, c)] if r is None else turn_job[(name, c)]
                base = 0 if r is None else FJ
                pool.wait_ge(g_act, (0 if r is None else r * NJ) + (base + job + 1))
                pool.wait_ge(roped, count)
                buf = rope_buf[(name, c)]
                cs, sn = cos[:, c * BANK:c * BANK + n], sin[:, c * BANK:c * BANK + n]
                pool.tensor_tensor(pool_t[:, 0, 0:n], raw[:, buf, 0, 0:n], sn, ALU.mult).then_inc(p_step, 1)
                pool.tensor_tensor(pool_t[:, 1, 0:n], raw[:, buf, 1, 0:n], cs, ALU.mult).then_inc(p_step, 1)
                pool.wait_ge(p_step, count * 2 + 2)
                pool.tensor_tensor(pool_t[:, 0, 0:n], pool_t[:, 0, 0:n], pool_t[:, 1, 0:n], ALU.add).then_inc(r_pool, 1)

            def copy_values(j):
                cols = slice(j * DV, (j + 1) * DV)
                pool.tensor_tensor(VC[0:KEEP, j, 0:DV], CVs[:, cols], zero[0:KEEP, :].broadcast_to([KEEP, DV]), ALU.add).then_inc(v_copied, 1)
                pool.tensor_copy(V[:, :, j, :, 0:DV], Vs[:, :, :, cols]).then_inc(v_copied, 1)

            r = 0
            for x in first:
                if x[0] == "ROPE":
                    rope(r, x[1], x[2], None)
                    r += 1
            for j in range(HG):
                copy_values(j)
            with pool.Fori(0, B * G) as n:
                r = 0
                for x in plan:
                    if x[0] == "ROPE":
                        rope(n * NR + (NR + r), x[1], x[2], n)
                        r += 1
                    if x[0] == "MIX":
                        mix_group(pool, n)
                    if x == ("OUT", 1):
                        pool.wait_ge(g_act, n * NJ + (FJ + chosen_o_job(0)))
                        copy_values(0)
                for j in range(1, HG):
                    pool.wait_ge(pv_mm, n * NPV + (j + 1) * GT)
                    pool.wait_ge(g_act, n * NJ + (FJ + chosen_o_job(j)))
                    copy_values(j)

        @block.vector
        def _(dve):
            dve.wait_ge(const_in, CONSTS)

            def split_job(job, index, m):
                dve.wait_ge(g_act, index)
                scale = QSC / (XSC * WSC)
                if job[1] == "plain":
                    stage = {"q": Qs[:, 0], "w": Ws[:, 0], "k": Ks[:, :, :]}[job[2]]
                    cols = slice(job[3] * BANK, (job[3] + 1) * BANK)
                    dve.scalar_tensor_tensor(stage[:, 1, cols], psG[:, :], scale, stage[:, 0, cols],
                                             ALU.mult, ALU.subtract).then_inc(g_dve, 1)
                else:
                    dve.scalar_tensor_tensor(Cs[:, 0, 1, :], psG[:, 0:KEEP], scale, Cs[:, 0, 0, :],
                                             ALU.mult, ALU.subtract).then_inc(g_dve, 1)

            def rope(count, name, c):
                n = KEEP if name == "chosen" else BANK
                stage = {"q": Qs, "w": Ws, "chosen": Cs}[name]
                cols = slice(c * BANK, c * BANK + n)
                buf = rope_buf[(name, c)]
                steps = Steps(dve, r_step, count * 6)
                steps.wait()
                steps.done(dve.tensor_tensor(turned_[:, 0, 0:n], raw[:, buf, 0, 0:n], cos[:, c * BANK:c * BANK + n], ALU.mult))
                steps.one(dve.tensor_tensor(turned_[:, 1, 0:n], raw[:, buf, 1, 0:n], sin[:, c * BANK:c * BANK + n], ALU.mult))
                steps.one(dve.tensor_tensor(turned_[:, 0, 0:n], turned_[:, 0, 0:n], turned_[:, 1, 0:n], ALU.subtract))
                steps.one(dve.tensor_copy(stage[:, 1, 0, cols], turned_[:, 0, 0:n]))
                steps.done(dve.tensor_tensor(stage[:, 1, 1, cols], turned_[:, 0, 0:n], stage[:, 1, 0, cols], ALU.subtract))

            def join(count, name, c):
                n = KEEP if name == "chosen" else BANK
                stage = {"q": Qs, "w": Ws, "chosen": Cs}[name]
                cols = slice(c * BANK, c * BANK + n)
                steps = Steps(dve, r_step, count * 6 + 5)
                dve.wait_ge(r_pool, count + 1)
                steps.one(dve.tensor_copy(stage[:, 2, 0, cols], pool_t[:, 0, 0:n]))
                dve.tensor_tensor(stage[:, 2, 1, cols], pool_t[:, 0, 0:n], stage[:, 2, 0, cols], ALU.subtract).then_inc(roped, 1)

            def maxima_piece(turns, before, n):
                k, i, c = MAXIMA[n]
                dve.wait_ge(m_mm, turns + (before + 1))
                if k == CHOSEN_KEYS:
                    ins = dve.tensor_reduce(maxima[:, 2 * GT:3 * GT], psM[:, before % 2, :].rearrange("p (i k) -> p i k", k=KEEP), AX, ALU.max)
                else:
                    w = min((i + 1) * P - c * BANK, BANK)
                    ins = dve.tensor_reduce(parts[:, k, c, i:i + 1], psM[:, before % 2, 0:w], AX, ALU.max)
                ins.then_inc(m_red, 1)

            def merge(done):
                dve.wait_ge(m_red, done)
                dve.tensor_reduce(maxima[:, 0:2 * GT].rearrange("p (k i) -> p k i", k=2),
                                  parts[:, :, :, :].rearrange("p k c i -> p k i c"), AX, ALU.max).then_inc(m_ready, 1)

            def invert(n):
                dve.wait_ge(sums_in, n * 16 + 32)
                dve.wait_ge(gates_in, n * 16 + 16)
                steps = Steps(dve, inverted, n)
                steps.one(dve.reciprocal(sums[:, :], sums[:, :]))
                dve.tensor_scalar(sums[:, :], sums[:, :], gates[:, 0:1], QSC, ALU.mult, ALU.mult).then_inc(inverse, 1)

            dve.memset(sums[:, :], 1.0).then_inc(set_sums, 1)
            dve.memset(parts[:, :, :, :], -3.0e38).then_inc(set_sums, 1)
            dve.wait_ge(set_sums, 2)
            done, q = 0, 0
            r = 0
            for x in first:
                if x[0] in ("G", "MAXROW"):
                    q += 1
                if is_split(x):
                    split_job(x, q, 0)
                if x[0] == "ROPE":
                    dve.wait_ge(g_act, first_turn[(x[1], x[2])] + 1)
                    rope(r, x[1], x[2])
                if x[0] == "JOIN":
                    join(r, x[1], x[2])
                    r += 1
                if x[0] == "MAX":
                    maxima_piece(0, done, x[2])
                    done += 1
                if x[0] == "MERGE":
                    merge(done)
            with dve.Fori(0, B * G) as n:
                done, q, r, heads = 0, 0, 0, 0
                for x in plan:
                    if x[0] in ("G", "MAXROW"):
                        q += 1
                    if is_split(x):
                        split_job(x, n * NJ + (FJ + q), n)
                    if x[0] == "OUT":
                        j = x[1]
                        dve.wait_ge(pv_mm, n * NPV + (j + 1) * GT)
                        dve.wait_ge(o_moved, n * (64 * HG) + 64 * j)
                        dve.tensor_copy(o_raw[:, :], psO[:, :]).then_inc(o_out, 1)
                    if x[0] == "HIDE":
                        j, p = x[1], x[2]
                        dve.wait_ge(exp_done, n * NU + unit_of[(j, WINDOW_KEYS, p, (p * P) // BANK)] + 1)
                        corner = prob[:, (j * GT + p) % 2, :, p * P:(p + 1) * P]
                        dve.tensor_tensor(corner, corner, least[:, :].unsqueeze(1).broadcast_to([P, 2, P]), ALU.min).then_inc(hidden, 1)
                    if x[0] == "INVERT":
                        invert(n)
                    if x[0] == "ROPE":
                        dve.wait_ge(g_act, n * NJ + (FJ + turn_job[(x[1], x[2])] + 1))
                        rope(n * NR + (NR + r), x[1], x[2])
                    if x[0] == "JOIN":
                        join(n * NR + (NR + r), x[1], x[2])
                        r += 1
                    if x[0] == "MAX":
                        if x[2] == 0:
                            dve.wait_ge(g_mm, n * NJ + (FJ + row_jobs[heads - 1] if heads else FJ))
                        maxima_piece(n * (HG * NM), NM + done, x[2])
                        done += 1
                    if x[0] == "MERGE":
                        merge(n * (HG * NM) + (NM + done))
                        heads += 1
            invert(B * G)
            dve.wait_ge(set_, 2)
            mix_group(dve, B * G)

        @block.scalar
        def _(act):
            act.wait_ge(const_in, CONSTS)

            def copy_job(job, q, m, ropes, start):
                act.wait_ge(g_mm, q)
                scale = 1.0 / (XSC * WSC)
                kind = job[1]
                if kind == "v":
                    if not start:
                        act.wait_ge(v_copied, m * (2 * HG))
                    i = job[3] * (BANK // P)
                    act.activation(Vs[:, job[2], i:i + BANK // P, :], psG[:, :].rearrange("p (i d) -> p i d", d=P),
                                   ACT.Copy, scale=scale).then_inc(g_act, 1)
                elif kind == "chosen_v":
                    act.activation(CVs[:, :], psG[0:KEEP, 0:P], ACT.Copy, scale=scale).then_inc(g_act, 1)
                elif kind == "plain":
                    if not start:
                        for j in range(HG):
                            act.wait_ge(slot_in[j], m * (16 * SLOT_DMAS))
                    stage = {"q": Qs[:, 0], "w": Ws[:, 0], "k": Ks[:, :, :]}[job[2]]
                    act.activation(stage[:, 0, job[3] * BANK:(job[3] + 1) * BANK], psG[:, :], ACT.Copy,
                                   scale=QSC * scale).then_inc(g_act, 1)
                elif kind == "chosen_k":
                    act.wait_ge(roped, ropes("chosen", 0))
                    act.activation(raw[:, rope_buf[("chosen", 0)], :, 0:KEEP],
                                   psG[:, KEEP:3 * KEEP].rearrange("p (y t) -> p y t", y=2), ACT.Copy, scale=QSC * scale)
                    act.activation(Cs[:, 0, 0, :], psG[:, 0:KEEP], ACT.Copy, scale=QSC * scale).then_inc(g_act, 1)
                elif kind == "turn":
                    act.wait_ge(roped, ropes(job[2], job[3]))
                    act.activation(raw[:, rope_buf[(job[2], job[3])], job[4], :], psG[:, :], ACT.Copy,
                                   scale=QSC * scale).then_inc(g_act, 1)

            def chosen_out(q, moved):
                act.wait_ge(g_mm, q)
                act.wait_ge(oc_moved, moved)
                act.activation(oc_raw[:, :], psG[:, :], ACT.Copy).then_inc(g_act, 1)

            def max_row(q, j, heads):
                act.wait_ge(g_mm, q)
                act.wait_ge(rows_in, heads * 16)
                act.activation(max_rows[:, :], psG[0:3 * GT, 0:P], ACT.Copy, scale=-1.0 / SHIFT).then_inc(g_act, 1)
                act.wait_ge(g_act, q)
                act.dma_start(Q[D:K99, j, 0, :].rearrange("k (i t) -> k i t", t=P), max_rows[:, :]).then_inc(rows_in, 16)

            q = 0
            for x in first:
                if x[0] == "G":
                    q += 1
                    copy_job(x, q, 0, lambda name, c: max(rope_order.index((name, c)) - 1, 0), True)
                if x[0] == "MAXROW":
                    q += 1
                    max_row(q, 0, 0)
            with act.Fori(0, B * G) as n:
                q = u = heads = 0
                for x in plan:
                    if x[0] == "G" and x[1] == "chosen_o":
                        q += 1
                        chosen_out(n * NJ + (FJ + q), n * (64 * HG) + 64 * x[2])
                    elif x[0] == "G":
                        q += 1
                        copy_job(x, n * NJ + (FJ + q), n + 1,
                                 lambda name, c: n * NR + (NR + max(rope_order.index((name, c)) - 1, 0)), False)
                    elif x[0] == "MAXROW":
                        q += 1
                        max_row(n * NJ + (FJ + q), x[1], n * HG + (heads + 1))
                        heads += 1
                    elif x[0] == "S":
                        _s, j, k, p, c = x
                        act.wait_ge(s_mm, n * NU + (u + 1))
                        a, end = max(p * P, c * BANK), (c + 1) * BANK
                        tile = psS[:, u % RING, a - c * BANK:BANK]
                        if k == CHOSEN_KEYS:
                            if j == 0:
                                act.wait_ge(g_mm, n * NJ + FJ)
                            else:
                                act.wait_ge(g_mm, n * NJ + (FJ + chosen_o_job(j - 1)))
                            act.activation(prob_c[0:KEEP, a:end], tile[0:KEEP, :], ACT.Exp, scale=EXP_SCALE).then_inc(exp_done, 1)
                        else:
                            pair = j * GT + p
                            if c == (p * P) // BANK:
                                act.wait_ge(pv_mm, n * NPV + (pair - 1) if pair > 1 else n * NPV)
                            act.activation(prob[:, pair % 2, k, a:end], tile, ACT.Exp, scale=EXP_SCALE).then_inc(exp_done, 1)
                        u += 1

        @block.tensor
        def _(pe):
            pe.wait_ge(const_in, CONSTS)
            pe.wait_ge(ones_set, 4)

            def three(out, left, right):
                terms = [(l[a], r[b]) for l, r in zip(left, right) for a, b in PRODUCTS]
                for i, (l, r) in enumerate(terms):
                    last = pe.matmul(out, l, r, start=(i == 0), stop=(i == len(terms) - 1))
                return last

            def project(job):
                kind = job[1]
                if kind == "v":
                    for i in range(BANK // P):
                        t = job[3] * (BANK // P) + i
                        tile = slice(t * P, (t + 1) * P)
                        out = psG[:, i * P:(i + 1) * P]
                        if job[2] == LATENT_KEYS:
                            last = three(out, [[NB[QL:P, l, tile] for l in range(HL)]], [[w_dv[:, l, :] for l in range(HL)]])
                        else:
                            last = three(out, [[XB[:, c, l, tile] for l in range(HL)] for c in range(CK)],
                                         [[w_winv[:, l, c, :] for l in range(HL)] for c in range(CK)])
                elif kind == "chosen_v":
                    last = three(psG[0:KEEP, 0:P], [[SB[:, c, l, :] for l in range(HL)] for c in range(CK)],
                                 [[w_selv[:, l, c, :] for l in range(HL)] for c in range(CK)])
                elif kind == "chosen_k":
                    for y in range(3):
                        last = three(psG[:, y * KEEP:(y + 1) * KEEP],
                                     [[w_sel[:, l, c, y, :] for l in range(HL)] for c in range(CK)],
                                     [[SB[:, c, l, :] for l in range(HL)] for c in range(CK)])
                else:
                    name, c = job[2], job[3]
                    y = 0 if kind == "plain" else 1 + job[4]
                    cols = slice(c * BANK, (c + 1) * BANK)
                    if name == "q":
                        last = three(psG[:, :], [[w_q[:, l, y, :] for l in range(HL)]], [[NB[0:QL, l, cols] for l in range(HL)]])
                    elif name == "k":
                        last = three(psG[:, :], [[w_dk[:, l, :] for l in range(HL)]], [[NB[QL:P, l, cols] for l in range(HL)]])
                    else:
                        last = three(psG[:, :], [[w_win[:, l, k, y, :] for l in range(HL)] for k in range(CK)],
                                     [[XB[:, k, l, cols] for l in range(HL)] for k in range(CK)])
                last.then_inc(g_mm, 1)

            def bank_free(before, jobs_done, split_done):
                if before is not None and is_split(before):
                    pe.wait_ge(g_dve, split_done)
                else:
                    pe.wait_ge(g_act, jobs_done)

            def maxima_piece(j, n, turns, before):
                k, i, c = MAXIMA[n]
                buf = before % 2
                if before > 1:
                    pe.wait_ge(m_red, turns + (before - 1))
                if k == CHOSEN_KEYS:
                    for t in range(GT):
                        last = pe.matmul(psM[:, buf, t * KEEP:(t + 1) * KEEP], Q[0:D, j, 0, t * P:(t + 1) * P], KC[0:D, j, 0, :],
                                         start=True, stop=True)
                else:
                    keys = (K1, KW)[k]
                    w = min((i + 1) * P - c * BANK, BANK)
                    diagonal = (i * P) // BANK == c
                    last = pe.matmul(psM[:, buf, 0:w], Q[0:D, j, 0, i * P:(i + 1) * P],
                                     keys[0:D, j, 0, c * BANK:c * BANK + w], start=True, stop=not diagonal)
                    if diagonal:
                        last = pe.matmul(psM[:, buf, w - P:w], mask[:, 0, :], mask[:, 1, :], start=False, stop=True)
                last.then_inc(m_mm, 1)

            def scores(j, k, p, c, u):
                keys = (K1, KW, KC)[k]
                rows = KEEP if k == CHOSEN_KEYS else P
                a = max(p * P, c * BANK)
                out = psS[0:rows, u % RING, a - c * BANK:BANK]
                tile = slice(p * rows, (p + 1) * rows)
                cols = slice(a, (c + 1) * BANK)
                pe.matmul(out, keys[:, j, 0, tile], Q[:, j, 0, cols], start=True, stop=False)
                pe.matmul(out, keys[0:D, j, 0, tile], Q[0:D, j, 1, cols], start=False, stop=False)
                last = pe.matmul(out, keys[0:D, j, 1, tile], Q[0:D, j, 0, cols], start=False, stop=True)
                return last

            def values(j, p, c):
                a = max(p * P, c * BANK)
                for k in range(2):
                    last = pe.matmul(psO[64 * k:64 * k + 64, a:(c + 1) * BANK], V[:, k, j, p, :],
                                     prob[:, (j * GT + p) % 2, k, a:(c + 1) * BANK], start=(p == 0),
                                     stop=(p * P + P >= (c + 1) * BANK))
                return last

            pe.wait_ge(w_in, 16 * 6)
            q = d = done = 0
            before = None
            for x in first:
                if x[0] == "G":
                    if q:
                        bank_free(before, q, d)
                    project(x)
                    q += 1
                    d += is_split(x)
                    before = x
                if x[0] == "MAX":
                    if x[2] == 0:
                        pe.wait_ge(slot_in[0], 16 * SLOT_DMAS)
                    maxima_piece(0, x[2], 0, done)
                    done += 1
                if x[0] == "MAXROW":
                    bank_free(before, q, d)
                    pe.wait_ge(m_ready, 1)
                    pe.transpose(psG[0:3 * GT, 0:P], maxima[:, :], ident[:, :]).then_inc(g_mm, 1)
                    before = x
            with pe.Fori(0, B * G) as n:
                q = d = done = u = heads = 0
                for x in plan:
                    kind = x[0]
                    if kind == "G" and x[1] != "chosen_o":
                        if x[1:] == PROJECT[0]:
                            pe.wait_ge(w_in, n * (16 * 6) + 2 * 16 * 6)
                        bank_free(before, n * NJ + (FJ + q), n * ND + (FD + d))
                        project(x)
                        q += 1
                        d += is_split(x)
                        before = x
                    elif kind == "G":
                        j = x[2]
                        pe.wait_ge(exp_done, n * NU + unit_of[(j, CHOSEN_KEYS, 0, HB - 1)] + 1)
                        bank_free(before, n * NJ + (FJ + q), n * ND + (FD + d))
                        for c in range(HB):
                            last = pe.matmul(psG[64 * c:64 * c + 64, :], VC[:, j, :], prob_c[:, c * BANK:(c + 1) * BANK],
                                             start=True, stop=True)
                        last.then_inc(g_mm, 1)
                        q += 1
                        before = x
                    elif kind == "MAXROW":
                        bank_free(before, n * NJ + (FJ + q), n * ND + (FD + d))
                        pe.wait_ge(m_ready, n * HG + heads + 2)
                        pe.transpose(psG[0:3 * GT, 0:P], maxima[:, :], ident[:, :]).then_inc(g_mm, 1)
                        q += 1
                        heads += 1
                        before = x
                    elif kind == "MAX":
                        if x[2] == 0:
                            pe.wait_ge(slot_in[x[1]], n * (16 * SLOT_DMAS) + (16 * SLOT_DMAS) * (2 if x[1] == 0 else 1))
                        maxima_piece(x[1], x[2], n * (HG * NM), NM + done)
                        done += 1
                    elif kind == "S":
                        _s, j, k, p, c = x
                        if k == LATENT_KEYS and p == 0 and c == 0:
                            pe.wait_ge(rows_in, n * (16 * HG) + 16 * (j + 1))
                        pe.wait_ge(exp_done, n * NU + (u + 1 - RING) if u >= RING else n * NU)
                        scores(j, k, p, c, u).then_inc(s_mm, 1)
                        u += 1
                    elif kind == "PV":
                        _p, j, p, c = x
                        if p == 0 and c == 0:
                            pe.wait_ge(o_out, n * HG + j)
                            pe.wait_ge(v_copied, n * (2 * HG) + 2 * (j + 1))
                        if c == (p * P) // BANK:
                            pe.wait_ge(hidden, n * (HG * GT) + (j * GT + p + 1))
                        else:
                            pe.wait_ge(exp_done, n * NU + unit_of[(j, WINDOW_KEYS, p, c)] + 1)
                        last = values(j, p, c)
                        if c == HB - 1:
                            last.then_inc(pv_mm, 1)


def project_out(nc, X, dram, s):
    with ExitStack() as ctx:
        def sb(n, shape, dt=F32):
            return ctx.enter_context(nc.sbuf_tensor("o_" + n, shape, dt))

        def sem(n):
            return nc.alloc_semaphore("o_" + n)

        wp, ws = sb("wp", [P, G, C]), sb("ws", [P, HL, G, C], F16)
        O = sb("O", [P, 2, G, HL, T], F16)
        ps = ctx.enter_context(nc.psum_tensor("o_ps", [P, 4, BANK], F32))
        loaded, hi, ready, summed, added = (sem(n) for n in ("loaded", "hi", "ready", "summed", "added"))
        o_in, x_in = [sem(f"o_in{e}") for e in range(2)], [sem(f"x_in{b}") for b in range(B)]
        block = ctx.enter_context(nc.Block())

        @block.sync
        def _(sp):
            sp.dma_start(wp[:, :, :], dram["w_proj"].rearrange("(g p) c -> p g c", p=P)).then_inc(loaded, 16)
            with sp.Fori(0, B // 2) as t:
                for e in range(2):
                    b = sp.snap(t * 2 + e)
                    sp.wait_ge(summed, t * (2 * GT))
                    sp.dma_start(O[:, e, :, :, :].rearrange("p g l t -> p g (l t)"),
                                 s["mixed"][1:B * G + 1].rearrange("(b g) p c -> b p g c", g=G)[bass.ds(b, 1)].rearrange("b p g c -> p (b g) c")).then_inc(o_in[e], 16)
            sp.wait_ge(added, NT)

        @block.scalar
        def _(act):
            act.wait_ge(loaded, 16)
            act.activation(ws[:, 0, :, :], wp[:, :, :], ACT.Copy, scale=WSC).then_inc(hi, 1)
            for b in range(B):
                act.dma_start(X[:, b * GT:(b + 1) * GT, :],
                              s["x1"].rearrange("(i p) c -> p i c", p=P)[:, b * GT:(b + 1) * GT, :]).then_inc(x_in[b], 16)

        @block.vector
        def _(dve):
            dve.wait_ge(hi, 1)
            dve.scalar_tensor_tensor(ws[:, 1, :, :], wp[:, :, :], WSC, ws[:, 0, :, :], ALU.mult, ALU.subtract).then_inc(ready, 1)
            def add(b, i):
                dve.wait_ge(summed, b * GT + (i + 1))
                x = X[:, b * GT + i, :]
                dve.scalar_tensor_tensor(x, ps[:, i % 4, 0:C], 1.0 / (QSC * WSC), x, ALU.mult, ALU.add).then_inc(added, 1)

            for b in range(B):
                dve.wait_ge(x_in[b], 16)
                for i in range(GT):
                    add(b, i)

        @block.tensor
        def _(pe):
            pe.wait_ge(ready, 1)
            with pe.Fori(0, B // 2) as t:
                for e in range(2):
                    pe.wait_ge(o_in[e], t * 16 + 16)
                    for i in range(GT):
                        m = e * GT + i - 3
                        pe.wait_ge(added, t * (2 * GT) + m if m > 0 else t * (2 * GT))
                        for g in range(G):
                            for a, b in PRODUCTS:
                                last = pe.matmul(ps[:, i % 4, 0:C], O[:, e, g, a, i * P:(i + 1) * P], ws[:, b, g, :],
                                                 start=(g == 0 and (a, b) == HIHI), stop=(g == G - 1 and (a, b) == LOHI))
                        last.then_inc(summed, 1)


def scratch():
    return [
        ("disp1", (SLOTS, C), F32), ("eout1", (SLOTS, C), F32), ("disp2", (SLOTS, C), F32), ("eout2", (SLOTS, C), F32),
        ("x1", (N, C), F32), ("xn", (N, C), F32), ("wsplit", (G, P, W_COLS), F16), ("xt", (B, P, CK * HL * T), F16),
        ("lat", (B, P, HL * T), F16), ("kr", (B, ROPE, HL * T), F16), ("sel", (B, P, CK * HL * KEEP), F16),
        ("score_n", (P, NT), F32), ("score_t", (N,), F32), ("rank_t", (N,), F32), ("gl", (P, B * 3), F32),
        ("gates", (B, P, 3), F32), ("mixed", (B * G + 1, P, HL * T), F16), ("sums", (3, HG, T), F32), ("inverses", (3, HG, T), F32),
    ]


def macaron_block(nc, x, out, dram, consts):
    s = {name: nc.dram_tensor("s_" + name, shape, dt).ap() for name, shape, dt in scratch()}
    dram = {**dram, **s}
    with nc.cleanup_on_exit(), nc.sbuf_tensor("X", [P, NT, C], F32) as X:
        ffn(nc, "1", X, dram, consts, x, s["x1"], beside=split_weights)
        latents(nc, X, dram, consts, s)
    with nc.cleanup_on_exit():
        select_tokens(nc, consts, s)
        attention(nc, consts, s)
    with nc.cleanup_on_exit(), nc.sbuf_tensor("X2", [P, NT, C], F32) as X:
        project_out(nc, X, dram, s)
        ffn(nc, "2", X, dram, consts, None, out)


_INS = ["L0_attn_x", "L0_attn_w_cq", "L0_attn_g_qnorm", "L0_attn_w_dq_nope", "L0_attn_w_dq_rope", "L0_attn_w_ckv",
        "L0_attn_g_kvnorm", "L0_attn_w_dk_nope", "L0_attn_w_dv", "L0_attn_w_krope", "L0_attn_w_imp",
        "L0_attn_w_selk", "L0_attn_w_selv", "L0_attn_w_wink", "L0_attn_w_winv", "L0_attn_w_gate",
        "L0_attn_w_proj", "L0_ffn_Wr", "L0_ffn_W1", "L0_ffn_W2"]


def kernel(**inputs):
    import numpy as _np
    import concourse.bacc as _bacc
    from concourse import mybir as _mybir
    from concourse.bass_utils import run_bass_kernel_spmd as _run

    nc = _bacc.Bacc("TRN2", target_bir_lowering=False, num_devices=1)
    arrays, dram, consts = {}, {}, {}
    for name in _INS:
        a = _np.ascontiguousarray(inputs[name])
        arrays[f"in_{name}"] = a
        short = name.replace("L0_attn_", "").replace("L0_ffn_", "")
        dram[short] = nc.dram_tensor(f"in_{name}", a.shape, _mybir.dt.from_np(a.dtype), kind="ExternalInput").ap()
    for name, a in constants().items():
        arrays[name] = a
        consts[name] = nc.dram_tensor(name, a.shape, _mybir.dt.from_np(a.dtype), kind="ExternalInput").ap()
    out = nc.dram_tensor("out_0", (N, C), _mybir.dt.float32, kind="ExternalOutput").ap()
    x = dram["x"].rearrange("b t c -> (b t) c")
    macaron_block(nc, x, out, dram, consts)
    r = _run(nc, [arrays], core_ids=[0])
    return r.results[0]["out_0"].reshape(B, T, C)
```
